# Optimizing a Trainium2 kernel written in Bass

```python
import numpy as np
import jax
import jax.numpy as jnp

def _softmax(x, axis=-1):
    return jax.nn.softmax(x, axis=axis)

def _gelu(x):
    return jax.nn.gelu(x, approximate=True)

def _silu(x):
    return jax.nn.silu(x)

def _sigmoid(x):
    return jax.nn.sigmoid(x)

def _layernorm(x, axis=-1, eps=1e-05):
    m = jnp.mean(x, axis=axis, keepdims=True)
    v = jnp.var(x, axis=axis, keepdims=True)
    return (x - m) / jnp.sqrt(v + eps)

def _scatter_add(tgt, idx, src, axis=0):
    return tgt.at[idx].add(src)

def _segment_sum(src, seg, n):
    return jax.ops.segment_sum(src, seg, n)
kernel_name = 'mk_adaln_d1_jaxref_r4_6be65d'

def setup_inputs(seed: int=0):
    np.random.seed(seed)
    _w = jnp.asarray

    def _L0_attn_setup():
        import jax, jax.numpy as jnp
        import numpy as np
        D_MODEL = 256
        NHEAD = 16
        HEAD_DIM = D_MODEL // NHEAD
        WINDOW = 128
        BATCH = 2
        SEQ = 1024

        def _sliding_window_attention(q, k, v, window):
            B, H, S, D = q.shape
            W = window
            nc = S // W
            qc = q.reshape(B, H, nc, W, D)
            kb = k.reshape(B, H, nc, W, D)
            vb = v.reshape(B, H, nc, W, D)
            kprev = jnp.pad(kb, ((0, 0), (0, 0), (1, 0), (0, 0), (0, 0)))[:, :, :-1]
            vprev = jnp.pad(vb, ((0, 0), (0, 0), (1, 0), (0, 0), (0, 0)))[:, :, :-1]
            k2 = jnp.concatenate([kprev, kb], axis=3)
            v2 = jnp.concatenate([vprev, vb], axis=3)
            scores = jnp.einsum('bhcid,bhcjd->bhcij', qc, k2) / jnp.sqrt(jnp.asarray(D, dtype=q.dtype))
            i = jnp.arange(W)[:, None]
            j = jnp.arange(2 * W)[None, :]
            band = (j >= i + 1) & (j <= i + W)
            c = jnp.arange(nc)[:, None, None]
            valid = band[None] & ((c > 0) | (j[None] >= W))
            neg_inf = jnp.asarray(-jnp.inf, dtype=scores.dtype)
            scores = jnp.where(valid[None, None], scores, neg_inf)
            attn = jax.nn.softmax(scores, axis=-1)
            out = jnp.einsum('bhcij,bhcjd->bhcid', attn, v2)
            return out.reshape(B, H, S, D)
        key = jax.random.key(seed)
        kx, kq, kk, kv, ko = jax.random.split(key, 5)
        scale = 0.02
        return {'x': jax.random.normal(kx, (BATCH, SEQ, D_MODEL), dtype=jnp.float32), 'Wq': jax.random.normal(kq, (D_MODEL, D_MODEL), dtype=jnp.float32) * scale, 'Wk': jax.random.normal(kk, (D_MODEL, D_MODEL), dtype=jnp.float32) * scale, 'Wv': jax.random.normal(kv, (D_MODEL, D_MODEL), dtype=jnp.float32) * scale, 'Wo': jax.random.normal(ko, (D_MODEL, D_MODEL), dtype=jnp.float32) * scale}
    _L0_attn_in = _L0_attn_setup()

    def _L0_ffn_setup():
        import jax, jax.numpy as jnp
        import numpy as np
        HIDDEN = 256
        INTER = 1024
        N_EXPERTS = 8

        def geglu(x, w1, w2, w3):
            return jax.nn.gelu(x @ w1, approximate=False) * (x @ w2) @ w3
        key = jax.random.key(seed)
        ks = jax.random.split(key, 8)
        s = 0.02
        x = jax.random.normal(ks[0], (2, 512, HIDDEN), dtype=jnp.float32)
        w1s = jax.random.normal(ks[1], (HIDDEN, INTER), dtype=jnp.float32) * s
        w2s = jax.random.normal(ks[2], (HIDDEN, INTER), dtype=jnp.float32) * s
        w3s = jax.random.normal(ks[3], (INTER, HIDDEN), dtype=jnp.float32) * s
        W1 = jax.random.normal(ks[4], (N_EXPERTS, HIDDEN, INTER), dtype=jnp.float32) * s
        W2 = jax.random.normal(ks[5], (N_EXPERTS, HIDDEN, INTER), dtype=jnp.float32) * s
        W3 = jax.random.normal(ks[6], (N_EXPERTS, INTER, HIDDEN), dtype=jnp.float32) * s
        Wg = jax.random.normal(ks[7], (HIDDEN, N_EXPERTS), dtype=jnp.float32) * s
        return {'x': x, 'w1s': w1s, 'w2s': w2s, 'w3s': w3s, 'W1': W1, 'W2': W2, 'W3': W3, 'Wg': Wg}
    _L0_ffn_in = _L0_ffn_setup()
    _L0_c = _w((lambda *s: np.random.randn(*s).astype(np.float32) * 0.05)(2, 256))
    _L0_wmod = _w((lambda *s: np.random.randn(*s).astype(np.float32) * 0.05)(256, 6 * 256) * 256 ** (-0.5))
    _d = {'L0_attn_x': _L0_attn_in['x'], 'L0_attn_Wq': _L0_attn_in['Wq'], 'L0_attn_Wk': _L0_attn_in['Wk'], 'L0_attn_Wv': _L0_attn_in['Wv'], 'L0_attn_Wo': _L0_attn_in['Wo'], 'L0_ffn_w1s': _L0_ffn_in['w1s'], 'L0_ffn_w2s': _L0_ffn_in['w2s'], 'L0_ffn_w3s': _L0_ffn_in['w3s'], 'L0_ffn_W1': _L0_ffn_in['W1'], 'L0_ffn_W2': _L0_ffn_in['W2'], 'L0_ffn_W3': _L0_ffn_in['W3'], 'L0_ffn_Wg': _L0_ffn_in['Wg'], 'L0_c': _L0_c, 'L0_wmod': _L0_wmod}
    _x0 = _d['L0_attn_x']
    _d['L0_attn_x'] = jax.random.normal(jax.random.fold_in(jax.random.key(seed), 1), (2, 2048, 256), dtype=_x0.dtype)
    del _x0
    return _d

def reference(L0_attn_x, L0_attn_Wq, L0_attn_Wk, L0_attn_Wv, L0_attn_Wo, L0_ffn_w1s, L0_ffn_w2s, L0_ffn_w3s, L0_ffn_W1, L0_ffn_W2, L0_ffn_W3, L0_ffn_Wg, L0_c, L0_wmod):

    def _L0_attn_ref(x, Wq, Wk, Wv, Wo):
        import jax, jax.numpy as jnp
        import numpy as np
        D_MODEL = 256
        NHEAD = 16
        HEAD_DIM = D_MODEL // NHEAD
        WINDOW = 128
        BATCH = 2
        SEQ = 1024

        def _sliding_window_attention(q, k, v, window):
            B, H, S, D = q.shape
            W = window
            nc = S // W
            qc = q.reshape(B, H, nc, W, D)
            kb = k.reshape(B, H, nc, W, D)
            vb = v.reshape(B, H, nc, W, D)
            kprev = jnp.pad(kb, ((0, 0), (0, 0), (1, 0), (0, 0), (0, 0)))[:, :, :-1]
            vprev = jnp.pad(vb, ((0, 0), (0, 0), (1, 0), (0, 0), (0, 0)))[:, :, :-1]
            k2 = jnp.concatenate([kprev, kb], axis=3)
            v2 = jnp.concatenate([vprev, vb], axis=3)
            scores = jnp.einsum('bhcid,bhcjd->bhcij', qc, k2) / jnp.sqrt(jnp.asarray(D, dtype=q.dtype))
            i = jnp.arange(W)[:, None]
            j = jnp.arange(2 * W)[None, :]
            band = (j >= i + 1) & (j <= i + W)
            c = jnp.arange(nc)[:, None, None]
            valid = band[None] & ((c > 0) | (j[None] >= W))
            neg_inf = jnp.asarray(-jnp.inf, dtype=scores.dtype)
            scores = jnp.where(valid[None, None], scores, neg_inf)
            attn = jax.nn.softmax(scores, axis=-1)
            out = jnp.einsum('bhcij,bhcjd->bhcid', attn, v2)
            return out.reshape(B, H, S, D)
        B, S, E = x.shape
        q = (x @ Wq.T).reshape(B, S, NHEAD, HEAD_DIM).transpose(0, 2, 1, 3)
        k = (x @ Wk.T).reshape(B, S, NHEAD, HEAD_DIM).transpose(0, 2, 1, 3)
        v = (x @ Wv.T).reshape(B, S, NHEAD, HEAD_DIM).transpose(0, 2, 1, 3)
        attn_out = _sliding_window_attention(q, k, v, WINDOW)
        attn_out = attn_out.transpose(0, 2, 1, 3).reshape(B, S, E)
        return attn_out @ Wo.T

    def _L0_ffn_ref(x, w1s, w2s, w3s, W1, W2, W3, Wg):
        import jax, jax.numpy as jnp
        import numpy as np
        HIDDEN = 256
        INTER = 1024
        N_EXPERTS = 8

        def geglu(x, w1, w2, w3):
            return jax.nn.gelu(x @ w1, approximate=False) * (x @ w2) @ w3
        B, T, C = x.shape
        xf = x.reshape(-1, C)
        shared = geglu(xf, w1s, w2s, w3s)
        logits = xf @ Wg
        idx = jnp.argmax(logits, axis=-1)
        final = jnp.zeros_like(xf)
        for e in range(N_EXPERTS):
            y = geglu(xf, W1[e], W2[e], W3[e])
            final = final + jnp.where((idx == e)[:, None], y, 0.0)
        return (shared + final).reshape(B, T, C)
    x = L0_attn_x
    mod = (_silu(L0_c) @ L0_wmod).reshape(L0_c.shape[0], 6, 1, -1)
    sa, ca, ga, sb, cb, gb = (mod[:, 0], mod[:, 1], mod[:, 2], mod[:, 3], mod[:, 4], mod[:, 5])
    ga = (2 * (ga >= 0) - 1) * jnp.maximum(jnp.abs(ga), 0.25)
    gb = (2 * (gb >= 0) - 1) * jnp.maximum(jnp.abs(gb), 0.25)
    h = _layernorm(x, axis=-1) * (1 + ca) + sa
    x = x + ga * _L0_attn_ref(h, L0_attn_Wq, L0_attn_Wk, L0_attn_Wv, L0_attn_Wo)
    h = _layernorm(x, axis=-1) * (1 + cb) + sb
    x = x + gb * _L0_ffn_ref(h, L0_ffn_w1s, L0_ffn_w2s, L0_ffn_w3s, L0_ffn_W1, L0_ffn_W2, L0_ffn_W3, L0_ffn_Wg)
    return x

_drawn_inputs = setup_inputs


def setup_inputs(seed=0):
    import zlib

    import numpy as np

    out = dict(_drawn_inputs(seed))
    spreads = {}
    factors = {'L0_attn_Wq': 8.0,
     'L0_attn_Wk': 8.0,
     'L0_attn_Wv': 8.0,
     'L0_attn_Wo': 8.0,
     'L0_ffn_w1s': 6.578,
     'L0_ffn_w2s': 6.419,
     'L0_ffn_w3s': 6.42,
     'L0_ffn_W1': 6.572,
     'L0_ffn_W2': 6.403,
     'L0_ffn_W3': 6.399,
     'L0_ffn_Wg': 6.809,
     'L0_c': 4.423,
     'L0_wmod': 4.538}
    for name, (base, spread) in spreads.items():
        noise = np.random.default_rng([zlib.crc32(name.encode()), seed]).standard_normal(out[name].shape)
        drawn = base * np.exp(spread * noise) if base else spread * noise
        out[name] = jnp.asarray(drawn.astype(out[name].dtype))
    for name, factor in factors.items():
        out[name] = (out[name] * factor).astype(out[name].dtype)
    return out
```

```python
import concourse.bass as bass
from concourse import mybir
from contextlib import ExitStack

F32 = mybir.dt.float32
F32R = mybir.dt.float32r
BF16 = mybir.dt.bfloat16
F16 = mybir.dt.float16
I32 = mybir.dt.int32
U32 = mybir.dt.uint32
ALU = mybir.AluOpType
ACT = mybir.ActivationFunctionType
AX = mybir.AxisListType
ds = bass.ds

P = 128
B, S, D = 2, 2048, 256
T = B * S
KD = D // P
H, HD = 16, 16
F = 1024
KF = F // P
E = 8
CHUNKS = T // P
TILE = 256
SUB = TILE // P
STEPS = T // TILE
TILES_MAX = T // TILE + E
SORTED = (TILES_MAX + 1) * TILE
EPS = 1e-5
MASKED = -1e30
VROW = 50
VCOLS = 3 * HD + 1
PAIRS = H // 2
RSQRT_MAGIC = 0x5F3759DF + 1


class OwnOrder:

    def __init__(self, eng, sem, passed=0):
        self.eng, self.sem, self.passed, self.n = eng, sem, passed, 0

    def __call__(self, ins):
        ins.then_inc(self.sem, 1)
        self.n += 1

    def wait(self):
        self.eng.wait_ge(self.sem, self.passed + self.n)

    def step(self, ins):
        self(ins)
        self.wait()


class Tensors:

    def __init__(self, nc, stack):
        self.nc, self.stack = nc, stack

    def sb(self, name, shape, dtype=F32):
        return self.stack.enter_context(self.nc.sbuf_tensor(name, shape, dtype))

    def ps(self, name, shape):
        return self.stack.enter_context(self.nc.psum_tensor(name, shape, F32))

    def sem(self, name):
        return self.stack.enter_context(self.nc.semaphore(name))


def rsqrt(nc, order, y, guess, v, t, g):
    n = y.shape[-1]
    order.step(nc.gpsimd.tensor_tensor(y.bitcast(I32), guess, g.magic[:, 0:n], ALU.add))
    for i in range(3):
        order.step(nc.gpsimd.tensor_tensor(t, y, y, ALU.mult))
        order.step(nc.gpsimd.tensor_tensor(t, t, v, ALU.mult))
        order.step(nc.gpsimd.tensor_tensor(t, t, g.three_halves[:, 0:n], ALU.add))
        last = nc.gpsimd.tensor_tensor(y, y, t, ALU.mult)
        if i < 2:
            order.step(last)
    return last


def apart(nc, g):
    nc.vector.tensor_copy(g.scrap[:, 0:1], g.scrap[:, 1:2])


def setup(nc, g, dram):
    with ExitStack() as stack:
        t = Tensors(nc, stack)
        cond = t.sb("cond", [P, KD, B])
        cond_e = t.sb("cond_e", [P, KD, B])
        cond_silu = t.sb("cond_silu", [P, KD, B])
        cond_wide = t.sb("cond_wide", [P, KD, B, P])
        wmod = t.sb("wmod", [P, KD, 6 * D])
        wqkv = t.sb("wqkv", [P, KD, 3 * D])
        zeros = t.sb("zeros", [P, 10, D])
        sign = t.sb("gate_sign", [P, B, D])
        size = t.sb("gate_size", [P, B, D])
        col_ps = t.ps("col_ps", [P, 512])
        row_ps = t.ps("row_ps", [P, 2, 512])
        cond_in, wmod_in, wq_in, wo_in = (t.sem(n) for n in ("cond_in", "wmod_in", "wq_in", "wo_in"))
        act_done, col_done, row_done, row_used = (
            t.sem(n) for n in ("s_act_done", "s_col_done", "s_row_done", "s_row_used"))
        silu_done, dve_own, pool_own, zeroed, zero_out = (
            t.sem(n) for n in ("silu_done", "s_dve_own", "s_pool_own", "zeroed", "zero_out"))

        with nc.Block() as block:

            @block.sync
            def _(sp):
                sp.dma_start(cond[:], dram["c"].rearrange("(k p) b -> p k b", p=P)).then_inc(cond_in, 16)
                sp.dma_start(wmod[:], dram["wmod"].rearrange("(k p) n -> p k n", p=P)).then_inc(wmod_in, 16)
                for i, w in enumerate(("wq", "wk", "wv")):
                    sp.dma_start(wqkv[:, :, i * D:(i + 1) * D],
                                 dram[w].rearrange("(k p) n -> p k n", p=P)).then_inc(wq_in, 16)
                sp.dma_start(g.wo[:], dram["wo"].rearrange("(k p) n -> p k n", p=P)).then_inc(wo_in, 16)
                sp.dma_start(g.wg[:], dram["wg"].rearrange("(k p) n -> p k n", p=P)).then_inc(wo_in, 16)
                sp.wait_ge(zeroed, 1)
                sp.dma_start(dram["qk"].rearrange("a f t -> (a f) t")[:, 0:P].rearrange("(m p) t -> p m t", p=P),
                             zeros[:, 0:4, :].rearrange("p a (c t) -> p (a c) t", t=P)).then_inc(zero_out, 16)
                sp.dma_start(dram["v"][0:P, :],
                             zeros[:, 0:2, :].rearrange("p a b -> p (a b)")[:, 0:H * VROW // 2].bitcast(BF16)
                             ).then_inc(zero_out, 16)
                for name in ("h_sorted", "y_sorted"):
                    rows = dram[name].rearrange("(a p) d -> p a d", p=P)
                    for a in range(0, SORTED // P, 10):
                        n = min(10, SORTED // P - a)
                        sp.dma_start(rows[:, a:a + n, :], zeros[:, 0:n, :]).then_inc(zero_out, 16)
                sp.wait_ge(cond_in, 16)
                sp.wait_ge(wo_in, 32)
                sp.wait_ge(zero_out, 16 * (2 + 2 * -(-SORTED // P // 10)))

            @block.gpsimd
            def _(pool):
                order = OwnOrder(pool, pool_own)
                nc.gpsimd.memset(zeros[:], 0.0).then_inc(zeroed, 1)
                order(nc.gpsimd.memset(g.ident[:], 0.0))
                order(nc.gpsimd.memset(g.mask[:], 0.0))
                order(nc.gpsimd.memset(g.magic[:], RSQRT_MAGIC))
                order(nc.gpsimd.memset(g.scrap[:], 0.0))
                order(nc.gpsimd.memset(g.three_halves[:], 1.5))
                order(nc.gpsimd.memset(g.ones[:], 1.0))
                order.step(nc.gpsimd.memset(g.before[:], 1.0))
                order.step(nc.gpsimd.affine_select(
                    out=g.ident[:], in_=g.ident[:], compare_op=ALU.not_equal, fill=1.0, base=0,
                    pattern=[[-1, P]], channel_multiplier=1))
                order(nc.gpsimd.tensor_copy(g.identb[:], g.ident[:]))
                order(nc.gpsimd.affine_select(
                    out=g.before[:], in_=g.before[:], compare_op=ALU.is_gt, fill=0.0, base=0,
                    pattern=[[1, P]], channel_multiplier=-1))
                for m in range(16):
                    for head in range(2):
                        prev = g.mask[:, m, head * 256:head * 256 + P]
                        own = g.mask[:, m, head * 256 + P:head * 256 + 2 * P]
                        if m % (S // TILE) == 0:
                            order(nc.gpsimd.memset(prev, MASKED))
                        else:
                            order(nc.gpsimd.affine_select(
                                out=prev, in_=prev, compare_op=ALU.is_gt, fill=MASKED, base=0,
                                pattern=[[1, P]], channel_multiplier=-1))
                        order(nc.gpsimd.affine_select(
                            out=own, in_=own, compare_op=ALU.is_ge, fill=MASKED, base=0,
                            pattern=[[-1, P]], channel_multiplier=1))
                order.wait()

            @block.scalar
            def _(act):
                act.wait_ge(cond_in, 16)
                nc.scalar.activation(cond_e[:], cond[:], ACT.Exp, scale=-1.0).then_inc(act_done, 1)
                act.wait_ge(wq_in, 48)
                nc.scalar.activation(g.wqkv_hi[:, :, 0:D], wqkv[:, :, 0:D], ACT.Copy,
                                     scale=HD ** -0.5).then_inc(act_done, 1)
                nc.scalar.activation(g.wqkv_hi[:, :, D:3 * D], wqkv[:, :, D:3 * D], ACT.Copy).then_inc(act_done, 1)

            @block.vector
            def _(dve):
                order = OwnOrder(dve, dve_own)
                dve.wait_ge(act_done, 1)
                order.step(nc.vector.tensor_scalar(cond_e[:], cond_e[:], 1.0, None, ALU.add))
                order.step(nc.vector.reciprocal(cond_e[:], cond_e[:]))
                order.step(nc.vector.tensor_tensor(cond_silu[:], cond[:], cond_e[:], ALU.mult))
                nc.vector.tensor_copy(
                    cond_wide[:], cond_silu[:].unsqueeze(3).broadcast_to([P, KD, B, P])).then_inc(silu_done, 1)
                dve.wait_ge(col_done, 1)
                cols = col_ps[:, 0:2 * KD * B].rearrange("p (s m b) -> p s m b", s=2, m=KD)
                order(nc.vector.tensor_copy(g.shift_a[:], cols[:, 0].rearrange("p m b -> p b m")))
                order(nc.vector.tensor_scalar(g.scale_a[:], cols[:, 1].rearrange("p m b -> p b m"),
                                              1.0, None, ALU.add))
                for b in range(B):
                    dve.wait_ge(row_done, b + 1)
                    order(nc.vector.tensor_copy(g.gate_a[:, b, :], row_ps[:, 0, 0:D]))
                    order(nc.vector.tensor_copy(g.shift_b[:, b, :], row_ps[:, 0, D:2 * D]))
                    order(nc.vector.tensor_scalar(g.scale_b[:, b, :], row_ps[:, 1, 0:D], 1.0, None, ALU.add))
                    nc.vector.tensor_copy(g.gate_b[:, b, :], row_ps[:, 1, D:2 * D]).then_inc(row_used, 1)
                dve.wait_ge(row_used, B)
                order.wait()
                for gate in (g.gate_a, g.gate_b):
                    order.step(nc.vector.tensor_scalar(sign[:], gate[:], 0.0, 2.0, ALU.is_ge, ALU.mult))
                    order.step(nc.vector.tensor_scalar(sign[:], sign[:], 1.0, None, ALU.subtract))
                    order.step(nc.vector.tensor_tensor(size[:], gate[:], sign[:], ALU.mult))
                    order.step(nc.vector.tensor_scalar(size[:], size[:], 0.25, None, ALU.max))
                    order.step(nc.vector.tensor_tensor(gate[:], size[:], sign[:], ALU.mult))
                dve.wait_ge(act_done, 3)
                order(nc.vector.scalar_tensor_tensor(
                    g.wqkv_lo[:, :, 0:D], wqkv[:, :, 0:D], HD ** -0.5, g.wqkv_hi[:, :, 0:D].bitcast(F32),
                    ALU.mult, ALU.subtract))
                order(nc.vector.tensor_tensor(g.wqkv_lo[:, :, D:3 * D], wqkv[:, :, D:3 * D],
                                              g.wqkv_hi[:, :, D:3 * D].bitcast(F32), ALU.subtract))
                order(nc.vector.memset(g.v_ones[:], 1.0))
                order.wait()

            @block.tensor
            def _(pe):
                pe.wait_ge(silu_done, 1)
                pe.wait_ge(wmod_in, 16)
                for n in range(2 * KD):
                    for k in range(KD):
                        last = nc.tensor.matmul(col_ps[:, n * B:(n + 1) * B], wmod[:, k, n * P:(n + 1) * P],
                                                cond_silu[:, k, :], start=(k == 0), stop=(k == KD - 1))
                last.then_inc(col_done, 1)
                for b in range(B):
                    if b:
                        pe.wait_ge(row_used, b)
                    for half in range(2):
                        for k in range(KD):
                            last = nc.tensor.matmul(row_ps[:, half, :], cond_wide[:, k, b, :],
                                                    wmod[:, k, 2 * D + half * 512:2 * D + (half + 1) * 512],
                                                    start=(k == 0), stop=(k == KD - 1))
                    last.then_inc(row_done, 1)


def project(nc, g, dram):
    with ExitStack() as stack:
        t = Tensors(nc, stack)
        xn = t.sb("xn", [P, 2, SUB, D])
        h_t = t.sb("h_t", [P, 2, KD, TILE])
        h_hi = t.sb("h_hi", [P, 2, KD, TILE], F32R)
        h_lo = t.sb("h_lo", [P, 2, KD, TILE], F32R)
        qk = t.sb("qk_hilo", [P, 2, 2, 4, TILE], F32R)
        v_rows = t.sb("v_rows", [P, 2, SUB, H, VROW], BF16)
        v_rest = t.sb("v_rest", [P, 2, SUB, D])
        stats = t.sb("stats", [P, 2, SUB, 6])
        mean_var = t.sb("mean_var", [P, 2, SUB, 2])
        var = t.sb("var", [P, 2, SUB])
        minus_half_var = t.sb("minus_half_var", [P, 2, SUB])
        guess = t.sb("guess", [P, 2, SUB], I32)
        rstd = t.sb("rstd", [P, 2, SUB])
        newt = t.sb("newt", [P, 2, SUB])
        h_ps = t.ps("h_ps", [P, KD, TILE])
        qk_ps = t.ps("qk_ps", [P, 2, 2, 512])
        v_ps = t.ps("v_ps", [P, 2, SUB, D])
        x_in = [t.sem(f"x_in{u}") for u in range(2)]
        qk_out = [t.sem(f"qk_out{u}") for u in range(2)]
        v_out = [t.sem(f"v_out{u}") for u in range(2)]
        names = ("guess_ready", "rstd_ready", "xn_ready", "h_transposed", "hi_ready", "lo_ready",
                 "qk_done", "v_done", "qk_hi", "v_0", "v_1", "qk_split", "v_rest_ready", "v_split", "dve_own",
                 "pool_own")
        s = {n: t.sem("p_" + n) for n in names}

        def steps(eng, body):
            with eng.Fori(0, STEPS // 2 - 2) as k:
                for u in range(2):
                    body(2 * k + u, u, k, None)
            for k in range(STEPS // 2 - 2, STEPS // 2):
                for u in range(2):
                    body(2 * k + u, u, k, 2 * k + u)

        def inside(n, ahead):
            return n is None or n + ahead < STEPS

        with nc.Block() as block:

            @block.sync
            def _(sp):
                def load(m, u, k):
                    sp.dma_start(g.x[:, ds(m * SUB, SUB), :],
                                 dram["x"][ds(m * TILE, TILE), :].rearrange("(s p) d -> p s d", p=P)
                                 ).then_inc(x_in[u], 16)

                for m in range(4):
                    if m >= 2:
                        sp.wait_ge(x_in[m % 2], 16)
                    load(m, m % 2, 0)

                def body(n, u, k, last):
                    if inside(last, 4):
                        sp.wait_ge(x_in[u], 16 * (k + 2))
                        load(n + 4, u, k)
                    sp.wait_ge(s["qk_split"], n + 3)
                    sp.dma_start(dram["qk"].rearrange("a (m p) t -> p (a m) t", p=P)[:, :, ds(n * TILE + P, TILE)],
                                 qk[:, u].rearrange("p a m t -> p (a m) t").bitcast(F32)).then_inc(qk_out[u], 16)
                    sp.wait_ge(s["v_split"], n + 3)
                    sp.dma_start(dram["v"][ds(n * TILE + P, TILE), :].rearrange("(s p) c -> p s c", p=P),
                                 v_rows[:, u].rearrange("p s h c -> p s (h c)")).then_inc(v_out[u], 16)

                steps(sp, body)
                for u in range(2):
                    sp.wait_ge(qk_out[u], 16 * (STEPS // 2 + 1))
                    sp.wait_ge(v_out[u], 16 * (STEPS // 2 + 1))

            @block.gpsimd
            def _(pool):
                pool.sem_inc(s["qk_split"], 2)
                pool.sem_inc(s["v_rest_ready"], 2)
                pool.sem_inc(s["v_split"], 2)
                for u in range(2):
                    pool.sem_inc(qk_out[u], 16)
                    pool.sem_inc(v_out[u], 16)
                for u in range(2):
                    nc.gpsimd.tensor_copy(v_rows[:, u, :, :, 3 * HD:VROW], g.v_ones[:])

                def find_rstd(m, u, passed):
                    order = OwnOrder(pool, s["pool_own"], passed)
                    pool.wait_ge(s["guess_ready"], m + 1)
                    rsqrt(nc, order, rstd[:, u], guess[:, u], minus_half_var[:, u], newt[:, u],
                          g).then_inc(s["rstd_ready"], 1)
                    return order.n

                per = 0
                for m in range(3):
                    per = find_rstd(m, m % 2, m * per)

                def body(n, u, k, last):
                    if inside(last, 3):
                        find_rstd(n + 3, 1 - u, (n + 3) * per)
                    pool.wait_ge(s["v_rest_ready"], n + 3)
                    nc.gpsimd.tensor_tensor(g.scrap[:, 2:3], g.scrap[:, 1:2], g.scrap[:, 1:2], ALU.add)
                    rest = v_rest[:, u].rearrange("p s (h d) -> p s h d", h=H)
                    nc.gpsimd.tensor_copy(v_rows[:, u, :, :, HD:2 * HD], rest).then_inc(s["v_1"], 1)
                    pool.wait_ge(s["v_1"], n + 1)
                    for c in range(SUB):
                        last_ins = nc.gpsimd.tensor_tensor(
                            v_rows[:, u, c, :, 2 * HD:3 * HD], rest[:, c],
                            v_rows[:, u, c, :, HD:2 * HD], ALU.subtract)
                    last_ins.then_inc(s["v_split"], 1)

                steps(pool, body)

            @block.scalar
            def _(act):
                def evacuate_h(m, u, batch):
                    act.wait_ge(s["h_transposed"], m + 1)
                    for kd in range(KD):
                        sc = g.scale_a[:].rearrange("p b m -> p (b m)")[:, ds(batch * KD + kd, 1)]
                        sh = g.shift_a[:].rearrange("p b m -> p (b m)")[:, ds(batch * KD + kd, 1)]
                        nc.scalar.activation(h_t[:, u, kd], h_ps[:, kd], ACT.Identity, bias=sh, scale=sc)
                        last_ins = nc.scalar.activation(h_hi[:, u, kd], h_ps[:, kd], ACT.Identity, bias=sh, scale=sc)
                    last_ins.then_inc(s["hi_ready"], 1)

                evacuate_h(0, 0, 0)

                def body(n, u, k, last):
                    if inside(last, 1):
                        evacuate_h(n + 1, 1 - u, (n + 1) // (STEPS // B))
                    act.wait_ge(s["qk_done"], n + 1)
                    act.wait_ge(qk_out[u], 16 * (k + 1))
                    for half in range(2):
                        last_ins = nc.scalar.activation(
                            qk[:, u, 0, 2 * half:2 * half + 2].rearrange("p m t -> p (m t)"),
                            qk_ps[:, u, half], ACT.Copy)
                    last_ins.then_inc(s["qk_hi"], 1)
                    act.wait_ge(s["v_done"], n + 1)
                    act.wait_ge(v_out[u], 16 * (k + 1))
                    for c in range(SUB):
                        last_ins = nc.scalar.activation(v_rows[:, u, c, :, 0:HD],
                                                        v_ps[:, u, c].rearrange("p (h d) -> p h d", h=H), ACT.Copy)
                    last_ins.then_inc(s["v_0"], 1)

                steps(act, body)

            @block.vector
            def _(dve):
                def take_stats(m, u, k, passed):
                    order = OwnOrder(dve, s["dve_own"], passed)
                    dve.wait_ge(x_in[u], 16 * (k + 1))
                    apart(nc, g)
                    for c in range(SUB):
                        order(nc.vector.bn_stats(stats[:, u, c], g.x[:, ds(m * SUB + c, 1), :].rearrange("p a d -> p (a d)")))
                    order.wait()
                    apart(nc, g)
                    for c in range(SUB):
                        order(nc.vector.bn_aggr(mean_var[:, u, c], stats[:, u, c]))
                    order.wait()
                    order(nc.vector.tensor_scalar(minus_half_var[:, u], mean_var[:, u, :, 1], EPS, -0.5,
                                                  ALU.add, ALU.mult))
                    order.step(nc.vector.tensor_scalar(var[:, u], mean_var[:, u, :, 1], EPS, None, ALU.add))
                    nc.vector.tensor_scalar(guess[:, u], var[:, u].bitcast(I32), 1, -1, ALU.logical_shift_right,
                                            ALU.bitwise_xor).then_inc(s["guess_ready"], 1)
                    return order.n

                def normalise(m, u):
                    dve.wait_ge(s["rstd_ready"], m + 1)
                    for c in range(SUB):
                        last_ins = nc.vector.tensor_scalar(
                            xn[:, u, c], g.x[:, ds(m * SUB + c, 1), :].rearrange("p a d -> p (a d)"),
                            mean_var[:, u, c, 0:1], rstd[:, u, c:c + 1], ALU.subtract, ALU.mult)
                    last_ins.then_inc(s["xn_ready"], 1)

                def rest_of_h(m, u):
                    dve.wait_ge(s["hi_ready"], m + 1)
                    nc.vector.tensor_tensor(h_lo[:, u], h_t[:, u], h_hi[:, u].bitcast(F32),
                                            ALU.subtract).then_inc(s["lo_ready"], 1)

                per = take_stats(0, 0, 0, 0)
                take_stats(1, 1, 0, per)
                normalise(0, 0)
                take_stats(2, 0, 1, 2 * per)
                normalise(1, 1)
                rest_of_h(0, 0)

                def body(n, u, k, last):
                    if inside(last, 1):
                        rest_of_h(n + 1, 1 - u)
                    if inside(last, 2):
                        dve.wait_ge(s["h_transposed"], n + 1)
                        normalise(n + 2, u)
                    if inside(last, 3):
                        take_stats(n + 3, 1 - u, k + 1 + u, (n + 3) * per)
                    dve.wait_ge(s["qk_hi"], n + 1)
                    for half in range(2):
                        last_ins = nc.vector.tensor_tensor(
                            qk[:, u, 1, 2 * half:2 * half + 2].rearrange("p m t -> p (m t)"), qk_ps[:, u, half],
                            qk[:, u, 0, 2 * half:2 * half + 2].rearrange("p m t -> p (m t)").bitcast(F32), ALU.subtract)
                    last_ins.then_inc(s["qk_split"], 1)
                    dve.wait_ge(s["v_0"], n + 1)
                    dve.wait_ge(s["v_split"], n + 1)
                    for c in range(SUB):
                        last_ins = nc.vector.tensor_tensor(
                            v_rest[:, u, c].rearrange("p (h d) -> p h d", h=H),
                            v_ps[:, u, c].rearrange("p (h d) -> p h d", h=H), v_rows[:, u, c, :, 0:HD], ALU.subtract)
                    last_ins.then_inc(s["v_rest_ready"], 1)

                steps(dve, body)

            @block.tensor
            def _(pe):
                def transpose_h(m, u):
                    pe.wait_ge(s["xn_ready"], m + 1)
                    for kd in range(KD):
                        for c in range(SUB):
                            last_ins = nc.tensor.transpose(h_ps[:, kd, c * P:(c + 1) * P],
                                                           xn[:, u, c, kd * P:(kd + 1) * P], g.ident[:])
                    last_ins.then_inc(s["h_transposed"], 1)

                transpose_h(0, 0)

                def body(n, u, k, last):
                    pe.wait_ge(s["lo_ready"], n + 1)
                    if inside(last, 1):
                        transpose_h(n + 1, 1 - u)
                    pe.wait_ge(s["qk_split"], n + 1)
                    for m in range(4):
                        products(nc, qk_ps[:, u, m // 2, (m % 2) * TILE:(m % 2 + 1) * TILE],
                                 [(g.wqkv_hi[:, kd, m * P:(m + 1) * P], g.wqkv_lo[:, kd, m * P:(m + 1) * P],
                                   h_hi[:, u, kd], h_lo[:, u, kd]) for kd in range(KD)], s["qk_done"] if m == 3 else None)
                    pe.wait_ge(s["v_rest_ready"], n + 1)
                    for c in range(SUB):
                        cols = slice(c * P, (c + 1) * P)
                        last_ins = products(nc, v_ps[:, u, c],
                                            [(h_hi[:, u, kd, cols], h_lo[:, u, kd, cols],
                                              g.wqkv_hi[:, kd, 2 * D:3 * D], g.wqkv_lo[:, kd, 2 * D:3 * D])
                                             for kd in range(KD)], None)
                    last_ins.then_inc(s["v_done"], 1)

                steps(pe, body)


def products(nc, out, operands, done):
    n = len(operands)
    for i, (l_hi, l_lo, r_hi, r_lo) in enumerate(operands):
        nc.tensor.matmul(out, l_lo, r_hi, start=(i == 0), stop=False)
        nc.tensor.matmul(out, l_hi, r_lo, start=False, stop=False)
        last = nc.tensor.matmul(out, l_hi, r_hi, start=False, stop=(i == n - 1))
    if done is not None:
        last.then_inc(done, 1)
    return last


def attend(nc, g, dram):
    with ExitStack() as stack:
        t = Tensors(nc, stack)
        q_stack = t.sb("q_stack", [4 * HD, 2, H, P], F32R)
        k_stack = t.sb("k_stack", [4 * HD, 2, H, 2 * P], F32R)
        v_win = t.sb("v_win", [P, 2, 2, H * VROW], BF16)
        neg_max = t.sb("neg_max", [P, 2, 2])
        probs = t.sb("probs", [P, 2, 2, 2 * P])
        pt_hi = t.sb("pt_hi", [P, 2, 4, P], F16)
        pt_lo = t.sb("pt_lo", [P, 2, 4, P], F16)
        sums = t.sb("inv_sums", [P, 2, PAIRS])
        att_raw = t.sb("att_raw", [P, 2, PAIRS, HD])
        att = t.sb("att", [P, 2, PAIRS, HD])
        att_t = t.sb("att_t", [P, KD, P])
        gated = t.sb("gated", [P, D])
        stats = t.sb("stats2", [P, 6])
        mean_var = t.sb("mean_var2", [P, 2])
        var = t.sb("var2", [P, 1])
        minus_half_var = t.sb("minus_half_var2", [P, 1])
        guess = t.sb("guess2", [P, 1], I32)
        rstd = t.sb("rstd2", [P, 1])
        newt = t.sb("newt2", [P, 1])
        xn = t.sb("xn2", [P, D])
        h_mul = t.sb("h_mul", [P, D])
        h = t.sb("h2", [P, 2, D])
        h_t = t.sb("h2_t", [P, KD, P])
        s_ps = t.ps("s_ps", [P, 2, 512])
        pt_ps = t.ps("pt_ps", [P, 2, 512])
        o_ps = t.ps("o_ps", [P, 2, 512])
        wo_ps = t.ps("wo_ps", [P, 512])
        h_ps = t.ps("h2_ps", [P, 512])
        qkv_in = [t.sem(f"qkv_in{u}") for u in range(2)]
        h_out = [t.sem(f"h_out{u}") for u in range(2)]
        names = ("scored", "max_ready", "exp_done", "p_transposed", "hi_done", "lo_done", "pv_done", "o_used",
                 "att_ready", "att_transposed", "att_t_ready", "wo_done", "wo_used", "guess_ready",
                 "rstd_ready", "xn_ready", "h_ready", "h_transposed", "h_t_ready", "logits_done",
                 "logits_used", "dve_own", "pool_own")
        s = {n: t.sem("a_" + n) for n in names}
        LOADS = 9

        def chunks(eng, body, epilogue=None):
            body(0, 0, 0, True, False)
            body(1, 1, 0, False, False)
            with eng.Fori(1, CHUNKS // 2 - 1) as k:
                for u in range(2):
                    body(2 * k + u, u, k, False, False)
            body(CHUNKS - 2, 0, CHUNKS // 2 - 1, False, False)
            body(CHUNKS - 1, 1, CHUNKS // 2 - 1, False, True)
            if epilogue:
                epilogue(CHUNKS, 0)

        with nc.Block() as block:

            @block.sync
            def _(sp):
                def load(c, u):
                    for part in range(4):
                        rows = slice(part * HD, (part + 1) * HD)
                        q = dram["qk"][part // 2, 0:D, ds(c * P + P, P)].rearrange("(h d) t -> d h t", d=HD)
                        k = dram["qk"][part % 2, D:2 * D, ds(c * P, 2 * P)].rearrange("(h d) t -> d h t", d=HD)
                        sp.dma_start(q_stack[rows, u].bitcast(F32), q).then_inc(qkv_in[u], 16)
                        sp.dma_start(k_stack[rows, u].bitcast(F32), k).then_inc(qkv_in[u], 16)
                    sp.dma_start(v_win[:, u], dram["v"][ds(c * P, 2 * P), :].rearrange("(w p) n -> p w n", p=P)
                                 ).then_inc(qkv_in[u], 16)

                def store_h(c, u):
                    sp.wait_ge(s["h_ready"], c)
                    sp.dma_start(dram["h_rows"][ds(c * P - P, P), :], h[:, 1 - u, :]).then_inc(h_out[1 - u], 16)

                load(0, 0)
                load(1, 1)

                def body(c, u, k, first, last):
                    if not first:
                        store_h(c, u)
                    if not isinstance(c, int) or c + 2 < CHUNKS:
                        sp.wait_ge(s["pv_done"], 8 * c + 8 + 2)
                        load(c + 2, u)

                chunks(sp, body, store_h)
                for u in range(2):
                    sp.wait_ge(h_out[u], 16 * (CHUNKS // 2 + 1))

            @block.gpsimd
            def _(pool):
                for name, n in (("p_transposed", 2), ("pv_done", 2), ("o_used", 2), ("att_transposed", 1),
                                ("wo_used", 1), ("logits_used", 1)):
                    pool.sem_inc(s[name], n)
                for u in range(2):
                    pool.sem_inc(h_out[u], 16)
                OWN = 13

                def after(c, u):
                    order = OwnOrder(pool, s["pool_own"], (c - 1) * OWN)
                    pool.wait_ge(s["guess_ready"], c)
                    rsqrt(nc, order, rstd[:], guess[:], minus_half_var[:], newt[:], g).then_inc(s["rstd_ready"], 1)
                    batch = (c - 1) // (CHUNKS // B)
                    pool.wait_ge(s["xn_ready"], c)
                    order.step(nc.gpsimd.tensor_tensor(
                        h_mul[:], xn[:], g.scale_b[:, ds(batch, 1), :].rearrange("p a d -> p (a d)"), ALU.mult))
                    pool.wait_ge(h_out[1 - u], 16 * ((c - 1) // 2 + 1))
                    nc.gpsimd.tensor_tensor(
                        h[:, 1 - u], h_mul[:], g.shift_b[:, ds(batch, 1), :].rearrange("p a d -> p (a d)"),
                        ALU.add).then_inc(s["h_ready"], 1)
                    assert order.n == OWN

                chunks(pool, lambda c, u, k, first, last: None if first else after(c, u), after)

            @block.scalar
            def _(act):
                def exps(n, p):
                    r = p % 2
                    act.wait_ge(s["max_ready"], n + 1)
                    act.wait_ge(s["p_transposed"], n + 1)
                    for i in range(2):
                        last_ins = nc.scalar.activation(probs[:, r, i], s_ps[:, r, i * 2 * P:(i + 1) * 2 * P],
                                                        ACT.Exp, bias=neg_max[:, r, i:i + 1])
                    last_ins.then_inc(s["exp_done"], 1)

                def att_evac(c):
                    act.wait_ge(s["att_transposed"], c + 1)
                    nc.scalar.activation(att_t[:].rearrange("p k t -> p (k t)"), wo_ps[:, 0:D],
                                         ACT.Copy).then_inc(s["att_t_ready"], 1)

                def h_evac(c):
                    act.wait_ge(s["h_transposed"], c)
                    nc.scalar.activation(h_t[:].rearrange("p k t -> p (k t)"), h_ps[:, 0:D],
                                         ACT.Copy).then_inc(s["h_t_ready"], 1)

                exps(0, 0)

                def body(c, u, k, first, last):
                    for p in range(PAIRS):
                        n = 8 * c + p
                        if not (last and p == PAIRS - 1):
                            exps(n + 1, p + 1)
                        act.wait_ge(s["p_transposed"], n + 3)
                        act.wait_ge(s["pv_done"], n + 1)
                        nc.scalar.activation(pt_hi[:, p % 2].rearrange("p a t -> p (a t)"), pt_ps[:, p % 2],
                                             ACT.Copy).then_inc(s["hi_done"], 1)
                        if p == 1 and not first:
                            att_evac(c)
                        if p == 7 and not first:
                            h_evac(c)

                def epilogue(c, u):
                    att_evac(c)
                    h_evac(c)

                chunks(act, body, epilogue)

            @block.vector
            def _(dve):
                def row_max(n, p):
                    dve.wait_ge(s["scored"], n + 1)
                    nc.vector.tensor_reduce(neg_max[:, p % 2, :], s_ps[:, p % 2].rearrange("p (i t) -> p i t", i=2),
                                            AX.X, ALU.max, negate=True).then_inc(s["max_ready"], 1)

                def evacuate_o(c, half, order):
                    dve.wait_ge(s["pv_done"], 8 * c + 4 * half + 4 + 2)
                    o = o_ps[:, half, 0:PAIRS * VROW].rearrange("p (h c) -> p h c", h=PAIRS)
                    order(nc.vector.tensor_reduce(
                        att_raw[:, half], o[:, :, 0:3 * HD].rearrange("p h (a d) -> p h d a", a=3), AX.X, ALU.add))
                    nc.vector.reciprocal(sums[:, half], o[:, :, 3 * HD]).then_inc(s["o_used"], 1)
                    order.wait()
                    dve.wait_ge(s["o_used"], 2 * c + half + 3)
                    if half == 0:
                        dve.wait_ge(s["att_transposed"], c + 1)
                    nc.vector.tensor_tensor(
                        att[:, half], att_raw[:, half], sums[:, half].unsqueeze(2).broadcast_to([P, PAIRS, HD]),
                        ALU.mult).then_inc(s["att_ready"], 1)

                def residual(c, order):
                    dve.wait_ge(s["wo_done"], c)
                    batch = (c - 1) // (CHUNKS // B)
                    x = g.x[:, ds(c - 1, 1), :].rearrange("p a d -> p (a d)")
                    nc.vector.tensor_tensor(gated[:], wo_ps[:, D:2 * D],
                                            g.gate_a[:, ds(batch, 1), :].rearrange("p a d -> p (a d)"),
                                            ALU.mult).then_inc(s["wo_used"], 1)
                    dve.wait_ge(s["wo_used"], c + 1)
                    order(nc.vector.tensor_tensor(x, x, gated[:], ALU.add))
                    order.wait()
                    apart(nc, g)
                    order(nc.vector.bn_stats(stats[:], x))
                    order.wait()
                    apart(nc, g)
                    order.step(nc.vector.bn_aggr(mean_var[:], stats[:]))
                    order(nc.vector.tensor_scalar(minus_half_var[:], mean_var[:, 1:2], EPS, -0.5, ALU.add, ALU.mult))
                    order.step(nc.vector.tensor_scalar(var[:], mean_var[:, 1:2], EPS, None, ALU.add))
                    nc.vector.tensor_scalar(guess[:], var[:].bitcast(I32), 1, -1, ALU.logical_shift_right,
                                            ALU.bitwise_xor).then_inc(s["guess_ready"], 1)

                def normalise(c):
                    dve.wait_ge(s["rstd_ready"], c)
                    x = g.x[:, ds(c - 1, 1), :].rearrange("p a d -> p (a d)")
                    nc.vector.tensor_scalar(xn[:], x, mean_var[:, 0:1], rstd[:, 0:1], ALU.subtract,
                                            ALU.mult).then_inc(s["xn_ready"], 1)

                def keep_logits(c):
                    dve.wait_ge(s["logits_done"], c)
                    nc.vector.tensor_copy(g.logits[:, ds(c - 1, 1), :].rearrange("p a e -> p (a e)"),
                                          h_ps[:, D:D + E]).then_inc(s["logits_used"], 1)

                row_max(0, 0)
                row_max(1, 1)
                EVAC, RES = 1, 5

                def body(c, u, k, first, last):
                    for p in range(PAIRS):
                        n = 8 * c + p
                        dve.wait_ge(s["hi_done"], n + 1)
                        nc.vector.tensor_tensor(pt_lo[:, p % 2].rearrange("p a t -> p (a t)"), pt_ps[:, p % 2],
                                                pt_hi[:, p % 2].rearrange("p a t -> p (a t)"),
                                                ALU.subtract).then_inc(s["lo_done"], 1)
                        if not (last and p >= PAIRS - 2):
                            row_max(n + 2, p)
                        if p == 0 and not first:
                            evacuate_o(c - 1, 1, OwnOrder(dve, s["dve_own"], (2 * EVAC + RES) * (c - 1) + EVAC))
                        if p == 3 and not first:
                            residual(c, OwnOrder(dve, s["dve_own"], (2 * EVAC + RES) * (c - 1) + 2 * EVAC))
                        if p == 4:
                            evacuate_o(c, 0, OwnOrder(dve, s["dve_own"], (2 * EVAC + RES) * c))
                        if p == 5 and not first:
                            normalise(c)
                        if p == 7 and not first:
                            keep_logits(c)

                def epilogue(c, u):
                    evacuate_o(c - 1, 1, OwnOrder(dve, s["dve_own"], (2 * EVAC + RES) * (c - 1) + EVAC))
                    residual(c, OwnOrder(dve, s["dve_own"], (2 * EVAC + RES) * (c - 1) + 2 * EVAC))
                    normalise(c)
                    keep_logits(c)

                chunks(dve, body, epilogue)

            @block.tensor
            def _(pe):
                def scores(n, p, u, k, guard=True):
                    r = p % 2
                    if p == 0:
                        pe.wait_ge(qkv_in[u], 16 * LOADS * (k + 1))
                    if guard:
                        pe.wait_ge(s["exp_done"], n - 1)
                    mask = g.mask[:, ds(k, 1), :].rearrange("p a t -> p (a t)") if u == 0 else g.mask[:, 1, :]
                    nc.tensor.matmul(s_ps[:, r], g.identb[:], mask, start=True, stop=False)
                    for i in range(2):
                        last_ins = nc.tensor.matmul(s_ps[:, r, i * 2 * P:(i + 1) * 2 * P], q_stack[:, u, 2 * p + i],
                                                    k_stack[:, u, 2 * p + i], start=False, stop=(i == 1))
                    last_ins.then_inc(s["scored"], 1)

                def transpose_probs(n, p):
                    pe.wait_ge(s["exp_done"], n + 1)
                    for i in range(2):
                        for w in range(2):
                            last_ins = nc.tensor.transpose(pt_ps[:, p % 2, (2 * i + w) * P:(2 * i + w + 1) * P],
                                                           probs[:, p % 2, i, w * P:(w + 1) * P], g.ident[:])
                    last_ins.then_inc(s["p_transposed"], 1)

                def weigh(c, n, p, u):
                    pe.wait_ge(s["lo_done"], n + 1)
                    half = p // 4
                    if p % 4 == 0:
                        pe.wait_ge(s["o_used"], 2 * c + half + 1)
                    for i in range(2):
                        head = 2 * p + i
                        col = (head % PAIRS) * VROW
                        for w in range(2):
                            for part, pt in enumerate((pt_lo, pt_hi)):
                                last_ins = nc.tensor.matmul(
                                    o_ps[:, half, col:col + VCOLS], pt[:, p % 2, 2 * i + w],
                                    v_win[:, u, w, head * VROW:head * VROW + VCOLS],
                                    start=(w == 0 and part == 0), stop=(w == 1 and part == 1))
                    last_ins.then_inc(s["pv_done"], 1)

                def transpose_att(c):
                    pe.wait_ge(s["att_ready"], 2 * c)
                    pe.wait_ge(s["wo_used"], c)
                    a = att[:].rearrange("p a h d -> p (a h d)")
                    for kd in range(KD):
                        last_ins = nc.tensor.transpose(wo_ps[:, kd * P:(kd + 1) * P], a[:, kd * P:(kd + 1) * P], g.ident[:])
                    last_ins.then_inc(s["att_transposed"], 1)

                def project_att(c):
                    pe.wait_ge(s["att_t_ready"], c)
                    for kd in range(KD):
                        last_ins = nc.tensor.matmul(wo_ps[:, D:2 * D], att_t[:, kd], g.wo[:, kd],
                                                    start=(kd == 0), stop=(kd == KD - 1))
                    last_ins.then_inc(s["wo_done"], 1)

                def transpose_h(c, u):
                    pe.wait_ge(s["h_ready"], c)
                    pe.wait_ge(s["logits_used"], c)
                    for kd in range(KD):
                        last_ins = nc.tensor.transpose(h_ps[:, kd * P:(kd + 1) * P], h[:, 1 - u, kd * P:(kd + 1) * P],
                                                       g.ident[:])
                    last_ins.then_inc(s["h_transposed"], 1)

                def route_h(c):
                    pe.wait_ge(s["h_t_ready"], c)
                    for kd in range(KD):
                        last_ins = nc.tensor.matmul(h_ps[:, D:D + E], h_t[:, kd], g.wg[:, kd],
                                                    start=(kd == 0), stop=(kd == KD - 1))
                    last_ins.then_inc(s["logits_done"], 1)

                scores(0, 0, 0, 0, guard=False)
                scores(1, 1, 0, 0, guard=False)
                transpose_probs(0, 0)

                def body(c, u, k, first, last):
                    for p in range(PAIRS):
                        n = 8 * c + p
                        if p == 1 and not first:
                            transpose_att(c)
                        if p == 3 and not first:
                            project_att(c)
                        if p == 7 and not first:
                            transpose_h(c, u)
                        if p < PAIRS - 2:
                            scores(n + 2, p + 2, u, k)
                        elif not last:
                            scores(n + 2, p + 2 - PAIRS, 1 - u, k + u)
                        if not (last and p == PAIRS - 1):
                            transpose_probs(n + 1, (p + 1) % PAIRS)
                        weigh(c, n, p, u)
                        if p == 7 and not first:
                            route_h(c)

                def epilogue(c, u):
                    transpose_att(c)
                    project_att(c)
                    transpose_h(c, u)
                    route_h(c)

                chunks(pe, body, epilogue)


def route(nc, g, dram):
    with ExitStack() as stack:
        t = Tensors(nc, stack)
        less_eight = t.sb("less_eight", [P, E])
        top = t.sb("top", [P, CHUNKS])
        onehot = t.sb("onehot", [P, CHUNKS, E])
        held = t.sb("held", [P, CHUNKS, E])
        counts = t.sb("counts", [P, CHUNKS, E])
        sums = t.sb("count_sums", [P, 2, CHUNKS, E])
        whole = t.sb("whole", [P, E], I32)
        tiles = t.sb("tiles", [P, E])
        tile_sums = t.sb("tile_sums", [P, 2, E])
        bounds = t.sb("bounds_f", [P, E + 1])
        rank_ps = t.ps("rank_ps", [P, 512])
        count_ps = t.ps("count_ps", [P, 512])
        raw_in, hi_done, lo_done, eight_ready, chosen, ranked, own = (
            t.sem("r_" + n) for n in ("raw_in", "hi_done", "lo_done", "eight_ready", "chosen", "ranked", "own"))

        with nc.Block() as block:

            @block.sync
            def _(sp):
                load_weights(sp, g, dram["w1s"], dram["w2s"], dram["w3s"], raw_in)
                sp.wait_ge(raw_in, 48)

            @block.scalar
            def _(act):
                for i in range(3):
                    act.wait_ge(raw_in, 48)
                    cols = slice(i * KD * F, (i + 1) * KD * F)
                    nc.scalar.activation(g.w_hi[:, 0, cols], g.raw[:, cols], ACT.Copy).then_inc(hi_done, 1)

            @block.gpsimd
            def _(pool):
                for e in range(E):
                    last = nc.gpsimd.memset(less_eight[:, e:e + 1], float(e - E))
                last.then_inc(eight_ready, 1)
                for i in range(3):
                    pool.wait_ge(hi_done, i + 1)
                    cols = slice(i * KD * F, (i + 1) * KD * F)
                    nc.gpsimd.tensor_tensor(g.w_lo[:, 0, cols], g.raw[:, cols], g.w_hi[:, 0, cols].bitcast(F32),
                                            ALU.subtract).then_inc(lo_done, 1)
                pool.wait_ge(lo_done, 3)

            @block.vector
            def _(dve):
                order = OwnOrder(dve, own)
                wide = [P, CHUNKS, E]
                order.step(nc.vector.tensor_reduce(top[:], g.logits[:], AX.X, ALU.max))
                order.step(nc.vector.tensor_tensor(onehot[:], g.logits[:], top[:].unsqueeze(2).broadcast_to(wide),
                                                   ALU.is_ge))
                dve.wait_ge(eight_ready, 1)
                experts = less_eight[:].unsqueeze(1).broadcast_to(wide)
                order.step(nc.vector.tensor_tensor(held[:], onehot[:], experts, ALU.mult))
                order.step(nc.vector.tensor_reduce(top[:], held[:], AX.X, ALU.min))
                nc.vector.tensor_tensor(onehot[:], experts, top[:].unsqueeze(2).broadcast_to(wide),
                                        ALU.is_equal).then_inc(chosen, 1)
                dve.wait_ge(ranked, 1)
                flat = lambda a: a.rearrange("p c e -> p (c e)")
                order(nc.vector.tensor_copy(flat(counts[:]), count_ps[:, 0:CHUNKS * E]))
                order.step(nc.vector.tensor_copy(flat(sums[:, 0]), count_ps[:, 0:CHUNKS * E]))
                now, d = 0, 1
                while d < CHUNKS:
                    order(nc.vector.tensor_tensor(sums[:, 1 - now, d:], sums[:, now, d:], sums[:, now, :CHUNKS - d],
                                                  ALU.add))
                    order.step(nc.vector.tensor_copy(sums[:, 1 - now, :d], sums[:, now, :d]))
                    now, d = 1 - now, 2 * d
                order.step(nc.vector.tensor_scalar(tiles[:], sums[:, now, CHUNKS - 1], float(TILE - 1), None, ALU.add))
                order.step(nc.vector.tensor_copy(whole[:], tiles[:]))
                order.step(nc.vector.tensor_scalar(whole[:], whole[:], TILE.bit_length() - 1, None,
                                                   ALU.logical_shift_right))
                order.step(nc.vector.tensor_copy(tiles[:], whole[:]))
                order.step(nc.vector.tensor_scalar(tiles[:], tiles[:], 1.0, None, ALU.max))
                order.step(nc.vector.tensor_copy(tile_sums[:, 0], tiles[:]))
                at, d = 0, 1
                while d < E:
                    order(nc.vector.tensor_tensor(tile_sums[:, 1 - at, d:], tile_sums[:, at, d:],
                                                  tile_sums[:, at, :E - d], ALU.add))
                    order.step(nc.vector.tensor_copy(tile_sums[:, 1 - at, :d], tile_sums[:, at, :d]))
                    at, d = 1 - at, 2 * d
                order(nc.vector.memset(bounds[:, 0:1], float(STEPS)))
                order(nc.vector.tensor_scalar(bounds[:, 1:], tile_sums[:, at], float(STEPS), None, ALU.add))
                order.step(nc.vector.tensor_tensor(tiles[:], tile_sums[:, at], tiles[:], ALU.subtract))
                order(nc.vector.tensor_copy(g.bounds[:], bounds[:]))
                order(nc.vector.tensor_scalar(tiles[:], tiles[:], float(TILE), None, ALU.mult))
                order.step(nc.vector.tensor_tensor(sums[:, now], sums[:, now], counts[:], ALU.subtract))
                order.step(nc.vector.tensor_tensor(sums[:, now], sums[:, now],
                                                   rank_ps[:, 0:CHUNKS * E].rearrange("p (c e) -> p c e", e=E), ALU.add))
                order.step(nc.vector.tensor_tensor(sums[:, now], sums[:, now],
                                                   tiles[:].unsqueeze(1).broadcast_to(wide), ALU.add))
                order.step(nc.vector.tensor_tensor(sums[:, now], sums[:, now], onehot[:], ALU.mult))
                order.step(nc.vector.tensor_reduce(top[:], sums[:, now], AX.X, ALU.add))
                order.step(nc.vector.tensor_copy(g.slots[:], top[:]))

            @block.tensor
            def _(pe):
                pe.wait_ge(chosen, 1)
                flat = onehot[:].rearrange("p c e -> p (c e)")
                nc.tensor.matmul(rank_ps[:, 0:CHUNKS * E], g.before[:], flat, start=True, stop=True)
                nc.tensor.matmul(count_ps[:, 0:CHUNKS * E], g.ones[:], flat, start=True, stop=True).then_inc(ranked, 1)


def load_weights(eng, g, w1, w2, w3, done):
    for i, w in enumerate((w1, w2, w3)):
        n = w.shape[1]
        eng.dma_start(g.raw[:, i * KD * F:(i + 1) * KD * F].rearrange("p (k n) -> p k n", n=n),
                      w.rearrange("(k p) n -> p k n", p=P)).then_inc(done, 16)


PIECES = 8
PIECE = 3 * KD * F // PIECES


def experts(nc, g, dram):
    with ExitStack() as stack:
        t = Tensors(nc, stack)
        rows = t.sb("rows", [P, SUB, D])
        index = t.sb("index", [P, SUB], U32)
        h_hi = t.sb("e_h_hi", [P, KD, TILE], F32R)
        h_lo = t.sb("e_h_lo", [P, KD, TILE], F32R)
        gelu = t.sb("gelu", [P, 2, TILE])
        a = t.sb("a", [P, 3, TILE])
        a_hi = t.sb("a_hi", [P, KF, TILE], F32R)
        a_lo = t.sb("a_lo", [P, KF, TILE], F32R)
        gated = t.sb("gated_y", [P, SUB, D])
        y = t.sb("y", [P, SUB, D])
        gu_ps = t.ps("gu_ps", [P, 4, 512])
        h_ps = t.ps("e_h_ps", [P, KD, TILE])
        y_ps = t.ps("y_ps", [P, SUB, 512])
        names = ("rows_in", "scattered", "index_ready", "h_transposed", "h_hi_ready", "h_ready", "gu_done", "gelu_done",
                 "mul_done", "a_hi_done", "a_ready", "y_done", "gated_ready", "y_used", "y_out", "raw_in",
                 "hi_split", "lo_split", "all_stored")
        s = {n: t.sem("e_" + n) for n in names}

        def tiles(eng, body, before=None):
            body(0, 0, 0, False, False)
            with eng.Fori(1, STEPS - 1) as i:
                body(i, 0, None, False, False)
            body(STEPS - 1, 0, None, False, True)

            def expert(e, slot, more):
                first = eng.value_load(g.bounds[0:1, ds(e, 1)], min_val=STEPS, max_val=STEPS + TILES_MAX - 1)
                end = eng.value_load(g.bounds[0:1, ds(e + 1, 1)], min_val=STEPS + 1, max_val=STEPS + TILES_MAX)
                if before:
                    before(e)
                body(first, slot, e + 1 if more else None, True, False)
                with eng.If(end > first + 1):
                    with eng.Fori(first + 1, end) as i:
                        body(i, slot, None, True, False)

            with eng.Fori(0, E // 2 - 1) as k:
                for u in range(2):
                    expert(2 * k + u, (u + 1) % 2, True)
            for e in (E - 2, E - 1):
                expert(e, (e + 1) % 2, e < E - 1)

        def load_next_weights(pool, e):
            load_weights(pool, g, *(dram[n][ds(e, 1)].rearrange("a k n -> (a k) n") for n in ("W1", "W2", "W3")),
                         s["raw_in"])

        with nc.Block() as block:

            @block.sync
            def _(sp):
                def load(source, at):
                    sp.dma_start(rows[:], dram[source][ds(at, TILE), :].rearrange("(s p) d -> p s d", p=P)
                                 ).then_inc(s["rows_in"], 16)

                def body(i, slot, nxt, routed, last):
                    snap = (lambda v: v) if isinstance(i, int) else (lambda v: sp.snap(sp.to_reg(v)))
                    scattered = snap(SUB * 16 * (i + 1))
                    at = snap((i + 1 - STEPS if routed or last else i + 1) * TILE)
                    sp.wait_ge(s["h_transposed"], i + 1)
                    if not routed:
                        sp.wait_ge(s["scattered"], scattered)
                    load("h_sorted" if routed or last else "h_rows", at)
                    if routed:
                        at = snap((i - STEPS) * TILE)
                        sp.wait_ge(s["y_used"], i + 2)
                        sp.dma_start(dram["y_sorted"][ds(at, TILE), :].rearrange(
                            "(s p) d -> p s d", p=P), y[:]).then_inc(s["y_out"], 16)

                load("h_rows", 0)
                tiles(sp, body)
                end = sp.value_load(g.bounds[0:1, E:E + 1], min_val=STEPS + E, max_val=STEPS + TILES_MAX)
                y_all, rows_all = sp.snap(sp.to_reg(16 * end)), sp.snap(sp.to_reg(16 * (end + 1)))
                sp.wait_ge(s["y_out"], y_all)
                sp.wait_ge(s["rows_in"], rows_all)
                sp.sem_inc(s["all_stored"], 1)

            @block.gpsimd
            def _(pool):
                pool.sem_inc(s["mul_done"], 4)
                pool.sem_inc(s["y_used"], 1)
                pool.sem_inc(s["y_out"], 16 * STEPS)
                load_next_weights(pool, 0)

                def body(i, slot, nxt, routed, last):
                    if not routed:
                        pool.wait_ge(s["rows_in"], 16 * (i + 1))
                        nc.gpsimd.tensor_tensor(g.scrap[:, 2:3], g.scrap[:, 1:2], g.scrap[:, 1:2], ALU.add)
                        nc.gpsimd.tensor_copy(index[:], g.slots[:, ds(i * SUB, SUB)]).then_inc(s["index_ready"], 1)
                        pool.wait_ge(s["index_ready"], i + 1)
                        nc.gpsimd.tensor_tensor(g.scrap[:, 3:4], g.scrap[:, 1:2], g.scrap[:, 1:2], ALU.add)
                        for c in range(SUB):
                            nc.gpsimd.indirect_dma_start(
                                out=dram["h_sorted"][:, :],
                                out_offset=bass.IndirectOffsetOnAxis(ap=index[:, c:c + 1], axis=0),
                                in_=rows[:, c, :], in_offset=None).then_inc(s["scattered"], 16)
                        if last:
                            pool.wait_ge(s["scattered"], SUB * 16 * STEPS)
                        else:
                            pool.wait_ge(s["scattered"], SUB * 16 * (i + 1))
                    if nxt is not None:
                        for p in range(PIECES):
                            pool.wait_ge(s["hi_split"], PIECES * nxt + p + 1)
                            cols = slice(p * PIECE, (p + 1) * PIECE)
                            ins = nc.gpsimd.tensor_tensor(g.w_lo[:, 1 - slot, cols], g.raw[:, cols],
                                                          g.w_hi[:, 1 - slot, cols].bitcast(F32), ALU.subtract)
                        ins.then_inc(s["lo_split"], 1)
                        if not isinstance(nxt, int) or nxt + 1 < E:
                            pool.wait_ge(s["lo_split"], nxt + 1)
                            nc.gpsimd.tensor_tensor(g.scrap[:, 4:5], g.scrap[:, 1:2], g.scrap[:, 1:2], ALU.add)
                            load_next_weights(pool, nxt + 1)

                tiles(pool, body)

            @block.scalar
            def _(act):
                def evacuate_h(i):
                    act.wait_ge(s["h_transposed"], i + 1)
                    nc.scalar.activation(h_hi[:], h_ps[:], ACT.Copy).then_inc(s["h_hi_ready"], 1)

                def body(i, slot, nxt, routed, last):
                    for j in range(KF):
                        act.wait_ge(s["gu_done"], KF * i + j + 1)
                        act.wait_ge(s["mul_done"], KF * i + j - 1 + 4)
                        nc.scalar.activation(gelu[:, j % 2], gu_ps[:, j % 4, 0:TILE], ACT.Gelu).then_inc(s["gelu_done"], 1)
                        if nxt is not None:
                            if j == 0:
                                act.wait_ge(s["raw_in"], 48 * (nxt + 1))
                            cols = slice(j * PIECE, (j + 1) * PIECE)
                            nc.scalar.activation(g.w_hi[:, 1 - slot, cols], g.raw[:, cols],
                                                 ACT.Copy).then_inc(s["hi_split"], 1)
                    evacuate_h(i + 1)
                    if routed:
                        act.wait_ge(s["y_done"], i + 1)
                        act.wait_ge(s["y_out"], 16 * i)
                        nc.scalar.activation(y[:], y_ps[:, :, 0:D], ACT.Copy).then_inc(s["y_used"], 1)

                evacuate_h(0)
                tiles(act, body)

            @block.vector
            def _(dve):
                def rest_of_h(i):
                    dve.wait_ge(s["h_hi_ready"], i + 1)
                    nc.vector.tensor_tensor(h_lo[:], h_ps[:], h_hi[:].bitcast(F32), ALU.subtract).then_inc(s["h_ready"], 1)

                def body(i, slot, nxt, routed, last):
                    def low(j):
                        dve.wait_ge(s["a_hi_done"], KF * i + j + 1)
                        nc.vector.tensor_tensor(a_lo[:, j], a[:, j % 3], a_hi[:, j].bitcast(F32),
                                                ALU.subtract).then_inc(s["a_ready"], 1)

                    for j in range(KF):
                        dve.wait_ge(s["gelu_done"], KF * i + j + 1)
                        nc.vector.tensor_tensor(a[:, j % 3], gelu[:, j % 2], gu_ps[:, j % 4, TILE:2 * TILE],
                                                ALU.mult).then_inc(s["mul_done"], 1)
                        if j:
                            low(j - 1)
                        dve.wait_ge(s["mul_done"], KF * i + j + 1 + 4)
                        nc.vector.tensor_copy(a_hi[:, j], a[:, j % 3]).then_inc(s["a_hi_done"], 1)
                    low(KF - 1)
                    rest_of_h(i + 1)
                    if not routed:
                        dve.wait_ge(s["y_done"], i + 1)
                        gate = g.gate_b[:, ds(i // (STEPS // B), 1), :]
                        for c in range(SUB):
                            ins = nc.vector.tensor_tensor(gated[:, c], y_ps[:, c, 0:D],
                                                          gate.rearrange("p a d -> p (a d)"), ALU.mult)
                        ins.then_inc(s["y_used"], 1)
                        dve.wait_ge(s["y_used"], i + 2)
                        x = g.x[:, ds(i * SUB, SUB), :]
                        nc.vector.tensor_tensor(x, x, gated[:], ALU.add).then_inc(s["gated_ready"], 1)

                rest_of_h(0)
                tiles(dve, body)

            @block.tensor
            def _(pe):
                def transpose_h(i):
                    pe.wait_ge(s["rows_in"], 16 * (i + 1))
                    for kd in range(KD):
                        for c in range(SUB):
                            ins = nc.tensor.transpose(h_ps[:, kd, c * P:(c + 1) * P], rows[:, c, kd * P:(kd + 1) * P],
                                                      g.ident[:])
                    ins.then_inc(s["h_transposed"], 1)

                def weights(slot, which, k, cols, n):
                    at = which * KD * F + k * n
                    cols = slice(at + cols.start, at + cols.stop)
                    return g.w_hi[:, slot, cols], g.w_lo[:, slot, cols]

                def body(i, slot, nxt, routed, last):
                    for j in range(KF):
                        if j == 0:
                            pe.wait_ge(s["h_ready"], i + 1)
                        pe.wait_ge(s["mul_done"], KF * i + j + 1)
                        cols = slice(j * P, (j + 1) * P)
                        for which in range(2):
                            products(nc, gu_ps[:, j % 4, which * TILE:(which + 1) * TILE],
                                     [(*weights(slot, which, kd, cols, F), h_hi[:, kd], h_lo[:, kd])
                                      for kd in range(KD)], s["gu_done"] if which else None)
                    transpose_h(i + 1)
                    pe.wait_ge(s["y_used"], i + 1)
                    for k in range(KF):
                        pe.wait_ge(s["a_ready"], KF * i + k + 1)
                        w_hi, w_lo = weights(slot, 2, k, slice(0, D), D)
                        for c in range(SUB):
                            cols = slice(c * P, (c + 1) * P)
                            out = y_ps[:, c, 0:D]
                            nc.tensor.matmul(out, a_lo[:, k, cols], w_hi, start=(k == 0), stop=False)
                            nc.tensor.matmul(out, a_hi[:, k, cols], w_lo, start=False, stop=False)
                            ins = nc.tensor.matmul(out, a_hi[:, k, cols], w_hi, start=False, stop=(k == KF - 1))
                    ins.then_inc(s["y_done"], 1)

                transpose_h(0)
                tiles(pe, body, lambda e: pe.wait_ge(s["lo_split"], e + 1))


def combine(nc, g, dram):
    with ExitStack() as stack:
        t = Tensors(nc, stack)
        index = t.sb("c_index", [P, 2, 1], U32)
        routed = t.sb("routed", [P, 2, D])
        gated = t.sb("c_gated", [P, 2, D])
        out = [t.sem(f"c_out{u}") for u in range(2)]
        fetched = [t.sem(f"c_fetched{u}") for u in range(2)]
        index_ready, used, ready, own = (t.sem("c_" + n) for n in ("index_ready", "used", "ready", "own"))

        with nc.Block() as block:

            @block.gpsimd
            def _(pool):
                pool.sem_inc(used, 2)
                with pool.Fori(0, CHUNKS // 2) as k:
                    for u in range(2):
                        c = 2 * k + u
                        pool.wait_ge(used, c + 1)
                        nc.gpsimd.tensor_tensor(g.scrap[:, 2:3], g.scrap[:, 1:2], g.scrap[:, 1:2], ALU.add)
                        nc.gpsimd.tensor_copy(index[:, u], g.slots[:, ds(c, 1)]).then_inc(index_ready, 1)
                        pool.wait_ge(index_ready, c + 1)
                        nc.gpsimd.tensor_tensor(g.scrap[:, 3:4], g.scrap[:, 1:2], g.scrap[:, 1:2], ALU.add)
                        nc.gpsimd.indirect_dma_start(
                            out=routed[:, u, :], out_offset=None, in_=dram["y_sorted"][:, :],
                            in_offset=bass.IndirectOffsetOnAxis(ap=index[:, u, 0:1], axis=0)
                        ).then_inc(fetched[u], 16)

            @block.vector
            def _(dve):
                with dve.Fori(0, CHUNKS // 2) as k:
                    for u in range(2):
                        c = 2 * k + u
                        dve.wait_ge(fetched[u], 16 * (k + 1))
                        flat = lambda a: a.rearrange("p a d -> p (a d)")
                        nc.vector.tensor_tensor(gated[:, u], routed[:, u],
                                                flat(g.gate_b[:, ds(c // (CHUNKS // B), 1), :]), ALU.mult).then_inc(used, 1)
                        dve.wait_ge(used, c + 3)
                        x = flat(g.x[:, ds(c, 1), :])
                        nc.vector.tensor_tensor(x, x, gated[:, u], ALU.add).then_inc(ready, 1)

            @block.sync
            def _(sp):
                with sp.Fori(0, CHUNKS // 2) as k:
                    for u in range(2):
                        c = 2 * k + u
                        sp.wait_ge(ready, c + 1)
                        sp.dma_start(dram["out"][ds(c * P, P), :],
                                     g.x[:, ds(c, 1), :].rearrange("p a d -> p (a d)")).then_inc(out[u], 16)
                for u in range(2):
                    sp.wait_ge(out[u], 16 * (CHUNKS // 2))


class Globals:

    def __init__(self, t):
        self.x = t.sb("x_res", [P, CHUNKS, D])
        self.ident = t.sb("ident", [P, P])
        self.before = t.sb("before", [P, P])
        self.ones = t.sb("ones", [P, P])
        self.magic = t.sb("magic", [P, SUB], I32)
        self.three_halves = t.sb("three_halves", [P, SUB])
        self.logits = t.sb("logits", [P, CHUNKS, E])
        self.scrap = t.sb("scrap", [P, 5])
        self.gate_b = t.sb("gate_b", [P, B, D])

    def for_attention(self, t):
        self.identb = t.sb("identb", [P, P], BF16)
        self.mask = t.sb("mask", [P, 16, 512], BF16)
        self.v_ones = t.sb("v_ones", [P, SUB, H, 2], BF16)
        self.wqkv_hi = t.sb("wqkv_hi", [P, KD, 3 * D], F32R)
        self.wqkv_lo = t.sb("wqkv_lo", [P, KD, 3 * D], F32R)
        self.wo = t.sb("wo_sb", [P, KD, D])
        self.wg = t.sb("wg_sb", [P, KD, E])
        self.shift_a = t.sb("shift_a", [P, B, KD])
        self.scale_a = t.sb("scale_a", [P, B, KD])
        self.gate_a = t.sb("gate_a", [P, B, D])
        self.shift_b = t.sb("shift_b", [P, B, D])
        self.scale_b = t.sb("scale_b", [P, B, D])

    def for_experts(self, t):
        self.slots = t.sb("slots", [P, CHUNKS], U32)
        self.bounds = t.sb("bounds", [P, E + 1], I32)
        self.w_hi = t.sb("w_hi", [P, 2, 3 * KD * F], F32R)
        self.w_lo = t.sb("w_lo", [P, 2, 3 * KD * F], F32R)
        self.raw = t.sb("w_raw", [P, 3 * KD * F])


def adaln_block(nc, dram, stages=9):
    for name, shape, dtype in (("qk", [2, 2 * D, T + P], F32), ("v", [T + P, H * VROW], BF16),
                               ("h_rows", [T, D], F32), ("h_sorted", [SORTED, D], F32),
                               ("y_sorted", [SORTED, D], F32)):
        dram[name] = nc.dram_tensor(name + "_scratch", shape, dtype, kind="Internal").ap()
    with ExitStack() as stack:
        g = Globals(Tensors(nc, stack))
        with ExitStack() as inner:
            g.for_attention(Tensors(nc, inner))
            setup(nc, g, dram)
            project(nc, g, dram)
            if stages >= 2:
                attend(nc, g, dram)
        if stages >= 3:
            g.for_experts(Tensors(nc, stack))
            route(nc, g, dram)
            experts(nc, g, dram)
            combine(nc, g, dram)


_INPUTS = {"x": "L0_attn_x", "wq": "L0_attn_Wq", "wk": "L0_attn_Wk", "wv": "L0_attn_Wv", "wo": "L0_attn_Wo",
           "w1s": "L0_ffn_w1s", "w2s": "L0_ffn_w2s", "w3s": "L0_ffn_w3s", "W1": "L0_ffn_W1", "W2": "L0_ffn_W2",
           "W3": "L0_ffn_W3", "wg": "L0_ffn_Wg", "c": "L0_c", "wmod": "L0_wmod"}


def kernel(**inputs):
    import numpy as np
    import concourse.bacc as bacc
    from concourse import mybir
    from concourse.bass_utils import run_bass_kernel_spmd

    nc = bacc.Bacc("TRN2", target_bir_lowering=False, num_devices=1)
    arrays, dram = {}, {}
    for short, name in _INPUTS.items():
        a = np.asarray(inputs[name])
        if short == "x":
            a = a.reshape(T, D)
        if short in ("wq", "wk", "wv", "wo", "c"):
            a = a.T
        arrays["in_" + short] = np.ascontiguousarray(a)
        dram[short] = nc.dram_tensor("in_" + short, a.shape, mybir.dt.from_np(a.dtype), kind="ExternalInput").ap()
    dram["out"] = nc.dram_tensor("out_0_dram", (T, D), mybir.dt.float32, kind="ExternalOutput").ap()
    adaln_block(nc, dram)
    r = run_bass_kernel_spmd(nc, [arrays], core_ids=[0])
    return r.results[0]["out_0_dram"].reshape(B, S, D)
```

```python
import concourse.bass as bass
from concourse import mybir
from contextlib import ExitStack

F32 = mybir.dt.float32
F32R = mybir.dt.float32r
BF16 = mybir.dt.bfloat16
F16 = mybir.dt.float16
I32 = mybir.dt.int32
U32 = mybir.dt.uint32
ALU = mybir.AluOpType
ACT = mybir.ActivationFunctionType
AX = mybir.AxisListType
ds = bass.ds

P = 128
B, S, D = 2, 2048, 256
T = B * S
KD = D // P
H, HD = 16, 16
F = 1024
KF = F // P
E = 8
CHUNKS = T // P
TILE = 256
SUB = TILE // P
STEPS = T // TILE
TILES_MAX = T // TILE + E
SORTED = (TILES_MAX + 1) * TILE
XROW = D + 2
EPS = 1e-5
MASKED = -1e30
VROW = 50
VCOLS = 3 * HD + 1
PAIRS = H // 2
RSQRT_MAGIC = 0x5F3759DF + 1


class OwnOrder:

    def __init__(self, eng, sem, passed=0):
        self.eng, self.sem, self.passed, self.n = eng, sem, passed, 0

    def __call__(self, ins):
        ins.then_inc(self.sem, 1)
        self.n += 1

    def wait(self):
        self.eng.wait_ge(self.sem, self.passed + self.n)

    def step(self, ins):
        self(ins)
        self.wait()


class Tensors:

    def __init__(self, nc, stack):
        self.nc, self.stack = nc, stack

    def sb(self, name, shape, dtype=F32):
        return self.stack.enter_context(self.nc.sbuf_tensor(name, shape, dtype))

    def ps(self, name, shape):
        return self.stack.enter_context(self.nc.psum_tensor(name, shape, F32))

    def sem(self, name):
        return self.stack.enter_context(self.nc.semaphore(name))


def rsqrt(nc, order, y, guess, v, t, g):
    n = y.shape[-1]
    order.step(nc.gpsimd.tensor_tensor(y.bitcast(I32), guess, g.magic[:, 0:n], ALU.add))
    for i in range(3):
        order.step(nc.gpsimd.tensor_tensor(t, y, y, ALU.mult))
        order.step(nc.gpsimd.tensor_tensor(t, t, v, ALU.mult))
        order.step(nc.gpsimd.tensor_tensor(t, t, g.three_halves[:, 0:n], ALU.add))
        last = nc.gpsimd.tensor_tensor(y, y, t, ALU.mult)
        if i < 2:
            order.step(last)
    return last


def apart(nc, g):
    nc.vector.tensor_copy(g.scrap[:, 0:1], g.scrap[:, 1:2])


def setup(nc, g, dram):
    with ExitStack() as stack:
        t = Tensors(nc, stack)
        cond = t.sb("cond", [P, KD, B])
        cond_e = t.sb("cond_e", [P, KD, B])
        cond_silu = t.sb("cond_silu", [P, KD, B])
        cond_wide = t.sb("cond_wide", [P, KD, B, P])
        wmod = t.sb("wmod", [P, KD, 6 * D])
        wqkv = t.sb("wqkv", [P, KD, 3 * D])
        zeros = g.zeros
        number = t.sb("number", [P, CHUNKS], I32)
        sign = t.sb("gate_sign", [P, B, D])
        size = t.sb("gate_size", [P, B, D])
        col_ps = t.ps("col_ps", [P, 512])
        row_ps = t.ps("row_ps", [P, 2, 512])
        cond_in, wmod_in, wq_in, wo_in = (t.sem(n) for n in ("cond_in", "wmod_in", "wq_in", "wo_in"))
        act_done, col_done, row_done, row_used = (
            t.sem(n) for n in ("s_act_done", "s_col_done", "s_row_done", "s_row_used"))
        silu_done, dve_own, pool_own, zeroed = (
            t.sem(n) for n in ("silu_done", "s_dve_own", "s_pool_own", "zeroed"))
        pad_out, zero_out = g.pad_out, g.zero_out

        with nc.Block() as block:

            @block.sync
            def _(sp):
                sp.dma_start(cond[:], dram["c"].rearrange("(k p) b -> p k b", p=P)).then_inc(cond_in, 16)
                sp.dma_start(wmod[:], dram["wmod"].rearrange("(k p) n -> p k n", p=P)).then_inc(wmod_in, 16)
                for i, w in enumerate(("wq", "wk", "wv")):
                    sp.dma_start(wqkv[:, :, i * D:(i + 1) * D],
                                 dram[w].rearrange("(k p) n -> p k n", p=P)).then_inc(wq_in, 16)
                sp.dma_start(g.wo[:], dram["wo"].rearrange("(k p) n -> p k n", p=P)).then_inc(wo_in, 16)
                sp.dma_start(g.wg[:], dram["wg"].rearrange("(k p) n -> p k n", p=P)).then_inc(wo_in, 16)
                sp.wait_ge(zeroed, 1)
                sp.dma_start(dram["qk"].rearrange("a f t -> (a f) t")[:, 0:P].rearrange("(m p) t -> p m t", p=P),
                             zeros[:, 0:8, 0:P]).then_inc(pad_out, 16)
                sp.dma_start(dram["v"][0:P, :].rearrange("p (a b) -> p a b", a=2),
                             zeros[:, 0:2, 0:H * VROW // 4].rearrange("p a b -> p a b").bitcast(BF16)
                             ).then_inc(pad_out, 16)
                for name, width in (("h_sorted", D), ("x_sorted", XROW)):
                    rows = dram[name].rearrange("(a p) d -> p a d", p=P)
                    for a in range(0, SORTED // P, 10):
                        n = min(10, SORTED // P - a)
                        sp.dma_start(rows[:, a:a + n, :], zeros[:, 0:n, 0:width]).then_inc(zero_out, 16)
                sp.wait_ge(cond_in, 16)
                sp.wait_ge(wo_in, 32)
                sp.wait_ge(pad_out, 32)

            @block.gpsimd
            def _(pool):
                order = OwnOrder(pool, pool_own)
                order.step(nc.gpsimd.memset(zeros[:], 0.0))
                order.step(nc.gpsimd.iota(number[:, 0:10], pattern=[[0, 5], [P, SUB]], base=T, channel_multiplier=1))
                order.step(nc.gpsimd.tensor_copy(zeros[:, :, D], number[:, 0:10]))
                pool.sem_inc(zeroed, 1)
                order.step(nc.gpsimd.iota(number[:], pattern=[[P, CHUNKS]], base=0, channel_multiplier=1))
                order(nc.gpsimd.tensor_copy(g.x[:, :, D], number[:]))
                for b in range(B):
                    order(nc.gpsimd.memset(g.x[:, b * CHUNKS // B:(b + 1) * CHUNKS // B, D + 1:XROW], float(b)))
                order(nc.gpsimd.memset(g.ident[:], 0.0))
                order(nc.gpsimd.memset(g.mask[:], 0.0))
                order(nc.gpsimd.memset(g.magic[:], RSQRT_MAGIC))
                order(nc.gpsimd.memset(g.scrap[:], 0.0))
                order(nc.gpsimd.memset(g.three_halves[:], 1.5))
                order(nc.gpsimd.memset(g.ones[:], 1.0))
                order.step(nc.gpsimd.memset(g.before[:], 1.0))
                order.step(nc.gpsimd.affine_select(
                    out=g.ident[:], in_=g.ident[:], compare_op=ALU.not_equal, fill=1.0, base=0,
                    pattern=[[-1, P]], channel_multiplier=1))
                order(nc.gpsimd.tensor_copy(g.identb[:], g.ident[:]))
                order(nc.gpsimd.affine_select(
                    out=g.before[:], in_=g.before[:], compare_op=ALU.is_gt, fill=0.0, base=0,
                    pattern=[[1, P]], channel_multiplier=-1))
                for m in range(2):
                    for head in range(2):
                        prev = g.mask[:, m, head * 256:head * 256 + P]
                        own = g.mask[:, m, head * 256 + P:head * 256 + 2 * P]
                        if m == 0:
                            order(nc.gpsimd.memset(prev, MASKED))
                        else:
                            order(nc.gpsimd.affine_select(
                                out=prev, in_=prev, compare_op=ALU.is_gt, fill=MASKED, base=0,
                                pattern=[[1, P]], channel_multiplier=-1))
                        order(nc.gpsimd.affine_select(
                            out=own, in_=own, compare_op=ALU.is_ge, fill=MASKED, base=0,
                            pattern=[[-1, P]], channel_multiplier=1))
                order.wait()

            @block.scalar
            def _(act):
                act.wait_ge(cond_in, 16)
                nc.scalar.activation(cond_e[:], cond[:], ACT.Exp, scale=-1.0).then_inc(act_done, 1)
                act.wait_ge(wq_in, 48)
                nc.scalar.activation(g.wqkv_hi[:, :, 0:D], wqkv[:, :, 0:D], ACT.Copy,
                                     scale=HD ** -0.5).then_inc(act_done, 1)
                nc.scalar.activation(g.wqkv_hi[:, :, D:3 * D], wqkv[:, :, D:3 * D], ACT.Copy).then_inc(act_done, 1)

            @block.vector
            def _(dve):
                order = OwnOrder(dve, dve_own)
                dve.wait_ge(act_done, 1)
                order.step(nc.vector.tensor_scalar(cond_e[:], cond_e[:], 1.0, None, ALU.add))
                order.step(nc.vector.reciprocal(cond_e[:], cond_e[:]))
                order.step(nc.vector.tensor_tensor(cond_silu[:], cond[:], cond_e[:], ALU.mult))
                nc.vector.tensor_copy(
                    cond_wide[:], cond_silu[:].unsqueeze(3).broadcast_to([P, KD, B, P])).then_inc(silu_done, 1)
                dve.wait_ge(col_done, 1)
                cols = col_ps[:, 0:2 * KD * B].rearrange("p (s m b) -> p s m b", s=2, m=KD)
                order(nc.vector.tensor_copy(g.shift_a[:], cols[:, 0].rearrange("p m b -> p b m")))
                order(nc.vector.tensor_scalar(g.scale_a[:], cols[:, 1].rearrange("p m b -> p b m"),
                                              1.0, None, ALU.add))
                for b in range(B):
                    dve.wait_ge(row_done, b + 1)
                    order(nc.vector.tensor_copy(g.gate_a[:, b, :], row_ps[:, 0, 0:D]))
                    order(nc.vector.tensor_copy(g.shift_b[:, b, :], row_ps[:, 0, D:2 * D]))
                    order(nc.vector.tensor_scalar(g.scale_b[:, b, :], row_ps[:, 1, 0:D], 1.0, None, ALU.add))
                    nc.vector.tensor_copy(g.gate_b[:, b, :], row_ps[:, 1, D:2 * D]).then_inc(row_used, 1)
                dve.wait_ge(row_used, B)
                order.wait()
                for gate in (g.gate_a, g.gate_b):
                    order.step(nc.vector.tensor_scalar(sign[:], gate[:], 0.0, 2.0, ALU.is_ge, ALU.mult))
                    order.step(nc.vector.tensor_scalar(sign[:], sign[:], 1.0, None, ALU.subtract))
                    order.step(nc.vector.tensor_tensor(size[:], gate[:], sign[:], ALU.mult))
                    order.step(nc.vector.tensor_scalar(size[:], size[:], 0.25, None, ALU.max))
                    order.step(nc.vector.tensor_tensor(gate[:], size[:], sign[:], ALU.mult))
                order(nc.vector.tensor_tensor(g.gate_step[:], g.gate_b[:, 1, :], g.gate_b[:, 0, :], ALU.subtract))
                dve.wait_ge(act_done, 3)
                order(nc.vector.scalar_tensor_tensor(
                    g.wqkv_lo[:, :, 0:D], wqkv[:, :, 0:D], HD ** -0.5, g.wqkv_hi[:, :, 0:D].bitcast(F32),
                    ALU.mult, ALU.subtract))
                order(nc.vector.tensor_tensor(g.wqkv_lo[:, :, D:3 * D], wqkv[:, :, D:3 * D],
                                              g.wqkv_hi[:, :, D:3 * D].bitcast(F32), ALU.subtract))
                order.wait()

            @block.tensor
            def _(pe):
                pe.wait_ge(silu_done, 1)
                pe.wait_ge(wmod_in, 16)
                for n in range(2 * KD):
                    for k in range(KD):
                        last = nc.tensor.matmul(col_ps[:, n * B:(n + 1) * B], wmod[:, k, n * P:(n + 1) * P],
                                                cond_silu[:, k, :], start=(k == 0), stop=(k == KD - 1))
                last.then_inc(col_done, 1)
                for b in range(B):
                    if b:
                        pe.wait_ge(row_used, b)
                    for half in range(2):
                        for k in range(KD):
                            last = nc.tensor.matmul(row_ps[:, half, :], cond_wide[:, k, b, :],
                                                    wmod[:, k, 2 * D + half * 512:2 * D + (half + 1) * 512],
                                                    start=(k == 0), stop=(k == KD - 1))
                    last.then_inc(row_done, 1)


def project(nc, g, dram):
    with ExitStack() as stack:
        t = Tensors(nc, stack)
        xn = t.sb("xn", [P, 2, SUB, D])
        h_t = t.sb("h_t", [P, 2, KD, TILE])
        h_hi = t.sb("h_hi", [P, 2, KD, TILE], F32R)
        h_lo = t.sb("h_lo", [P, 2, KD, TILE], F32R)
        qk = t.sb("qk_hilo", [P, 2, 2, 4, TILE], F32R)
        v_rows = t.sb("v_rows", [P, 2, SUB, H, VROW], BF16)
        v_rest = t.sb("v_rest", [P, 2, SUB, D])
        stats = t.sb("stats", [P, 2, SUB, 6])
        mean_var = t.sb("mean_var", [P, 2, SUB, 2])
        var = t.sb("var", [P, 2, SUB])
        minus_half_var = t.sb("minus_half_var", [P, 2, SUB])
        guess = t.sb("guess", [P, 2, SUB], I32)
        rstd = t.sb("rstd", [P, 2, SUB])
        newt = t.sb("newt", [P, 2, SUB])
        h_ps = t.ps("h_ps", [P, KD, TILE])
        qk_ps = t.ps("qk_ps", [P, 2, 2, 512])
        v_ps = t.ps("v_ps", [P, 2, SUB, D])
        x_in = [t.sem(f"x_in{u}") for u in range(2)]
        qk_out = [t.sem(f"qk_out{u}") for u in range(2)]
        v_out = [t.sem(f"v_out{u}") for u in range(2)]
        names = ("guess_ready", "rstd_ready", "xn_ready", "h_transposed", "hi_ready", "lo_ready",
                 "qk_done", "v_done", "qk_hi", "qk_split", "v_0", "v_1", "v_rest_ready", "v_split", "dve_own",
                 "pool_own")
        s = {n: t.sem("p_" + n) for n in names}

        def steps(eng, body):
            with eng.Fori(0, STEPS // 2 - 2) as k:
                for u in range(2):
                    body(2 * k + u, u, k, None)
            for k in range(STEPS // 2 - 2, STEPS // 2):
                for u in range(2):
                    body(2 * k + u, u, k, 2 * k + u)

        def inside(n, ahead):
            return n is None or n + ahead < STEPS

        with nc.Block() as block:

            @block.sync
            def _(sp):
                def load(m, u, k):
                    sp.dma_start(g.x[:, ds(m * SUB, SUB), 0:D],
                                 dram["x"][ds(m * TILE, TILE), :].rearrange("(s p) d -> p s d", p=P)
                                 ).then_inc(x_in[u], 16)

                for m in range(4):
                    if m >= 2:
                        sp.wait_ge(x_in[m % 2], 16)
                    load(m, m % 2, 0)

                def body(n, u, k, last):
                    if inside(last, 4):
                        sp.wait_ge(x_in[u], 16 * (k + 2))
                        load(n + 4, u, k)
                    sp.wait_ge(s["qk_split"], n + 3)
                    sp.dma_start(dram["qk"].rearrange("a (m p) t -> p (a m) t", p=P)[:, :, ds(n * TILE + P, TILE)],
                                 qk[:, u].rearrange("p a m t -> p (a m) t").bitcast(F32)).then_inc(qk_out[u], 16)
                    sp.wait_ge(s["v_split"], n + 3)
                    sp.dma_start(dram["v"][ds(n * TILE + P, TILE), :].rearrange("(s p) c -> p s c", p=P),
                                 v_rows[:, u].rearrange("p s h c -> p s (h c)")).then_inc(v_out[u], 16)

                steps(sp, body)
                for u in range(2):
                    sp.wait_ge(qk_out[u], 16 * (STEPS // 2 + 1))
                    sp.wait_ge(v_out[u], 16 * (STEPS // 2 + 1))

            @block.gpsimd
            def _(pool):
                pool.sem_inc(s["qk_split"], 2)
                pool.sem_inc(s["v_rest_ready"], 2)
                pool.sem_inc(s["v_split"], 2)
                for u in range(2):
                    pool.sem_inc(qk_out[u], 16)
                    pool.sem_inc(v_out[u], 16)
                for u in range(2):
                    nc.gpsimd.memset(v_rows[:, u, :, :, 3 * HD:VROW], 1.0)

                def find_rstd(m, u, passed):
                    order = OwnOrder(pool, s["pool_own"], passed)
                    pool.wait_ge(s["guess_ready"], m + 1)
                    rsqrt(nc, order, rstd[:, u], guess[:, u], minus_half_var[:, u], newt[:, u],
                          g).then_inc(s["rstd_ready"], 1)
                    return order.n

                per = 0
                for m in range(3):
                    per = find_rstd(m, m % 2, m * per)

                def body(n, u, k, last):
                    if inside(last, 3):
                        find_rstd(n + 3, 1 - u, (n + 3) * per)
                    pool.wait_ge(s["v_rest_ready"], n + 3)
                    nc.gpsimd.tensor_tensor(g.scrap[:, 2:3], g.scrap[:, 1:2], g.scrap[:, 1:2], ALU.add)
                    rest = v_rest[:, u].rearrange("p s (h d) -> p s h d", h=H)
                    nc.gpsimd.tensor_copy(v_rows[:, u, :, :, HD:2 * HD], rest).then_inc(s["v_1"], 1)
                    pool.wait_ge(s["v_1"], n + 1)
                    for c in range(SUB):
                        last_ins = nc.gpsimd.tensor_tensor(
                            v_rows[:, u, c, :, 2 * HD:3 * HD], rest[:, c],
                            v_rows[:, u, c, :, HD:2 * HD], ALU.subtract)
                    last_ins.then_inc(s["v_split"], 1)

                steps(pool, body)

            @block.scalar
            def _(act):
                def evacuate_h(m, u, batch):
                    act.wait_ge(s["h_transposed"], m + 1)
                    for kd in range(KD):
                        sc = g.scale_a[:].rearrange("p b m -> p (b m)")[:, ds(batch * KD + kd, 1)]
                        sh = g.shift_a[:].rearrange("p b m -> p (b m)")[:, ds(batch * KD + kd, 1)]
                        nc.scalar.activation(h_t[:, u, kd], h_ps[:, kd], ACT.Identity, bias=sh, scale=sc)
                        last_ins = nc.scalar.activation(h_hi[:, u, kd], h_ps[:, kd], ACT.Identity, bias=sh, scale=sc)
                    last_ins.then_inc(s["hi_ready"], 1)

                evacuate_h(0, 0, 0)

                def body(n, u, k, last):
                    if inside(last, 1):
                        evacuate_h(n + 1, 1 - u, (n + 1) // (STEPS // B))
                    act.wait_ge(s["qk_done"], n + 1)
                    act.wait_ge(qk_out[u], 16 * (k + 1))
                    for half in range(2):
                        last_ins = nc.scalar.activation(
                            qk[:, u, 0, 2 * half:2 * half + 2].rearrange("p m t -> p (m t)"),
                            qk_ps[:, u, half], ACT.Copy)
                    last_ins.then_inc(s["qk_hi"], 1)
                    act.wait_ge(s["v_done"], n + 1)
                    act.wait_ge(v_out[u], 16 * (k + 1))
                    nc.scalar.activation(v_rows[:, u, :, :, 0:HD], v_ps[:, u].rearrange("p c (h d) -> p c h d", h=H),
                                         ACT.Copy).then_inc(s["v_0"], 1)

                steps(act, body)

            @block.vector
            def _(dve):
                def take_stats(m, u, k, passed):
                    order = OwnOrder(dve, s["dve_own"], passed)
                    dve.wait_ge(x_in[u], 16 * (k + 1))
                    apart(nc, g)
                    for c in range(SUB):
                        order(nc.vector.bn_stats(stats[:, u, c], g.x[:, ds(m * SUB + c, 1), 0:D].rearrange("p a d -> p (a d)")))
                    order.wait()
                    apart(nc, g)
                    for c in range(SUB):
                        order(nc.vector.bn_aggr(mean_var[:, u, c], stats[:, u, c]))
                    order.wait()
                    order(nc.vector.tensor_scalar(minus_half_var[:, u], mean_var[:, u, :, 1], EPS, -0.5,
                                                  ALU.add, ALU.mult))
                    order.step(nc.vector.tensor_scalar(var[:, u], mean_var[:, u, :, 1], EPS, None, ALU.add))
                    nc.vector.tensor_scalar(guess[:, u], var[:, u].bitcast(I32), 1, -1, ALU.logical_shift_right,
                                            ALU.bitwise_xor).then_inc(s["guess_ready"], 1)
                    return order.n

                def normalise(m, u):
                    dve.wait_ge(s["rstd_ready"], m + 1)
                    for c in range(SUB):
                        last_ins = nc.vector.tensor_scalar(
                            xn[:, u, c], g.x[:, ds(m * SUB + c, 1), 0:D].rearrange("p a d -> p (a d)"),
                            mean_var[:, u, c, 0:1], rstd[:, u, c:c + 1], ALU.subtract, ALU.mult)
                    last_ins.then_inc(s["xn_ready"], 1)

                def rest_of_h(m, u):
                    dve.wait_ge(s["hi_ready"], m + 1)
                    nc.vector.tensor_tensor(h_lo[:, u], h_t[:, u], h_hi[:, u].bitcast(F32),
                                            ALU.subtract).then_inc(s["lo_ready"], 1)

                per = take_stats(0, 0, 0, 0)
                take_stats(1, 1, 0, per)
                normalise(0, 0)
                take_stats(2, 0, 1, 2 * per)
                normalise(1, 1)
                rest_of_h(0, 0)

                def body(n, u, k, last):
                    if inside(last, 1):
                        rest_of_h(n + 1, 1 - u)
                    if inside(last, 2):
                        dve.wait_ge(s["h_transposed"], n + 1)
                        normalise(n + 2, u)
                    if inside(last, 3):
                        take_stats(n + 3, 1 - u, k + 1 + u, (n + 3) * per)
                    dve.wait_ge(s["qk_hi"], n + 1)
                    for half in range(2):
                        last_ins = nc.vector.tensor_tensor(
                            qk[:, u, 1, 2 * half:2 * half + 2].rearrange("p m t -> p (m t)"), qk_ps[:, u, half],
                            qk[:, u, 0, 2 * half:2 * half + 2].rearrange("p m t -> p (m t)").bitcast(F32), ALU.subtract)
                    last_ins.then_inc(s["qk_split"], 1)
                    dve.wait_ge(s["v_0"], n + 1)
                    dve.wait_ge(s["v_split"], n + 1)
                    nc.vector.tensor_tensor(
                        v_rest[:, u].rearrange("p c (h d) -> p c h d", h=H),
                        v_ps[:, u].rearrange("p c (h d) -> p c h d", h=H), v_rows[:, u, :, :, 0:HD],
                        ALU.subtract).then_inc(s["v_rest_ready"], 1)

                steps(dve, body)

            @block.tensor
            def _(pe):
                def transpose_h(m, u):
                    pe.wait_ge(s["xn_ready"], m + 1)
                    for kd in range(KD):
                        for c in range(SUB):
                            last_ins = nc.tensor.transpose(h_ps[:, kd, c * P:(c + 1) * P],
                                                           xn[:, u, c, kd * P:(kd + 1) * P], g.ident[:])
                    last_ins.then_inc(s["h_transposed"], 1)

                transpose_h(0, 0)

                def body(n, u, k, last):
                    pe.wait_ge(s["lo_ready"], n + 1)
                    if inside(last, 1):
                        transpose_h(n + 1, 1 - u)
                    pe.wait_ge(s["qk_split"], n + 1)
                    for m in range(4):
                        products(nc, qk_ps[:, u, m // 2, (m % 2) * TILE:(m % 2 + 1) * TILE],
                                 [(g.wqkv_hi[:, kd, m * P:(m + 1) * P], g.wqkv_lo[:, kd, m * P:(m + 1) * P],
                                   h_hi[:, u, kd], h_lo[:, u, kd]) for kd in range(KD)], s["qk_done"] if m == 3 else None)
                    pe.wait_ge(s["v_rest_ready"], n + 1)
                    for c in range(SUB):
                        cols = slice(c * P, (c + 1) * P)
                        last_ins = products(nc, v_ps[:, u, c],
                                            [(h_hi[:, u, kd, cols], h_lo[:, u, kd, cols],
                                              g.wqkv_hi[:, kd, 2 * D:3 * D], g.wqkv_lo[:, kd, 2 * D:3 * D])
                                             for kd in range(KD)], None)
                    last_ins.then_inc(s["v_done"], 1)

                steps(pe, body)


def products(nc, out, operands, done):
    n = len(operands)
    for i, (l_hi, l_lo, r_hi, r_lo) in enumerate(operands):
        nc.tensor.matmul(out, l_lo, r_hi, start=(i == 0), stop=False)
        nc.tensor.matmul(out, l_hi, r_lo, start=False, stop=False)
        last = nc.tensor.matmul(out, l_hi, r_hi, start=False, stop=(i == n - 1))
    if done is not None:
        last.then_inc(done, 1)
    return last


RING = 3


def attend(nc, g, dram):
    with ExitStack() as stack:
        t = Tensors(nc, stack)
        q_stack = t.sb("q_stack", [4 * HD, RING, H, P], F32R)
        k_stack = t.sb("k_stack", [4 * HD, RING, H, 2 * P], F32R)
        v_win = t.sb("v_win", [P, RING, 2, H * VROW], BF16)
        neg_max = t.sb("neg_max", [P, RING, 2])
        probs = t.sb("probs", [P, 2, 2, 2 * P])
        pt_hi = t.sb("pt_hi", [P, 2, 4, P], F16)
        pt_lo = t.sb("pt_lo", [P, 2, 4, P], F16)
        inverse = t.sb("inverse_sums", [P, 2, PAIRS])
        att_raw = t.sb("att_raw", [P, 2, PAIRS, HD])
        att = t.sb("att", [P, 2, PAIRS, HD])
        att_t = t.sb("att_t", [P, KD, P])
        gated = t.sb("gated", [P, D])
        stats = t.sb("stats2", [P, 6])
        mean_var = t.sb("mean_var2", [P, 2])
        var = t.sb("var2", [P, 1])
        minus_half_var = t.sb("minus_half_var2", [P, 1])
        guess = t.sb("guess2", [P, 1], I32)
        rstd = t.sb("rstd2", [P, 1])
        newt = t.sb("newt2", [P, 1])
        xn = t.sb("xn2", [P, D])
        h_mul = t.sb("h_mul", [P, D])
        h = t.sb("h2", [P, RING, D])
        h_t = t.sb("h2_t", [P, KD, P])
        s_ps = t.ps("s_ps", [P, RING, 512])
        pt_ps = t.ps("pt_ps", [P, 2, 512])
        o_ps = t.ps("o_ps", [P, 2, 512])
        rows_ps = t.ps("rows_ps", [P, 512])
        qkv_in = [t.sem(f"qkv_in{r}") for r in range(RING)]
        h_out = [t.sem(f"h_out{r}") for r in range(RING)]
        names = ("scored", "max_ready", "exp_done", "p_transposed", "hi_done", "lo_done", "pv_done", "o_used",
                 "att_ready", "att_transposed", "att_t_ready", "projected", "gated_ready", "x_ready", "guess_ready",
                 "rstd_ready", "xn_ready", "h_ready", "h_transposed", "h_t_ready", "logits_done",
                 "logits_used", "stats_ready", "dve_own", "pool_own")
        s = {n: t.sem("a_" + n) for n in names}
        LOADS = 9

        def chunks(body, eng):
            for c in range(2):
                body(c, c % RING, c // RING)
            with eng.Fori(0, (CHUNKS - 5) // RING) as k:
                for v in range(RING):
                    body(2 + v + RING * k, (2 + v) % RING, k + (2 + v) // RING)
            for c in range(CHUNKS - 3, CHUNKS + 2):
                body(c, c % RING, c // RING)

        def within(c, back=0, ahead=0):
            return not isinstance(c, int) or back <= c < CHUNKS + back - ahead

        def flat(a):
            return a.rearrange("p a d -> p (a d)")

        with nc.Block() as block:

            @block.sync
            def _(sp):
                def load(c, r):
                    for part in range(4):
                        rows = slice(part * HD, (part + 1) * HD)
                        q = dram["qk"][part // 2, 0:D, ds(c * P + P, P)].rearrange("(h d) t -> d h t", d=HD)
                        k = dram["qk"][part % 2, D:2 * D, ds(c * P, 2 * P)].rearrange("(h d) t -> d h t", d=HD)
                        sp.dma_start(q_stack[rows, r].bitcast(F32), q).then_inc(qkv_in[r], 16)
                        sp.dma_start(k_stack[rows, r].bitcast(F32), k).then_inc(qkv_in[r], 16)
                    sp.dma_start(v_win[:, r], dram["v"][ds(c * P, 2 * P), :].rearrange("(w p) n -> p w n", p=P)
                                 ).then_inc(qkv_in[r], 16)

                for c in range(RING):
                    load(c, c)

                def body(c, r, turn):
                    if within(c, back=2):
                        sp.wait_ge(s["h_ready"], c - 1)
                        sp.dma_start(dram["h_rows"][ds((c - 2) * P, P), :], h[:, (r + 1) % RING, :]
                                     ).then_inc(h_out[(r + 1) % RING], 16)
                    if within(c, ahead=RING):
                        sp.wait_ge(s["pv_done"], PAIRS * (c + 1) + 2)
                        load(c + RING, r)

                chunks(body, sp)
                for r in range(RING):
                    sp.wait_ge(h_out[r], 16 * ((CHUNKS - 1 - r) // RING + 2))

            @block.gpsimd
            def _(pool):
                for name, n in (("p_transposed", 2), ("pv_done", 2), ("o_used", 2), ("att_transposed", 1),
                                ("logits_used", 2)):
                    pool.sem_inc(s[name], n)
                for r in range(RING):
                    pool.sem_inc(h_out[r], 16)
                ROOT = 12
                OWN = ROOT + 1

                def body(c, r, turn):
                    if within(c, back=2):
                        order = OwnOrder(pool, s["pool_own"], OWN * (c - 2) + ROOT)
                        slot, its_turn = (r + 1) % RING, turn - (r < 2)
                        batch = (c - 2) // (CHUNKS // B)
                        pool.wait_ge(s["xn_ready"], c - 1)
                        order.step(nc.gpsimd.tensor_tensor(h_mul[:], xn[:], flat(g.scale_b[:, ds(batch, 1), :]),
                                                           ALU.mult))
                        pool.wait_ge(h_out[slot], 16 * (its_turn + 1))
                        nc.gpsimd.tensor_tensor(h[:, slot], h_mul[:], flat(g.shift_b[:, ds(batch, 1), :]),
                                                ALU.add).then_inc(s["h_ready"], 1)
                    if within(c, back=1):
                        x = flat(g.x[:, ds(c - 1, 1), 0:D])
                        pool.wait_ge(s["gated_ready"], c)
                        nc.gpsimd.tensor_tensor(x, x, gated[:], ALU.add).then_inc(s["x_ready"], 1)
                        order = OwnOrder(pool, s["pool_own"], OWN * (c - 1))
                        pool.wait_ge(s["guess_ready"], c)
                        rsqrt(nc, order, rstd[:], guess[:], minus_half_var[:], newt[:], g).then_inc(s["rstd_ready"], 1)

                chunks(body, pool)

            @block.scalar
            def _(act):
                def exps(n, p, r):
                    act.wait_ge(s["max_ready"], n + 1)
                    act.wait_ge(s["p_transposed"], n + 1)
                    for i in range(2):
                        ins = nc.scalar.activation(probs[:, p % 2, i], s_ps[:, r, i * 2 * P:(i + 1) * 2 * P],
                                                   ACT.Exp, bias=neg_max[:, r, i:i + 1])
                    ins.then_inc(s["exp_done"], 1)

                exps(0, 0, 0)

                def body(c, r, turn):
                    for p in range(PAIRS):
                        n = PAIRS * c + p
                        if within(c, ahead=(p == PAIRS - 1)):
                            exps(n + 1, p + 1, (PAIRS * r + p + 1) % RING)
                        if p == 3 and within(c, back=1):
                            act.wait_ge(s["att_transposed"], c + 1)
                            nc.scalar.activation(att_t[:].rearrange("p k t -> p (k t)"), rows_ps[:, 0:D],
                                                 ACT.Copy).then_inc(s["att_t_ready"], 1)
                        if p == 6 and within(c, back=2):
                            act.wait_ge(s["h_transposed"], c - 1)
                            nc.scalar.activation(h_t[:].rearrange("p k t -> p (k t)"), rows_ps[:, 0:D],
                                                 ACT.Copy).then_inc(s["h_t_ready"], 1)
                        if within(c):
                            act.wait_ge(s["p_transposed"], n + 3)
                            act.wait_ge(s["pv_done"], n + 1)
                            nc.scalar.activation(pt_hi[:, p % 2].rearrange("p a t -> p (a t)"), pt_ps[:, p % 2],
                                                 ACT.Copy).then_inc(s["hi_done"], 1)

                chunks(body, act)

            @block.vector
            def _(dve):
                def row_max(n, r):
                    dve.wait_ge(s["scored"], n + 1)
                    nc.vector.tensor_reduce(neg_max[:, r, :], s_ps[:, r].rearrange("p (i t) -> p i t", i=2),
                                            AX.X, ALU.max, negate=True).then_inc(s["max_ready"], 1)

                def sum_parts(c, half):
                    dve.wait_ge(s["pv_done"], PAIRS * c + 4 * half + 4 + 2)
                    o = o_ps[:, half, 0:PAIRS * VROW].rearrange("p (h c) -> p h c", h=PAIRS)
                    nc.vector.tensor_reduce(
                        att_raw[:, half], o[:, :, 0:3 * HD].rearrange("p h (a d) -> p h d a", a=3), AX.X, ALU.add)
                    nc.vector.reciprocal(inverse[:, half], o[:, :, 3 * HD]).then_inc(s["o_used"], 1)

                def divide(c, half):
                    dve.wait_ge(s["o_used"], 2 * c + half + 1 + 2)
                    if half == 0:
                        dve.wait_ge(s["att_transposed"], c + 1)
                    nc.vector.tensor_tensor(
                        att[:, half], att_raw[:, half], inverse[:, half].unsqueeze(2).broadcast_to([P, PAIRS, HD]),
                        ALU.mult).then_inc(s["att_ready"], 1)

                def gate(c):
                    dve.wait_ge(s["projected"], c)
                    nc.vector.tensor_tensor(gated[:], rows_ps[:, D:2 * D],
                                            flat(g.gate_a[:, ds((c - 1) // (CHUNKS // B), 1), :]),
                                            ALU.mult).then_inc(s["gated_ready"], 1)

                def statistics(c):
                    dve.wait_ge(s["x_ready"], c)
                    apart(nc, g)
                    nc.vector.bn_stats(stats[:], flat(g.x[:, ds(c - 1, 1), 0:D])).then_inc(s["stats_ready"], 1)

                def variance(c):
                    order = OwnOrder(dve, s["dve_own"], 3 * (c - 1))
                    dve.wait_ge(s["stats_ready"], c)
                    apart(nc, g)
                    order.step(nc.vector.bn_aggr(mean_var[:], stats[:]))
                    order(nc.vector.tensor_scalar(minus_half_var[:], mean_var[:, 1:2], EPS, -0.5, ALU.add, ALU.mult))
                    order.step(nc.vector.tensor_scalar(var[:], mean_var[:, 1:2], EPS, None, ALU.add))
                    nc.vector.tensor_scalar(guess[:], var[:].bitcast(I32), 1, -1, ALU.logical_shift_right,
                                            ALU.bitwise_xor).then_inc(s["guess_ready"], 1)

                def normalise(c):
                    dve.wait_ge(s["rstd_ready"], c - 1)
                    nc.vector.tensor_scalar(xn[:], flat(g.x[:, ds(c - 2, 1), 0:D]), mean_var[:, 0:1], rstd[:, 0:1],
                                            ALU.subtract, ALU.mult).then_inc(s["xn_ready"], 1)

                def keep_logits(c):
                    dve.wait_ge(s["logits_done"], c - 1)
                    nc.vector.tensor_copy(flat(g.logits[:, ds(c - 2, 1), :]), rows_ps[:, D:D + E]
                                          ).then_inc(s["logits_used"], 1)

                row_max(0, 0)
                row_max(1, 1)

                def body(c, r, turn):
                    for p in range(PAIRS):
                        n = PAIRS * c + p
                        if within(c, ahead=(p >= PAIRS - 2)):
                            row_max(n + 2, (PAIRS * r + p + 2) % RING)
                        if within(c):
                            dve.wait_ge(s["hi_done"], n + 1)
                            nc.vector.tensor_tensor(pt_lo[:, p % 2].rearrange("p a t -> p (a t)"), pt_ps[:, p % 2],
                                                    pt_hi[:, p % 2].rearrange("p a t -> p (a t)"),
                                                    ALU.subtract).then_inc(s["lo_done"], 1)
                        if p == 0 and within(c, back=1):
                            sum_parts(c - 1, 1)
                        if p == 1 and within(c, back=1):
                            divide(c - 1, 1)
                        if p == 2 and within(c, back=2):
                            normalise(c)
                        if p == 4 and within(c, back=1):
                            gate(c)
                        if p == 5 and within(c):
                            sum_parts(c, 0)
                        if p == 6 and within(c):
                            divide(c, 0)
                        if p == 6 and within(c, back=1):
                            statistics(c)
                        if p == 7 and within(c, back=1):
                            variance(c)
                        if p == 7 and within(c, back=2):
                            keep_logits(c)

                chunks(body, dve)

            @block.tensor
            def _(pe):
                def which_mask(c):
                    per = CHUNKS // B
                    which = (c + per - 1) // per - c // per
                    return which if isinstance(which, int) else pe.snap(pe.to_reg(which), min_val=0, max_val=1)

                def scores(n, p, r, turn, mask, guard=True):
                    bank = (PAIRS * r + p) % RING
                    if p == 0:
                        pe.wait_ge(qkv_in[r], 16 * LOADS * (turn + 1))
                    if guard:
                        pe.wait_ge(s["exp_done"], n - 2)
                    nc.tensor.matmul(s_ps[:, bank], g.identb[:], flat(g.mask[:, ds(mask, 1), :]),
                                     start=True, stop=False)
                    for i in range(2):
                        ins = nc.tensor.matmul(s_ps[:, bank, i * 2 * P:(i + 1) * 2 * P], q_stack[:, r, 2 * p + i],
                                               k_stack[:, r, 2 * p + i], start=False, stop=(i == 1))
                    ins.then_inc(s["scored"], 1)

                def transpose_probs(n, p):
                    pe.wait_ge(s["exp_done"], n + 1)
                    for i in range(2):
                        for w in range(2):
                            ins = nc.tensor.transpose(pt_ps[:, p % 2, (2 * i + w) * P:(2 * i + w + 1) * P],
                                                      probs[:, p % 2, i, w * P:(w + 1) * P], g.ident[:])
                    ins.then_inc(s["p_transposed"], 1)

                def weigh(c, n, p, r):
                    pe.wait_ge(s["lo_done"], n + 1)
                    half = p // 4
                    if p % 4 == 0:
                        pe.wait_ge(s["o_used"], 2 * c + half + 1)
                    for i in range(2):
                        head = 2 * p + i
                        col = (head % PAIRS) * VROW
                        for w in range(2):
                            for part, pt in enumerate((pt_lo, pt_hi)):
                                ins = nc.tensor.matmul(
                                    o_ps[:, half, col:col + VCOLS], pt[:, p % 2, 2 * i + w],
                                    v_win[:, r, w, head * VROW:head * VROW + VCOLS],
                                    start=(w == 0 and part == 0), stop=(w == 1 and part == 1))
                    ins.then_inc(s["pv_done"], 1)

                def transpose_rows(rows, done):
                    for kd in range(KD):
                        ins = nc.tensor.transpose(rows_ps[:, kd * P:(kd + 1) * P], rows[:, kd * P:(kd + 1) * P],
                                                  g.ident[:])
                    ins.then_inc(s[done], 1)

                def multiply_rows(rows_t, w, n, done):
                    for kd in range(KD):
                        ins = nc.tensor.matmul(rows_ps[:, D:D + n], rows_t[:, kd], w[:, kd],
                                               start=(kd == 0), stop=(kd == KD - 1))
                    ins.then_inc(s[done], 1)

                mask = which_mask(0)
                for p in range(RING):
                    scores(p, p, 0, 0, mask, guard=False)
                transpose_probs(0, 0)

                def body(c, r, turn):
                    mask = which_mask(c) if within(c) else None
                    for p in range(PAIRS):
                        n = PAIRS * c + p
                        q = p + RING
                        if p == 4 and within(c, back=1):
                            pe.wait_ge(s["att_t_ready"], c)
                            multiply_rows(att_t, g.wo, D, "projected")
                        if p == 7 and within(c, back=2):
                            pe.wait_ge(s["h_t_ready"], c - 1)
                            multiply_rows(h_t, g.wg, E, "logits_done")
                        if q < PAIRS:
                            if within(c):
                                scores(n + RING, q, r, turn, mask)
                        elif within(c, ahead=1):
                            if q == PAIRS:
                                mask = which_mask(c + 1)
                            scores(n + RING, q - PAIRS, (r + 1) % RING, turn + (r + 1) // RING, mask)
                        if within(c, ahead=(p == PAIRS - 1)):
                            transpose_probs(n + 1, p + 1)
                        if p == 2 and within(c, back=1):
                            pe.wait_ge(s["att_ready"], 2 * c)
                            pe.wait_ge(s["logits_used"], c)
                            transpose_rows(att[:].rearrange("p a h d -> p (a h d)"), "att_transposed")
                        if p == 5 and within(c, back=2):
                            pe.wait_ge(s["h_ready"], c - 1)
                            if within(c, back=1):
                                pe.wait_ge(s["gated_ready"], c)
                            transpose_rows(h[:, (r + 1) % RING], "h_transposed")
                        if within(c):
                            weigh(c, n, p, r)

                chunks(body, pe)


def route(nc, g, dram):
    with ExitStack() as stack:
        t = Tensors(nc, stack)
        less_eight = t.sb("less_eight", [P, E])
        top = t.sb("top", [P, CHUNKS])
        onehot = t.sb("onehot", [P, CHUNKS, E])
        held = t.sb("held", [P, CHUNKS, E])
        counts = t.sb("counts", [P, CHUNKS, E])
        sums = t.sb("count_sums", [P, 2, CHUNKS, E])
        whole = t.sb("whole", [P, E], I32)
        tiles = t.sb("tiles", [P, E])
        tile_sums = t.sb("tile_sums", [P, 2, E])
        bounds = t.sb("bounds_f", [P, E + 1])
        rank_ps = t.ps("rank_ps", [P, 512])
        count_ps = t.ps("count_ps", [P, 512])
        raw_in, hi_done, lo_done, eight_ready, chosen, ranked, own = (
            t.sem("r_" + n) for n in ("raw_in", "hi_done", "lo_done", "eight_ready", "chosen", "ranked", "own"))

        with nc.Block() as block:

            @block.sync
            def _(sp):
                load_weights(sp, g, dram["w1s"], dram["w2s"], dram["w3s"], raw_in)
                sp.wait_ge(raw_in, 48)

            @block.scalar
            def _(act):
                for i in range(3):
                    act.wait_ge(raw_in, 48)
                    cols = slice(i * KD * F, (i + 1) * KD * F)
                    nc.scalar.activation(g.w_hi[:, 0, cols], g.raw[:, cols], ACT.Copy).then_inc(hi_done, 1)

            @block.gpsimd
            def _(pool):
                for e in range(E):
                    last = nc.gpsimd.memset(less_eight[:, e:e + 1], float(e - E))
                last.then_inc(eight_ready, 1)
                for i in range(3):
                    pool.wait_ge(hi_done, i + 1)
                    cols = slice(i * KD * F, (i + 1) * KD * F)
                    nc.gpsimd.tensor_tensor(g.w_lo[:, 0, cols], g.raw[:, cols], g.w_hi[:, 0, cols].bitcast(F32),
                                            ALU.subtract).then_inc(lo_done, 1)
                pool.wait_ge(lo_done, 3)

            @block.vector
            def _(dve):
                order = OwnOrder(dve, own)
                wide = [P, CHUNKS, E]
                order.step(nc.vector.tensor_reduce(top[:], g.logits[:], AX.X, ALU.max))
                order.step(nc.vector.tensor_tensor(onehot[:], g.logits[:], top[:].unsqueeze(2).broadcast_to(wide),
                                                   ALU.is_ge))
                dve.wait_ge(eight_ready, 1)
                experts = less_eight[:].unsqueeze(1).broadcast_to(wide)
                order.step(nc.vector.tensor_tensor(held[:], onehot[:], experts, ALU.mult))
                order.step(nc.vector.tensor_reduce(top[:], held[:], AX.X, ALU.min))
                nc.vector.tensor_tensor(onehot[:], experts, top[:].unsqueeze(2).broadcast_to(wide),
                                        ALU.is_equal).then_inc(chosen, 1)
                dve.wait_ge(ranked, 1)
                flat = lambda a: a.rearrange("p c e -> p (c e)")
                order(nc.vector.tensor_copy(flat(counts[:]), count_ps[:, 0:CHUNKS * E]))
                order.step(nc.vector.tensor_copy(flat(sums[:, 0]), count_ps[:, 0:CHUNKS * E]))
                now, d = 0, 1
                while d < CHUNKS:
                    order(nc.vector.tensor_tensor(sums[:, 1 - now, d:], sums[:, now, d:], sums[:, now, :CHUNKS - d],
                                                  ALU.add))
                    order.step(nc.vector.tensor_copy(sums[:, 1 - now, :d], sums[:, now, :d]))
                    now, d = 1 - now, 2 * d
                order.step(nc.vector.tensor_scalar(tiles[:], sums[:, now, CHUNKS - 1], float(TILE - 1), None, ALU.add))
                order.step(nc.vector.tensor_copy(whole[:], tiles[:]))
                order.step(nc.vector.tensor_scalar(whole[:], whole[:], TILE.bit_length() - 1, None,
                                                   ALU.logical_shift_right))
                order.step(nc.vector.tensor_copy(tiles[:], whole[:]))
                order.step(nc.vector.tensor_scalar(tiles[:], tiles[:], 1.0, None, ALU.max))
                order.step(nc.vector.tensor_copy(tile_sums[:, 0], tiles[:]))
                at, d = 0, 1
                while d < E:
                    order(nc.vector.tensor_tensor(tile_sums[:, 1 - at, d:], tile_sums[:, at, d:],
                                                  tile_sums[:, at, :E - d], ALU.add))
                    order.step(nc.vector.tensor_copy(tile_sums[:, 1 - at, :d], tile_sums[:, at, :d]))
                    at, d = 1 - at, 2 * d
                order(nc.vector.memset(bounds[:, 0:1], float(STEPS)))
                order(nc.vector.tensor_scalar(bounds[:, 1:], tile_sums[:, at], float(STEPS), None, ALU.add))
                order.step(nc.vector.tensor_tensor(tiles[:], tile_sums[:, at], tiles[:], ALU.subtract))
                order(nc.vector.tensor_copy(g.bounds[:], bounds[:]))
                order(nc.vector.tensor_scalar(tiles[:], tiles[:], float(TILE), None, ALU.mult))
                order.step(nc.vector.tensor_tensor(sums[:, now], sums[:, now], counts[:], ALU.subtract))
                order.step(nc.vector.tensor_tensor(sums[:, now], sums[:, now],
                                                   rank_ps[:, 0:CHUNKS * E].rearrange("p (c e) -> p c e", e=E), ALU.add))
                order.step(nc.vector.tensor_tensor(sums[:, now], sums[:, now],
                                                   tiles[:].unsqueeze(1).broadcast_to(wide), ALU.add))
                order.step(nc.vector.tensor_tensor(sums[:, now], sums[:, now], onehot[:], ALU.mult))
                order.step(nc.vector.tensor_reduce(top[:], sums[:, now], AX.X, ALU.add))
                order.step(nc.vector.tensor_copy(g.slots[:], top[:]))

            @block.tensor
            def _(pe):
                pe.wait_ge(chosen, 1)
                flat = onehot[:].rearrange("p c e -> p (c e)")
                nc.tensor.matmul(rank_ps[:, 0:CHUNKS * E], g.before[:], flat, start=True, stop=True)
                nc.tensor.matmul(count_ps[:, 0:CHUNKS * E], g.ones[:], flat, start=True, stop=True).then_inc(ranked, 1)


def load_weights(eng, g, w1, w2, w3, done):
    for i, w in enumerate((w1, w2, w3)):
        n = w.shape[1]
        eng.dma_start(g.raw[:, i * KD * F:(i + 1) * KD * F].rearrange("p (k n) -> p k n", n=n),
                      w.rearrange("(k p) n -> p k n", p=P)).then_inc(done, 16)


PIECES = 8
PIECE = 3 * KD * F // PIECES


def experts(nc, g, dram):
    with ExitStack() as stack:
        t = Tensors(nc, stack)
        rows = t.sb("rows", [P, SUB, D])
        index_h = t.sb("index_h", [P, SUB], U32)
        index_x = t.sb("index_x", [P, SUB], U32)
        h_hi = t.sb("e_h_hi", [P, KD, TILE], F32R)
        h_lo = t.sb("e_h_lo", [P, KD, TILE], F32R)
        gelu = t.sb("gelu", [P, 2, TILE])
        a = t.sb("a", [P, 3, TILE])
        a_hi = t.sb("a_hi", [P, KF, TILE], F32R)
        a_lo = t.sb("a_lo", [P, KF, TILE], F32R)
        gated = t.sb("gated_y", [P, SUB, XROW])
        x_rows = t.sb("x_rows", [P, SUB, XROW])
        gates = t.sb("gates", [P, SUB, D])
        gu_ps = t.ps("gu_ps", [P, 4, 512])
        h_ps = t.ps("e_h_ps", [P, KD, TILE])
        y_ps = t.ps("y_ps", [P, SUB, 512])
        names = ("rows_in", "scattered", "index_h_ready", "index_x_ready", "h_transposed", "h_hi_ready", "h_ready", "gu_done", "gelu_done",
                 "mul_done", "a_hi_done", "a_ready", "y_done", "x_ready", "y_used", "x_rows_out", "x_rows_free", "x_in", "gates_ready", "raw_in",
                 "hi_split", "lo_split", "gated_zero", "all_stored")
        s = {n: t.sem("e_" + n) for n in names}

        def tiles(eng, body, before=None):
            body(0, 0, 0, False, False)
            with eng.Fori(1, STEPS - 1) as i:
                body(i, 0, None, False, False)
            body(STEPS - 1, 0, None, False, True)

            def expert(e, slot, more):
                first = eng.value_load(g.bounds[0:1, ds(e, 1)], min_val=STEPS, max_val=STEPS + TILES_MAX - 1)
                end = eng.value_load(g.bounds[0:1, ds(e + 1, 1)], min_val=STEPS + 1, max_val=STEPS + TILES_MAX)
                if before:
                    before(e)
                body(first, slot, e + 1 if more else None, True, False)
                with eng.If(end > first + 1):
                    with eng.Fori(first + 1, end) as i:
                        body(i, slot, None, True, False)

            with eng.Fori(0, E // 2 - 1) as k:
                for u in range(2):
                    expert(2 * k + u, (u + 1) % 2, True)
            for e in (E - 2, E - 1):
                expert(e, (e + 1) % 2, e < E - 1)

        def load_next_weights(pool, e):
            load_weights(pool, g, *(dram[n][ds(e, 1)].rearrange("a k n -> (a k) n") for n in ("W1", "W2", "W3")),
                         s["raw_in"])

        with nc.Block() as block:

            @block.sync
            def _(sp):
                def load(source, at):
                    sp.dma_start(rows[:], dram[source][ds(at, TILE), :].rearrange("(s p) d -> p s d", p=P)
                                 ).then_inc(s["rows_in"], 16)

                def body(i, slot, nxt, routed, last):
                    snap = (lambda v: v) if isinstance(i, int) else (lambda v: sp.snap(sp.to_reg(v)))
                    scattered = snap(SUB * 16 * (i + 1))
                    at = snap((i + 1 - STEPS if routed or last else i + 1) * TILE)
                    x_at = snap((i - STEPS) * TILE)
                    sp.wait_ge(s["h_transposed"], i + 1)
                    if not routed:
                        sp.wait_ge(s["scattered"], scattered)
                    load("h_sorted" if routed or last else "h_rows", at)
                    if routed:
                        sp.wait_ge(s["x_rows_free"], i)
                        sp.dma_start(x_rows[:], dram["x_sorted"][ds(x_at, TILE), :].rearrange(
                            "(s p) d -> p s d", p=P)).then_inc(s["x_in"], 16)

                load("h_rows", 0)
                tiles(sp, body)
                end = sp.value_load(g.bounds[0:1, E:E + 1], min_val=STEPS + E, max_val=STEPS + TILES_MAX)
                rows_all = sp.snap(sp.to_reg(16 * (end + 1)))
                sp.wait_ge(s["x_rows_free"], end)
                sp.wait_ge(s["rows_in"], rows_all)
                sp.sem_inc(s["all_stored"], 1)

            @block.gpsimd
            def _(pool):
                pool.sem_inc(s["mul_done"], 4)
                pool.sem_inc(s["y_used"], 1)
                pool.sem_inc(s["x_in"], 16 * STEPS)
                pool.sem_inc(s["gates_ready"], STEPS)
                load_next_weights(pool, 0)

                def apart_on_pool(cell):
                    return nc.gpsimd.tensor_tensor(g.scrap[:, cell:cell + 1], g.scrap[:, 1:2], g.scrap[:, 1:2], ALU.add)

                def scatter(name, index, rows, done):
                    for c in range(SUB):
                        nc.gpsimd.indirect_dma_start(
                            out=dram[name][:, :],
                            out_offset=bass.IndirectOffsetOnAxis(ap=index[:, c:c + 1], axis=0),
                            in_=rows[:, c, :], in_offset=None).then_inc(s[done], 16)

                def scatter_h(i):
                    if not (isinstance(i, int) and i == 0):
                        pool.wait_ge(s["scattered"], SUB * 16 * i)
                    pool.wait_ge(s["rows_in"], 16 * (i + 1))
                    apart_on_pool(2)
                    nc.gpsimd.tensor_copy(index_h[:], g.slots[:, ds(i * SUB, SUB)]).then_inc(s["index_h_ready"], 1)
                    pool.wait_ge(s["index_h_ready"], i + 1)
                    apart_on_pool(3)
                    scatter("h_sorted", index_h, rows, "scattered")

                def body(i, slot, nxt, routed, last):
                    if not routed and not last:
                        scatter_h(i + 1)
                    if nxt is not None:
                        for p in range(PIECES):
                            pool.wait_ge(s["hi_split"], PIECES * nxt + p + 1)
                            cols = slice(p * PIECE, (p + 1) * PIECE)
                            ins = nc.gpsimd.tensor_tensor(g.w_lo[:, 1 - slot, cols], g.raw[:, cols],
                                                          g.w_hi[:, 1 - slot, cols].bitcast(F32), ALU.subtract)
                        ins.then_inc(s["lo_split"], 1)
                    if not (isinstance(i, int) and i == 0):
                        pool.wait_ge(s["x_rows_free"], i)
                    pool.wait_ge(s["x_ready"], i + 1)
                    apart_on_pool(5)
                    where = x_rows[:, :, D] if routed else g.slots[:, ds(i * SUB, SUB)]
                    nc.gpsimd.tensor_copy(index_x[:], where).then_inc(s["index_x_ready"], 1)
                    pool.wait_ge(s["index_x_ready"], i + 1)
                    apart_on_pool(6)
                    if routed:
                        scatter("out", index_x, x_rows[:, :, 0:D], "x_rows_out")
                    else:
                        scatter("x_sorted", index_x, x_rows, "x_rows_out")
                    pool.wait_ge(s["x_rows_out"], SUB * 16 * (i + 1))
                    apart_on_pool(7).then_inc(s["x_rows_free"], 1)
                    if nxt is not None and (not isinstance(nxt, int) or nxt + 1 < E):
                        pool.wait_ge(s["lo_split"], nxt + 1)
                        apart_on_pool(4)
                        load_next_weights(pool, nxt + 1)

                scatter_h(0)
                tiles(pool, body)

            @block.scalar
            def _(act):
                def evacuate_h(i):
                    act.wait_ge(s["h_transposed"], i + 1)
                    nc.scalar.activation(h_hi[:], h_ps[:], ACT.Copy).then_inc(s["h_hi_ready"], 1)

                def body(i, slot, nxt, routed, last):
                    for j in range(KF):
                        act.wait_ge(s["gu_done"], KF * i + j + 1)
                        act.wait_ge(s["mul_done"], KF * i + j - 1 + 4)
                        nc.scalar.activation(gelu[:, j % 2], gu_ps[:, j % 4, 0:TILE], ACT.Gelu).then_inc(s["gelu_done"], 1)
                        if nxt is not None:
                            if j == 0:
                                act.wait_ge(s["raw_in"], 48 * (nxt + 1))
                            cols = slice(j * PIECE, (j + 1) * PIECE)
                            nc.scalar.activation(g.w_hi[:, 1 - slot, cols], g.raw[:, cols],
                                                 ACT.Copy).then_inc(s["hi_split"], 1)
                    evacuate_h(i + 1)
                evacuate_h(0)
                tiles(act, body)

            @block.vector
            def _(dve):
                def rest_of_h(i):
                    dve.wait_ge(s["h_hi_ready"], i + 1)
                    nc.vector.tensor_tensor(h_lo[:], h_ps[:], h_hi[:].bitcast(F32), ALU.subtract).then_inc(s["h_ready"], 1)

                def body(i, slot, nxt, routed, last):
                    def low(j):
                        dve.wait_ge(s["a_hi_done"], KF * i + j + 1)
                        nc.vector.tensor_tensor(a_lo[:, j], a[:, j % 3], a_hi[:, j].bitcast(F32),
                                                ALU.subtract).then_inc(s["a_ready"], 1)

                    for j in range(KF):
                        dve.wait_ge(s["gelu_done"], KF * i + j + 1)
                        nc.vector.tensor_tensor(a[:, j % 3], gelu[:, j % 2], gu_ps[:, j % 4, TILE:2 * TILE],
                                                ALU.mult).then_inc(s["mul_done"], 1)
                        if j:
                            low(j - 1)
                        dve.wait_ge(s["mul_done"], KF * i + j + 1 + 4)
                        nc.vector.tensor_copy(a_hi[:, j], a[:, j % 3]).then_inc(s["a_hi_done"], 1)
                    low(KF - 1)
                    rest_of_h(i + 1)
                    if routed:
                        dve.wait_ge(s["x_in"], 16 * (i + 1))
                        for c in range(SUB):
                            ins = nc.vector.scalar_tensor_tensor(
                                gates[:, c], g.gate_step[:], x_rows[:, c, D + 1:XROW], g.gate_b[:, 0, :],
                                ALU.mult, ALU.add)
                        ins.then_inc(s["gates_ready"], 1)
                        dve.wait_ge(s["gates_ready"], i + 1)
                        gate = lambda c: gates[:, c]
                    else:
                        shared_gate = g.gate_b[:, ds(i // (STEPS // B), 1), :].rearrange("p a d -> p (a d)")
                        gate = lambda c: shared_gate
                    dve.wait_ge(s["y_done"], i + 1)
                    for c in range(SUB):
                        ins = nc.vector.tensor_tensor(gated[:, c, 0:D], y_ps[:, c, 0:D], gate(c), ALU.mult)
                    ins.then_inc(s["y_used"], 1)
                    dve.wait_ge(s["y_used"], i + 2)
                    if not routed and not (isinstance(i, int) and i == 0):
                        dve.wait_ge(s["x_rows_free"], i)
                    x, n = (x_rows[:], D) if routed else (g.x[:, ds(i * SUB, SUB), :], XROW)
                    nc.vector.tensor_tensor(x_rows[:, :, 0:n], x[:, :, 0:n], gated[:, :, 0:n],
                                            ALU.add).then_inc(s["x_ready"], 1)

                nc.vector.memset(gated[:], 0.0).then_inc(s["gated_zero"], 1)
                dve.wait_ge(s["gated_zero"], 1)
                rest_of_h(0)
                tiles(dve, body)

            @block.tensor
            def _(pe):
                def transpose_h(i):
                    pe.wait_ge(s["rows_in"], 16 * (i + 1))
                    for kd in range(KD):
                        for c in range(SUB):
                            ins = nc.tensor.transpose(h_ps[:, kd, c * P:(c + 1) * P], rows[:, c, kd * P:(kd + 1) * P],
                                                      g.ident[:])
                    ins.then_inc(s["h_transposed"], 1)

                def weights(slot, which, k, cols, n):
                    at = which * KD * F + k * n
                    cols = slice(at + cols.start, at + cols.stop)
                    return g.w_hi[:, slot, cols], g.w_lo[:, slot, cols]

                def body(i, slot, nxt, routed, last):
                    for j in range(KF):
                        if j == 0:
                            pe.wait_ge(s["h_ready"], i + 1)
                        pe.wait_ge(s["mul_done"], KF * i + j + 1)
                        cols = slice(j * P, (j + 1) * P)
                        for which in range(2):
                            products(nc, gu_ps[:, j % 4, which * TILE:(which + 1) * TILE],
                                     [(*weights(slot, which, kd, cols, F), h_hi[:, kd], h_lo[:, kd])
                                      for kd in range(KD)], s["gu_done"] if which else None)
                    transpose_h(i + 1)
                    pe.wait_ge(s["y_used"], i + 1)
                    for k in range(KF):
                        pe.wait_ge(s["a_ready"], KF * i + k + 1)
                        w_hi, w_lo = weights(slot, 2, k, slice(0, D), D)
                        for c in range(SUB):
                            cols = slice(c * P, (c + 1) * P)
                            out = y_ps[:, c, 0:D]
                            nc.tensor.matmul(out, a_lo[:, k, cols], w_hi, start=(k == 0), stop=False)
                            nc.tensor.matmul(out, a_hi[:, k, cols], w_lo, start=False, stop=False)
                            ins = nc.tensor.matmul(out, a_hi[:, k, cols], w_hi, start=False, stop=(k == KF - 1))
                    ins.then_inc(s["y_done"], 1)

                transpose_h(0)
                tiles(pe, body, lambda e: pe.wait_ge(s["lo_split"], e + 1))


class Globals:

    def __init__(self, t):
        self.x = t.sb("x_res", [P, CHUNKS, XROW])
        self.ident = t.sb("ident", [P, P])
        self.before = t.sb("before", [P, P])
        self.ones = t.sb("ones", [P, P])
        self.magic = t.sb("magic", [P, SUB], I32)
        self.three_halves = t.sb("three_halves", [P, SUB])
        self.logits = t.sb("logits", [P, CHUNKS, E])
        self.scrap = t.sb("scrap", [P, 8])
        self.gate_b = t.sb("gate_b", [P, B, D])
        self.gate_step = t.sb("gate_step", [P, D])

    def for_attention(self, t):
        self.identb = t.sb("identb", [P, P], BF16)
        self.mask = t.sb("mask", [P, 2, 512], BF16)
        self.zeros = t.sb("zeros", [P, 10, XROW])
        self.pad_out, self.zero_out = t.sem("pad_out"), t.sem("zero_out")
        self.wqkv_hi = t.sb("wqkv_hi", [P, KD, 3 * D], F32R)
        self.wqkv_lo = t.sb("wqkv_lo", [P, KD, 3 * D], F32R)
        self.wo = t.sb("wo_sb", [P, KD, D])
        self.wg = t.sb("wg_sb", [P, KD, E])
        self.shift_a = t.sb("shift_a", [P, B, KD])
        self.scale_a = t.sb("scale_a", [P, B, KD])
        self.gate_a = t.sb("gate_a", [P, B, D])
        self.shift_b = t.sb("shift_b", [P, B, D])
        self.scale_b = t.sb("scale_b", [P, B, D])

    def for_experts(self, t):
        self.slots = t.sb("slots", [P, CHUNKS], U32)
        self.bounds = t.sb("bounds", [P, E + 1], I32)
        self.w_hi = t.sb("w_hi", [P, 2, 3 * KD * F], F32R)
        self.w_lo = t.sb("w_lo", [P, 2, 3 * KD * F], F32R)
        self.raw = t.sb("w_raw", [P, 3 * KD * F])


def adaln_block(nc, dram, stages=9):
    for name, shape, dtype in (("qk", [2, 2 * D, T + P], F32), ("v", [T + P, H * VROW], BF16),
                               ("h_rows", [T, D], F32), ("h_sorted", [SORTED, D], F32),
                               ("x_sorted", [SORTED, XROW], F32)):
        dram[name] = nc.dram_tensor(name + "_scratch", shape, dtype, kind="Internal").ap()
    with ExitStack() as stack:
        g = Globals(Tensors(nc, stack))
        with ExitStack() as inner:
            g.for_attention(Tensors(nc, inner))
            setup(nc, g, dram)
            project(nc, g, dram)
            if stages >= 2:
                attend(nc, g, dram)
        if stages >= 3:
            g.for_experts(Tensors(nc, stack))
            route(nc, g, dram)
            experts(nc, g, dram)


_INPUTS = {"x": "L0_attn_x", "wq": "L0_attn_Wq", "wk": "L0_attn_Wk", "wv": "L0_attn_Wv", "wo": "L0_attn_Wo",
           "w1s": "L0_ffn_w1s", "w2s": "L0_ffn_w2s", "w3s": "L0_ffn_w3s", "W1": "L0_ffn_W1", "W2": "L0_ffn_W2",
           "W3": "L0_ffn_W3", "wg": "L0_ffn_Wg", "c": "L0_c", "wmod": "L0_wmod"}


def kernel(**inputs):
    import numpy as np
    import concourse.bacc as bacc
    from concourse import mybir
    from concourse.bass_utils import run_bass_kernel_spmd

    nc = bacc.Bacc("TRN2", target_bir_lowering=False, num_devices=1)
    arrays, dram = {}, {}
    for short, name in _INPUTS.items():
        a = np.asarray(inputs[name])
        if short == "x":
            a = a.reshape(T, D)
        if short in ("wq", "wk", "wv", "wo", "c"):
            a = a.T
        arrays["in_" + short] = np.ascontiguousarray(a)
        dram[short] = nc.dram_tensor("in_" + short, a.shape, mybir.dt.from_np(a.dtype), kind="ExternalInput").ap()
    dram["out"] = nc.dram_tensor("out_0_dram", (T + TILE, D), mybir.dt.float32, kind="ExternalOutput").ap()
    adaln_block(nc, dram)
    r = run_bass_kernel_spmd(nc, [arrays], core_ids=[0])
    return r.results[0]["out_0_dram"][0:T].reshape(B, S, D)
```

```python
import concourse.bass as bass
from concourse import mybir
from contextlib import ExitStack

F32 = mybir.dt.float32
F32R = mybir.dt.float32r
BF16 = mybir.dt.bfloat16
F16 = mybir.dt.float16
I32 = mybir.dt.int32
U32 = mybir.dt.uint32
ALU = mybir.AluOpType
ACT = mybir.ActivationFunctionType
AX = mybir.AxisListType
ds = bass.ds

P = 128
B, S, D = 2, 2048, 256
T = B * S
KD = D // P
H, HD = 16, 16
F = 1024
KF = F // P
E = 8
CHUNKS = T // P
TILE = 256
SUB = TILE // P
STEPS = T // TILE
TILES_MAX = T // TILE + E
SORTED = (TILES_MAX + 1) * TILE
XROW = D + 2
EPS = 1e-5
MASKED = -1e30
RING = 3
LOADS = 9
VROW = 50
VCOLS = 3 * HD + 1
PAIRS = H // 2


class OwnOrder:

    def __init__(self, eng, sem, passed=0):
        self.eng, self.sem, self.passed, self.n = eng, sem, passed, 0

    def __call__(self, ins):
        ins.then_inc(self.sem, 1)
        self.n += 1

    def wait(self):
        self.eng.wait_ge(self.sem, self.passed + self.n)

    def step(self, ins):
        self(ins)
        self.wait()


class Tensors:

    def __init__(self, nc, stack):
        self.nc, self.stack = nc, stack

    def sb(self, name, shape, dtype=F32):
        return self.stack.enter_context(self.nc.sbuf_tensor(name, shape, dtype))

    def ps(self, name, shape):
        return self.stack.enter_context(self.nc.psum_tensor(name, shape, F32))

    def sem(self, name):
        return self.stack.enter_context(self.nc.semaphore(name))


def rsqrt(nc, order, y, variance, v, t, g):
    n = y.shape[-1]
    order.step(nc.gpsimd.tensor_tensor(v, variance, g.eps[:, 0:n], ALU.add))
    order(nc.gpsimd.tensor_tensor(y, v, g.minus_half[:, 0:n], ALU.pow))
    order.step(nc.gpsimd.tensor_tensor(v, v, g.minus_half[:, 0:n], ALU.mult))
    order.step(nc.gpsimd.tensor_tensor(t, y, y, ALU.mult))
    order.step(nc.gpsimd.tensor_tensor(t, t, v, ALU.mult))
    order.step(nc.gpsimd.tensor_tensor(t, t, g.three_halves[:, 0:n], ALU.add))
    return nc.gpsimd.tensor_tensor(y, y, t, ALU.mult)


def apart(nc, g, cell=0):
    nc.vector.tensor_copy(g.scrap[:, cell:cell + 1], g.scrap[:, 1:2])


def apart_on_pool(nc, g, cell):
    return nc.gpsimd.tensor_tensor(g.scrap[:, cell:cell + 1], g.scrap[:, 1:2], g.scrap[:, 1:2], ALU.add)


def setup(nc, g, dram):
    with ExitStack() as stack:
        t = Tensors(nc, stack)
        cond = t.sb("cond", [P, KD, B])
        cond_e = t.sb("cond_e", [P, KD, B])
        cond_silu = t.sb("cond_silu", [P, KD, B])
        cond_wide, wmod = g.cond_wide, g.wmod
        wqkv = t.sb("wqkv", [P, KD, 3 * D])
        zeros = g.zeros
        number = t.sb("number", [P, CHUNKS], I32)
        col_ps = t.ps("col_ps", [P, 512])
        cond_in, wmod_in, wq_in = (t.sem(n) for n in ("cond_in", "wmod_in", "wq_in"))
        act_done, col_done = (t.sem(n) for n in ("s_act_done", "s_col_done"))
        silu_done, dve_own, pool_own, zeroed = (
            t.sem(n) for n in ("silu_done", "s_dve_own", "s_pool_own", "zeroed"))
        pad_out = g.pad_out

        with nc.Block() as block:

            @block.sync
            def _(sp):
                sp.dma_start(cond[:], dram["c"].rearrange("(k p) b -> p k b", p=P)).then_inc(cond_in, 16)
                wmod_rows = dram["wmod"].rearrange("(k p) n -> p k n", p=P)
                sp.dma_start(wmod[:, :, 0:2 * D], wmod_rows[:, :, 0:2 * D]).then_inc(wmod_in, 16)
                for i, w in enumerate(("wq", "wk", "wv")):
                    sp.dma_start(wqkv[:, :, i * D:(i + 1) * D],
                                 dram[w].rearrange("(k p) n -> p k n", p=P)).then_inc(wq_in, 16)
                for m in range(2):
                    load_tokens(sp, g, dram, m, m)
                sp.dma_start(wmod[:, :, 2 * D:6 * D], wmod_rows[:, :, 2 * D:6 * D]).then_inc(g.wmod_rest_in, 16)
                sp.dma_start(g.wo[:], dram["wo"].rearrange("(k p) n -> p k n", p=P)).then_inc(g.wo_in, 16)
                sp.dma_start(g.wg[:], dram["wg"].rearrange("(k p) n -> p k n", p=P)).then_inc(g.wo_in, 16)
                sp.wait_ge(zeroed, 1)
                sp.dma_start(dram["qk"].rearrange("a f t -> (a f) t")[:, 0:P].rearrange("(m p) t -> p m t", p=P),
                             zeros[:, 0:1, 0:P].broadcast_to([P, 8, P])).then_inc(pad_out, 16)
                sp.dma_start(dram["v"][0:P, :].rearrange("p (a b) -> p a b", a=2),
                             zeros[:, 0:2, 0:H * VROW // 4].rearrange("p a b -> p a b").bitcast(BF16)
                             ).then_inc(pad_out, 16)
                sp.wait_ge(cond_in, 16)

            @block.gpsimd
            def _(pool):
                order = OwnOrder(pool, pool_own)
                order.step(nc.gpsimd.memset(zeros[:], 0.0))
                order.step(nc.gpsimd.iota(number[:, 0:SUB], pattern=[[P, SUB]], base=T, channel_multiplier=1))
                order.step(nc.gpsimd.tensor_copy(zeros[:, :, D], number[:, 0:SUB]))
                pool.sem_inc(zeroed, 1)
                order.step(nc.gpsimd.iota(number[:], pattern=[[P, CHUNKS]], base=0, channel_multiplier=1))
                order(nc.gpsimd.tensor_copy(g.x[:, :, D], number[:]))
                for b in range(B):
                    order(nc.gpsimd.memset(g.x[:, b * CHUNKS // B:(b + 1) * CHUNKS // B, D + 1:XROW], float(b)))
                order(nc.gpsimd.memset(g.ident[:], 0.0))
                order(nc.gpsimd.memset(g.mask[:], 0.0))
                order(nc.gpsimd.memset(g.scrap[:], 0.0))
                order(nc.gpsimd.memset(g.eps[:], EPS))
                order(nc.gpsimd.memset(g.minus_half[:], -0.5))
                order.step(nc.gpsimd.memset(g.three_halves[:], 1.5))
                order.step(nc.gpsimd.affine_select(
                    out=g.ident[:], in_=g.ident[:], compare_op=ALU.not_equal, fill=1.0, base=0,
                    pattern=[[-1, P]], channel_multiplier=1))
                order(nc.gpsimd.tensor_copy(g.identb[:], g.ident[:]))
                for m in range(2):
                    for head in range(2):
                        prev = g.mask[:, m, head * 256:head * 256 + P]
                        own = g.mask[:, m, head * 256 + P:head * 256 + 2 * P]
                        if m == 0:
                            order(nc.gpsimd.memset(prev, MASKED))
                        else:
                            order(nc.gpsimd.affine_select(
                                out=prev, in_=prev, compare_op=ALU.is_gt, fill=MASKED, base=0,
                                pattern=[[1, P]], channel_multiplier=-1))
                        order(nc.gpsimd.affine_select(
                            out=own, in_=own, compare_op=ALU.is_ge, fill=MASKED, base=0,
                            pattern=[[-1, P]], channel_multiplier=1))
                order.wait()

            @block.scalar
            def _(act):
                act.wait_ge(cond_in, 16)
                nc.scalar.activation(cond_e[:], cond[:], ACT.Exp, scale=-1.0).then_inc(act_done, 1)
                act.wait_ge(wq_in, 48)
                nc.scalar.activation(g.wqkv_hi[:, :, 0:D], wqkv[:, :, 0:D], ACT.Copy,
                                     scale=HD ** -0.5).then_inc(act_done, 1)
                nc.scalar.activation(g.wqkv_hi[:, :, D:3 * D], wqkv[:, :, D:3 * D], ACT.Copy).then_inc(act_done, 1)

            @block.vector
            def _(dve):
                order = OwnOrder(dve, dve_own)
                dve.wait_ge(act_done, 1)
                order.step(nc.vector.tensor_scalar(cond_e[:], cond_e[:], 1.0, None, ALU.add))
                order.step(nc.vector.reciprocal(cond_e[:], cond_e[:]))
                order.step(nc.vector.tensor_tensor(cond_silu[:], cond[:], cond_e[:], ALU.mult))
                nc.vector.tensor_copy(
                    cond_wide[:], cond_silu[:].unsqueeze(3).broadcast_to([P, KD, B, P])).then_inc(silu_done, 1)
                dve.wait_ge(col_done, 1)
                cols = col_ps[:, 0:2 * KD * B].rearrange("p (s m b) -> p s m b", s=2, m=KD)
                order(nc.vector.tensor_copy(g.shift_a[:], cols[:, 0].rearrange("p m b -> p b m")))
                order(nc.vector.tensor_scalar(g.scale_a[:], cols[:, 1].rearrange("p m b -> p b m"),
                                              1.0, None, ALU.add))
                dve.wait_ge(act_done, 3)
                order(nc.vector.scalar_tensor_tensor(
                    g.wqkv_lo[:, :, 0:D], wqkv[:, :, 0:D], HD ** -0.5, g.wqkv_hi[:, :, 0:D].bitcast(F32),
                    ALU.mult, ALU.subtract))
                order(nc.vector.tensor_tensor(g.wqkv_lo[:, :, D:3 * D], wqkv[:, :, D:3 * D],
                                              g.wqkv_hi[:, :, D:3 * D].bitcast(F32), ALU.subtract))
                order.wait()

            @block.tensor
            def _(pe):
                pe.wait_ge(silu_done, 1)
                pe.wait_ge(wmod_in, 16)
                for n in range(2 * KD):
                    for k in range(KD):
                        last = nc.tensor.matmul(col_ps[:, n * B:(n + 1) * B], wmod[:, k, n * P:(n + 1) * P],
                                                cond_silu[:, k, :], start=(k == 0), stop=(k == KD - 1))
                last.then_inc(col_done, 1)


def load_tokens(sp, g, dram, m, u):
    sp.dma_start(g.x[:, ds(m * SUB, SUB), 0:D],
                 dram["x"][ds(m * TILE, TILE), :].rearrange("(s p) d -> p s d", p=P)).then_inc(g.x_in[u], 16)


def project(nc, g, dram):
    with ExitStack() as stack:
        t = Tensors(nc, stack)
        xn = t.sb("xn", [P, 2, SUB, D])
        h_t = t.sb("h_t", [P, 2, KD, TILE])
        h_hi = t.sb("h_hi", [P, 2, KD, TILE], F32R)
        h_lo = t.sb("h_lo", [P, 2, KD, TILE], F32R)
        qk, v_rows, qk_out, v_out = g.qk, g.v_rows, g.qk_out, g.v_out
        v_rest = t.sb("v_rest", [P, SUB, D])
        stats = t.sb("stats", [P, 2, SUB, 6])
        mean_var = t.sb("mean_var", [P, 2, SUB, 2])
        newv = t.sb("newv", [P, 2, SUB])
        rstd = t.sb("rstd", [P, 2, SUB])
        newt = t.sb("newt", [P, 2, SUB])
        h_ps = t.ps("h_ps", [P, KD, TILE])
        qk_ps = t.ps("qk_ps", [P, 2, 2, 512])
        v_ps = t.ps("v_ps", [P, 2, SUB, D])
        x_in = g.x_in
        names = ("var_ready", "rstd_ready", "xn_ready", "h_transposed", "hi_ready", "lo_ready",
                 "qk_done", "v_done", "qk_hi", "qk_split", "v_0", "v_1", "v_rest_ready", "v_split", "rows_done", "rows_used", "dve_own",
                 "pool_own")
        s = {n: t.sem("p_" + n) for n in names}

        def steps(eng, body):
            with eng.Fori(0, STEPS // 2 - 2) as k:
                for u in range(2):
                    body(2 * k + u, u, k, None)
            for k in range(STEPS // 2 - 2, STEPS // 2):
                for u in range(2):
                    body(2 * k + u, u, k, 2 * k + u)

        def inside(n, ahead):
            return n is None or n + ahead < STEPS

        with nc.Block() as block:

            @block.sync
            def _(sp):
                for m in range(2, 4):
                    sp.wait_ge(x_in[m % 2], 16)
                    load_tokens(sp, g, dram, m, m % 2)

                def body(n, u, k, last):
                    if inside(last, 4):
                        sp.wait_ge(x_in[u], 16 * (k + 2))
                        load_tokens(sp, g, dram, n + 4, u)
                    sp.wait_ge(s["qk_split"], n + 3)
                    sp.dma_start(dram["qk"].rearrange("a (m p) t -> p (a m) t", p=P)[:, :, ds(n * TILE + P, TILE)],
                                 qk[:, u].rearrange("p a m t -> p (a m) t").bitcast(F32)).then_inc(qk_out[u], 16)
                    sp.wait_ge(s["v_split"], n + 3)
                    sp.dma_start(dram["v"][ds(n * TILE + P, TILE), :].rearrange("(s p) c -> p s c", p=P),
                                 v_rows[:, u].rearrange("p s h c -> p s (h c)")).then_inc(v_out[u], 16)
                    if last == STEPS - 3:
                        sp.wait_ge(g.pad_out, 32)
                        sp.wait_ge(qk_out[0], 16 * 2)
                        sp.wait_ge(v_out[0], 16 * 2)
                        load_chunk(sp, g, dram, 0, 0)

                steps(sp, body)
                sp.wait_ge(g.wo_in, 32)

            @block.gpsimd
            def _(pool):
                pool.sem_inc(s["qk_split"], 2)
                pool.sem_inc(s["v_rest_ready"], 2)
                pool.sem_inc(s["v_split"], 2)
                for u in range(2):
                    pool.sem_inc(qk_out[u], 16)
                    pool.sem_inc(v_out[u], 16)
                for u in range(2):
                    nc.gpsimd.memset(v_rows[:, u, :, :, 3 * HD:VROW], 1.0)

                def find_rstd(m, u, passed):
                    order = OwnOrder(pool, s["pool_own"], passed)
                    pool.wait_ge(s["var_ready"], m + 1)
                    rsqrt(nc, order, rstd[:, u], mean_var[:, u, :, 1], newv[:, u], newt[:, u],
                          g).then_inc(s["rstd_ready"], 1)
                    return order.n

                per = 0
                for m in range(3):
                    per = find_rstd(m, m % 2, m * per)

                def body(n, u, k, last):
                    if inside(last, 3):
                        find_rstd(n + 3, 1 - u, (n + 3) * per)
                    pool.wait_ge(s["v_1"], n + 1)
                    for c in range(SUB):
                        last_ins = nc.gpsimd.tensor_tensor(
                            v_rows[:, u, c, :, 2 * HD:3 * HD], v_rest[:, c].rearrange("p (h d) -> p h d", h=H),
                            v_rows[:, u, c, :, HD:2 * HD], ALU.subtract)
                    last_ins.then_inc(s["v_split"], 1)

                steps(pool, body)

            @block.scalar
            def _(act):
                def evacuate_h(m, u, batch):
                    act.wait_ge(s["h_transposed"], m + 1)
                    for kd in range(KD):
                        sc = g.scale_a[:].rearrange("p b m -> p (b m)")[:, ds(batch * KD + kd, 1)]
                        sh = g.shift_a[:].rearrange("p b m -> p (b m)")[:, ds(batch * KD + kd, 1)]
                        nc.scalar.activation(h_t[:, u, kd], h_ps[:, kd], ACT.Identity, bias=sh, scale=sc)
                        last_ins = nc.scalar.activation(h_hi[:, u, kd], h_ps[:, kd], ACT.Identity, bias=sh, scale=sc)
                    last_ins.then_inc(s["hi_ready"], 1)

                for b in range(B):
                    act.wait_ge(s["rows_done"], b + 1)
                    nc.scalar.activation(g.gate_a[:, b, :], qk_ps[:, b, 0, 0:D], ACT.Copy)
                    nc.scalar.activation(g.shift_b[:, b, :], qk_ps[:, b, 0, D:2 * D], ACT.Copy)
                    nc.scalar.activation(g.scale_b[:, b, :], qk_ps[:, b, 1, 0:D], ACT.Copy, bias=1.0)
                    nc.scalar.activation(g.gate_b[:, b, :], qk_ps[:, b, 1, D:2 * D], ACT.Copy
                                         ).then_inc(s["rows_used"], 1)
                evacuate_h(0, 0, 0)

                def body(n, u, k, last):
                    if inside(last, 1):
                        evacuate_h(n + 1, 1 - u, (n + 1) // (STEPS // B))
                    act.wait_ge(s["qk_done"], n + 1)
                    act.wait_ge(qk_out[u], 16 * (k + 1))
                    for half in range(2):
                        last_ins = nc.scalar.activation(
                            qk[:, u, 0, 2 * half:2 * half + 2].rearrange("p m t -> p (m t)"),
                            qk_ps[:, u, half], ACT.Copy)
                    last_ins.then_inc(s["qk_hi"], 1)
                    act.wait_ge(s["v_done"], n + 1)
                    act.wait_ge(v_out[u], 16 * (k + 1))
                    nc.scalar.activation(v_rows[:, u, :, :, 0:HD], v_ps[:, u].rearrange("p c (h d) -> p c h d", h=H),
                                         ACT.Copy).then_inc(s["v_0"], 1)

                steps(act, body)

            @block.vector
            def _(dve):
                def take_stats(m, u, k, passed):
                    order = OwnOrder(dve, s["dve_own"], passed)
                    dve.wait_ge(x_in[u], 16 * (k + 1))
                    apart(nc, g)
                    for c in range(SUB):
                        order(nc.vector.bn_stats(stats[:, u, c], g.x[:, ds(m * SUB + c, 1), 0:D].rearrange("p a d -> p (a d)")))
                    order.wait()
                    apart(nc, g, cell=2)
                    for c in range(SUB):
                        last_ins = nc.vector.bn_aggr(mean_var[:, u, c], stats[:, u, c])
                    last_ins.then_inc(s["var_ready"], 1)
                    return order.n

                def normalise(m, u):
                    dve.wait_ge(s["rstd_ready"], m + 1)
                    for c in range(SUB):
                        last_ins = nc.vector.tensor_scalar(
                            xn[:, u, c], g.x[:, ds(m * SUB + c, 1), 0:D].rearrange("p a d -> p (a d)"),
                            mean_var[:, u, c, 0:1], rstd[:, u, c:c + 1], ALU.subtract, ALU.mult)
                    last_ins.then_inc(s["xn_ready"], 1)

                def rest_of_h(m, u):
                    dve.wait_ge(s["hi_ready"], m + 1)
                    nc.vector.tensor_tensor(h_lo[:, u], h_t[:, u], h_hi[:, u].bitcast(F32),
                                            ALU.subtract).then_inc(s["lo_ready"], 1)

                per = take_stats(0, 0, 0, 0)
                take_stats(1, 1, 0, per)
                normalise(0, 0)
                take_stats(2, 0, 1, 2 * per)
                normalise(1, 1)
                rest_of_h(0, 0)

                def body(n, u, k, last):
                    if inside(last, 1):
                        rest_of_h(n + 1, 1 - u)
                    if inside(last, 2):
                        dve.wait_ge(s["h_transposed"], n + 1)
                        normalise(n + 2, u)
                    if inside(last, 3):
                        take_stats(n + 3, 1 - u, k + 1 + u, (n + 3) * per)
                    dve.wait_ge(s["qk_hi"], n + 1)
                    for half in range(2):
                        last_ins = nc.vector.tensor_tensor(
                            qk[:, u, 1, 2 * half:2 * half + 2].rearrange("p m t -> p (m t)"), qk_ps[:, u, half],
                            qk[:, u, 0, 2 * half:2 * half + 2].rearrange("p m t -> p (m t)").bitcast(F32), ALU.subtract)
                    last_ins.then_inc(s["qk_split"], 1)
                    dve.wait_ge(s["v_0"], n + 1)
                    dve.wait_ge(s["v_split"], n + 2)
                    nc.vector.tensor_tensor(
                        v_rest[:].rearrange("p c (h d) -> p c h d", h=H),
                        v_ps[:, u].rearrange("p c (h d) -> p c h d", h=H), v_rows[:, u, :, :, 0:HD],
                        ALU.subtract).then_inc(s["v_rest_ready"], 1)
                    dve.wait_ge(s["v_rest_ready"], n + 3)
                    nc.vector.tensor_copy(v_rows[:, u, :, :, HD:2 * HD],
                                          v_rest[:].rearrange("p c (h d) -> p c h d", h=H)).then_inc(s["v_1"], 1)

                steps(dve, body)

            @block.tensor
            def _(pe):
                def transpose_h(m, u):
                    pe.wait_ge(s["xn_ready"], m + 1)
                    for kd in range(KD):
                        for c in range(SUB):
                            last_ins = nc.tensor.transpose(h_ps[:, kd, c * P:(c + 1) * P],
                                                           xn[:, u, c, kd * P:(kd + 1) * P], g.ident[:])
                    last_ins.then_inc(s["h_transposed"], 1)

                pe.wait_ge(g.wmod_rest_in, 16)
                for b in range(B):
                    for half in range(2):
                        for k in range(KD):
                            last_ins = nc.tensor.matmul(
                                qk_ps[:, b, half, :], g.cond_wide[:, k, b, :],
                                g.wmod[:, k, 2 * D + half * 512:2 * D + (half + 1) * 512],
                                start=(k == 0), stop=(k == KD - 1))
                    last_ins.then_inc(s["rows_done"], 1)
                transpose_h(0, 0)
                pe.wait_ge(s["rows_used"], B)

                def body(n, u, k, last):
                    pe.wait_ge(s["lo_ready"], n + 1)
                    if inside(last, 1):
                        transpose_h(n + 1, 1 - u)
                    pe.wait_ge(s["qk_split"], n + 1)
                    for m in range(4):
                        products(nc, qk_ps[:, u, m // 2, (m % 2) * TILE:(m % 2 + 1) * TILE],
                                 [(g.wqkv_hi[:, kd, m * P:(m + 1) * P], g.wqkv_lo[:, kd, m * P:(m + 1) * P],
                                   h_hi[:, u, kd], h_lo[:, u, kd]) for kd in range(KD)], s["qk_done"] if m == 3 else None)
                    pe.wait_ge(s["v_rest_ready"], n + 1)
                    for c in range(SUB):
                        cols = slice(c * P, (c + 1) * P)
                        last_ins = products(nc, v_ps[:, u, c],
                                            [(h_hi[:, u, kd, cols], h_lo[:, u, kd, cols],
                                              g.wqkv_hi[:, kd, 2 * D:3 * D], g.wqkv_lo[:, kd, 2 * D:3 * D])
                                             for kd in range(KD)], None)
                    last_ins.then_inc(s["v_done"], 1)

                steps(pe, body)


def products(nc, out, operands, done):
    n = len(operands)
    for i, (l_hi, l_lo, r_hi, r_lo) in enumerate(operands):
        nc.tensor.matmul(out, l_lo, r_hi, start=(i == 0), stop=False)
        nc.tensor.matmul(out, l_hi, r_lo, start=False, stop=False)
        last = nc.tensor.matmul(out, l_hi, r_hi, start=False, stop=(i == n - 1))
    if done is not None:
        last.then_inc(done, 1)
    return last


def load_chunk(sp, g, dram, c, r):
    for part in range(4):
        rows = slice(part * HD, (part + 1) * HD)
        q = dram["qk"][part // 2, 0:D, ds(c * P + P, P)].rearrange("(h d) t -> d h t", d=HD)
        k = dram["qk"][part % 2, D:2 * D, ds(c * P, 2 * P)].rearrange("(h d) t -> d h t", d=HD)
        sp.dma_start(g.q_stack[rows, r].bitcast(F32), q).then_inc(g.qkv_in[r], 16)
        sp.dma_start(g.k_stack[rows, r].bitcast(F32), k).then_inc(g.qkv_in[r], 16)
    sp.dma_start(g.v_win[:, r], dram["v"][ds(c * P, 2 * P), :].rearrange("(w p) n -> p w n", p=P)
                 ).then_inc(g.qkv_in[r], 16)


def attend(nc, g, dram):
    with ExitStack() as stack:
        t = Tensors(nc, stack)
        q_stack, k_stack, v_win, qkv_in = g.q_stack, g.k_stack, g.v_win, g.qkv_in
        neg_max = t.sb("neg_max", [P, RING, 2])
        probs = t.sb("probs", [P, 2, 2, 2 * P])
        pt_hi = t.sb("pt_hi", [P, 2, 4, P], F16)
        pt_lo = t.sb("pt_lo", [P, 2, 4, P], F16)
        inverse = t.sb("inverse_sums", [P, 2, PAIRS])
        att_raw = t.sb("att_raw", [P, 2, PAIRS, HD])
        att = t.sb("att", [P, 2, PAIRS, HD])
        att_t = t.sb("att_t", [P, KD, P])
        gated = t.sb("gated", [P, D])
        stats = t.sb("stats2", [P, 6])
        mean_var = t.sb("mean_var2", [P, 2])
        newv = t.sb("newv2", [P, 1])
        rstd = t.sb("rstd2", [P, 1])
        newt = t.sb("newt2", [P, 1])
        xn = t.sb("xn2", [P, D])
        h = t.sb("h2", [P, RING, D])
        h_t = t.sb("h2_t", [P, KD, P])
        s_ps = t.ps("s_ps", [P, RING, 512])
        pt_ps = t.ps("pt_ps", [P, RING, 512])
        o_ps = t.ps("o_ps", [P, 512])
        rows_ps = t.ps("rows_ps", [P, 512])
        h_out = [t.sem(f"h_out{r}") for r in range(RING)]
        zero_out, gates_own = t.sem("zero_out"), t.sem("gates_own")
        names = ("scored", "max_ready", "exp_done", "p_transposed", "hi_done", "lo_done", "pv_done", "o_used",
                 "att_ready", "att_transposed", "att_t_ready", "projected", "gated_ready", "x_ready", "var_ready",
                 "h_ready", "h_transposed", "h_t_ready", "logits_done",
                 "logits_used", "stats_ready", "pool_own")
        s = {n: t.sem("a_" + n) for n in names}
        def chunks(body, eng):
            for c in range(2):
                body(c, c % RING, c // RING)
            with eng.Fori(0, (CHUNKS - 5) // RING) as k:
                for v in range(RING):
                    body(2 + v + RING * k, (2 + v) % RING, k + (2 + v) // RING)
            for c in range(CHUNKS - 3, CHUNKS + 2):
                body(c, c % RING, c // RING)

        def within(c, back=0, ahead=0):
            return not isinstance(c, int) or back <= c < CHUNKS + back - ahead

        def flat(a):
            return a.rearrange("p a d -> p (a d)")

        with nc.Block() as block:

            @block.sync
            def _(sp):
                for c in range(1, RING):
                    for u in range(2):
                        stores = 2 if c < RING - 1 else STEPS // 2 + 1
                        sp.wait_ge(g.qk_out[u], 16 * stores)
                        sp.wait_ge(g.v_out[u], 16 * stores)
                    load_chunk(sp, g, dram, c, c)

                def pad(name, width, c):
                    rows = dram[name].rearrange("(a s p) d -> p a s d", p=P, s=SUB)
                    sp.dma_start(rows[:, :, c], g.zeros[:, c:c + 1, 0:width].broadcast_to(
                        [P, SORTED // TILE, width])).then_inc(zero_out, 16)

                def body(c, r, turn):
                    if within(c, back=2):
                        sp.wait_ge(s["h_ready"], c - 1)
                        sp.dma_start(dram["h_rows"][ds((c - 2) * P, P), :], h[:, (r + 1) % RING, :]
                                     ).then_inc(h_out[(r + 1) % RING], 16)
                    if within(c, ahead=RING):
                        sp.wait_ge(s["pv_done"], PAIRS * (c + 1) + 2)
                        load_chunk(sp, g, dram, c + RING, r)
                    if isinstance(c, int) and c < 2:
                        pad("h_sorted", D, c)
                    if isinstance(c, int) and CHUNKS - 3 <= c < CHUNKS - 1:
                        pad("x_sorted", XROW, c - (CHUNKS - 3))
                    if isinstance(c, int) and c == CHUNKS - 1:
                        load_weights(sp, g, dram["w1s"], dram["w2s"], dram["w3s"], g.shared_in)

                chunks(body, sp)
                for r in range(RING):
                    sp.wait_ge(h_out[r], 16 * ((CHUNKS - 1 - r) // RING + 2))
                sp.wait_ge(zero_out, 16 * 2 * SUB)

            @block.gpsimd
            def _(pool):
                for name, n in (("p_transposed", 2), ("pv_done", 2), ("o_used", 2), ("att_transposed", 1),
                                ("logits_used", 2)):
                    pool.sem_inc(s[name], n)
                for r in range(RING):
                    pool.sem_inc(h_out[r], 16)
                OWN = 10

                def body(c, r, turn):
                    if within(c, back=1):
                        x = flat(g.x[:, ds(c - 1, 1), 0:D])
                        batch = (c - 1) // (CHUNKS // B)
                        slot, its_turn = (r + 2) % RING, turn - (r < 1)
                        pool.wait_ge(s["gated_ready"], c)
                        nc.gpsimd.tensor_tensor(x, x, gated[:], ALU.add).then_inc(s["x_ready"], 1)
                        order = OwnOrder(pool, s["pool_own"], OWN * (c - 1))
                        pool.wait_ge(s["var_ready"], c)
                        order.step(rsqrt(nc, order, rstd[:], mean_var[:, 1:2], newv[:], newt[:], g))
                        apart_on_pool(nc, g, 3)
                        order.step(nc.gpsimd.tensor_tensor(xn[:], x, mean_var[:, 0:1].broadcast_to([P, D]),
                                                           ALU.subtract))
                        order.step(nc.gpsimd.tensor_tensor(xn[:], xn[:], rstd[:].broadcast_to([P, D]), ALU.mult))
                        apart_on_pool(nc, g, 4)
                        order.step(nc.gpsimd.tensor_tensor(xn[:], xn[:], flat(g.scale_b[:, ds(batch, 1), :]),
                                                           ALU.mult))
                        pool.wait_ge(h_out[slot], 16 * (its_turn + 1))
                        apart_on_pool(nc, g, 5)
                        nc.gpsimd.tensor_tensor(h[:, slot], xn[:], flat(g.shift_b[:, ds(batch, 1), :]),
                                                ALU.add).then_inc(s["h_ready"], 1)
                        assert order.n == OWN

                chunks(body, pool)

            @block.scalar
            def _(act):
                def exps(n, p, r):
                    act.wait_ge(s["max_ready"], n + 1)
                    act.wait_ge(s["p_transposed"], n + 1)
                    for i in range(2):
                        ins = nc.scalar.activation(probs[:, p % 2, i], s_ps[:, r, i * 2 * P:(i + 1) * 2 * P],
                                                   ACT.Exp, bias=neg_max[:, r, i:i + 1])
                    ins.then_inc(s["exp_done"], 1)

                exps(0, 0, 0)

                def body(c, r, turn):
                    for p in range(PAIRS):
                        n = PAIRS * c + p
                        if within(c, ahead=(p == PAIRS - 1)):
                            exps(n + 1, p + 1, (PAIRS * r + p + 1) % RING)
                        if p == 3 and within(c, back=1):
                            act.wait_ge(s["att_transposed"], c + 1)
                            nc.scalar.activation(att_t[:].rearrange("p k t -> p (k t)"), rows_ps[:, 0:D],
                                                 ACT.Copy).then_inc(s["att_t_ready"], 1)
                        if p == 6 and within(c, back=2):
                            act.wait_ge(s["h_transposed"], c - 1)
                            nc.scalar.activation(h_t[:].rearrange("p k t -> p (k t)"), rows_ps[:, 0:D],
                                                 ACT.Copy).then_inc(s["h_t_ready"], 1)
                        if within(c):
                            act.wait_ge(s["p_transposed"], n + 3)
                            act.wait_ge(s["pv_done"], n + 1)
                            nc.scalar.activation(flat(pt_hi[:, p % 2]), pt_ps[:, (PAIRS * r + p) % RING],
                                                 ACT.Copy).then_inc(s["hi_done"], 1)

                chunks(body, act)

            @block.vector
            def _(dve):
                def row_max(n, r):
                    dve.wait_ge(s["scored"], n + 1)
                    nc.vector.tensor_reduce(neg_max[:, r, :], s_ps[:, r].rearrange("p (i t) -> p i t", i=2),
                                            AX.X, ALU.max, negate=True).then_inc(s["max_ready"], 1)

                def sum_parts(c, half):
                    dve.wait_ge(s["pv_done"], PAIRS * c + 4 * half + 4 + 2)
                    o = o_ps[:, 0:PAIRS * VROW].rearrange("p (h c) -> p h c", h=PAIRS)
                    nc.vector.tensor_reduce(
                        att_raw[:, half], o[:, :, 0:3 * HD].rearrange("p h (a d) -> p h d a", a=3), AX.X, ALU.add)
                    nc.vector.reciprocal(inverse[:, half], o[:, :, 3 * HD]).then_inc(s["o_used"], 1)

                def divide(c, half):
                    dve.wait_ge(s["o_used"], 2 * c + half + 1 + 2)
                    if half == 0:
                        dve.wait_ge(s["att_transposed"], c + 1)
                    nc.vector.tensor_tensor(
                        att[:, half], att_raw[:, half], inverse[:, half].unsqueeze(2).broadcast_to([P, PAIRS, HD]),
                        ALU.mult).then_inc(s["att_ready"], 1)

                def gate(c):
                    dve.wait_ge(s["projected"], c)
                    nc.vector.tensor_tensor(gated[:], rows_ps[:, D:2 * D],
                                            flat(g.gate_a[:, ds((c - 1) // (CHUNKS // B), 1), :]),
                                            ALU.mult).then_inc(s["gated_ready"], 1)

                def statistics(c):
                    dve.wait_ge(s["x_ready"], c)
                    apart(nc, g)
                    nc.vector.bn_stats(stats[:], flat(g.x[:, ds(c - 1, 1), 0:D])).then_inc(s["stats_ready"], 1)

                def variance(c):
                    dve.wait_ge(s["stats_ready"], c)
                    apart(nc, g, cell=2)
                    nc.vector.bn_aggr(mean_var[:], stats[:]).then_inc(s["var_ready"], 1)

                def keep_logits(c):
                    dve.wait_ge(s["logits_done"], c - 1)
                    nc.vector.tensor_copy(flat(g.logits[:, ds(c - 2, 1), :]), rows_ps[:, D:D + E]
                                          ).then_inc(s["logits_used"], 1)

                gates_order = OwnOrder(dve, gates_own)

                def bound_gate(rows, scratch):
                    order = gates_order
                    sign, size = (scratch[:, i * B * D:(i + 1) * B * D].rearrange("p (b d) -> p b d", b=B)
                                  for i in range(2))
                    order.step(nc.vector.tensor_scalar(sign, rows[:], 0.0, 2.0, ALU.is_ge, ALU.mult))
                    order.step(nc.vector.tensor_scalar(sign, sign, 1.0, None, ALU.subtract))
                    order.step(nc.vector.tensor_tensor(size, rows[:], sign, ALU.mult))
                    order.step(nc.vector.tensor_scalar(size, size, 0.25, None, ALU.max))
                    order.step(nc.vector.tensor_tensor(rows[:], size, sign, ALU.mult))

                row_max(0, 0)
                row_max(1, 1)
                bound_gate(g.gate_a, g.raw)

                def body(c, r, turn):
                    for p in range(PAIRS):
                        n = PAIRS * c + p
                        if within(c, ahead=(p >= PAIRS - 2)):
                            row_max(n + 2, (PAIRS * r + p + 2) % RING)
                        if p == 0 and within(c, back=1):
                            sum_parts(c - 1, 1)
                        if p == 4 and within(c):
                            sum_parts(c, 0)
                        if within(c):
                            dve.wait_ge(s["hi_done"], n + 1)
                            nc.vector.tensor_tensor(flat(pt_lo[:, p % 2]), pt_ps[:, (PAIRS * r + p) % RING],
                                                    pt_hi[:, p % 2].rearrange("p a t -> p (a t)"),
                                                    ALU.subtract).then_inc(s["lo_done"], 1)
                        if p == 1 and within(c, back=1):
                            divide(c - 1, 1)
                        if p == 4 and within(c, back=1):
                            gate(c)
                        if p == 5 and within(c, back=1):
                            statistics(c)
                        if p == 6 and within(c):
                            divide(c, 0)
                        if p == 6 and within(c, back=1):
                            variance(c)
                        if p == 7 and within(c, back=2):
                            if isinstance(c, int) and c == CHUNKS + 1:
                                bound_gate(g.gate_b, probs[:].rearrange("p r i t -> p (r i t)"))
                                gates_order.step(nc.vector.tensor_tensor(g.gate_step[:], g.gate_b[:, 1, :],
                                                                         g.gate_b[:, 0, :], ALU.subtract))
                            keep_logits(c)

                chunks(body, dve)

            @block.tensor
            def _(pe):
                def which_mask(c):
                    per = CHUNKS // B
                    which = (c + per - 1) // per - c // per
                    return which if isinstance(which, int) else pe.snap(pe.to_reg(which), min_val=0, max_val=1)

                def scores(n, p, r, turn, mask, guard=True):
                    bank = (PAIRS * r + p) % RING
                    if p == 0:
                        pe.wait_ge(qkv_in[r], 16 * LOADS * (turn + 1))
                    if guard:
                        pe.wait_ge(s["exp_done"], n - 2)
                    nc.tensor.matmul(s_ps[:, bank], g.identb[:], flat(g.mask[:, ds(mask, 1), :]),
                                     start=True, stop=False)
                    for i in range(2):
                        ins = nc.tensor.matmul(s_ps[:, bank, i * 2 * P:(i + 1) * 2 * P], q_stack[:, r, 2 * p + i],
                                               k_stack[:, r, 2 * p + i], start=False, stop=(i == 1))
                    ins.then_inc(s["scored"], 1)

                def transpose_probs(n, p, bank):
                    pe.wait_ge(s["exp_done"], n + 1)
                    for i in range(2):
                        for w in range(2):
                            ins = nc.tensor.transpose(pt_ps[:, bank, (2 * i + w) * P:(2 * i + w + 1) * P],
                                                      probs[:, p % 2, i, w * P:(w + 1) * P], g.ident[:])
                    ins.then_inc(s["p_transposed"], 1)

                def weigh(c, n, p, r):
                    pe.wait_ge(s["lo_done"], n + 1)
                    half = p // 4
                    if p % 4 == 0:
                        pe.wait_ge(s["o_used"], 2 * c + half + 2)
                    for i in range(2):
                        head = 2 * p + i
                        col = (head % PAIRS) * VROW
                        for w in range(2):
                            for part, pt in enumerate((pt_lo, pt_hi)):
                                ins = nc.tensor.matmul(
                                    o_ps[:, col:col + VCOLS], pt[:, p % 2, 2 * i + w],
                                    v_win[:, r, w, head * VROW:head * VROW + VCOLS],
                                    start=(w == 0 and part == 0), stop=(w == 1 and part == 1))
                    ins.then_inc(s["pv_done"], 1)

                def transpose_rows(rows, done):
                    for kd in range(KD):
                        ins = nc.tensor.transpose(rows_ps[:, kd * P:(kd + 1) * P], rows[:, kd * P:(kd + 1) * P],
                                                  g.ident[:])
                    ins.then_inc(s[done], 1)

                def multiply_rows(rows_t, w, n, done):
                    for kd in range(KD):
                        ins = nc.tensor.matmul(rows_ps[:, D:D + n], rows_t[:, kd], w[:, kd],
                                               start=(kd == 0), stop=(kd == KD - 1))
                    ins.then_inc(s[done], 1)

                mask = which_mask(0)
                for p in range(RING):
                    scores(p, p, 0, 0, mask, guard=False)
                transpose_probs(0, 0, 0)

                def body(c, r, turn):
                    mask = which_mask(c) if within(c) else None
                    for p in range(PAIRS):
                        n = PAIRS * c + p
                        q = p + RING
                        if p == 4 and within(c, back=1):
                            pe.wait_ge(s["att_t_ready"], c)
                            multiply_rows(att_t, g.wo, D, "projected")
                        if p == 7 and within(c, back=2):
                            pe.wait_ge(s["h_t_ready"], c - 1)
                            multiply_rows(h_t, g.wg, E, "logits_done")
                        if q < PAIRS:
                            if within(c):
                                scores(n + RING, q, r, turn, mask)
                        elif within(c, ahead=1):
                            if q == PAIRS:
                                mask = which_mask(c + 1)
                            scores(n + RING, q - PAIRS, (r + 1) % RING, turn + (r + 1) // RING, mask)
                        if within(c, ahead=(p == PAIRS - 1)):
                            transpose_probs(n + 1, p + 1, (PAIRS * r + p + 1) % RING)
                        if p == 2 and within(c, back=1):
                            pe.wait_ge(s["att_ready"], 2 * c)
                            pe.wait_ge(s["logits_used"], c)
                            transpose_rows(att[:].rearrange("p a h d -> p (a h d)"), "att_transposed")
                        if p == 5 and within(c, back=2):
                            pe.wait_ge(s["h_ready"], c - 1)
                            pe.wait_ge(*((s["gated_ready"], c) if within(c, back=1) else (s["logits_used"], c)))
                            transpose_rows(h[:, (r + 1) % RING], "h_transposed")
                        if within(c):
                            weigh(c, n, p, r)

                chunks(body, pe)


def route(nc, g, dram):
    with ExitStack() as stack:
        t = Tensors(nc, stack)
        less_eight = t.sb("less_eight", [P, E])
        top = t.sb("top", [P, CHUNKS])
        onehot = t.sb("onehot", [P, CHUNKS, E])
        held = t.sb("held", [P, CHUNKS, E])
        counts = t.sb("counts", [P, CHUNKS, E])
        sums = t.sb("count_sums", [P, 2, CHUNKS // 2 + CHUNKS, E])
        whole = t.sb("whole", [P, E], I32)
        tiles = t.sb("tiles", [P, E])
        tile_sums = t.sb("tile_sums", [P, 2, E // 2 + E])
        bounds = t.sb("bounds_f", [P, E + 1])
        rank_ps = t.ps("rank_ps", [P, 512])
        count_ps = t.ps("count_ps", [P, 512])
        hi_done, lo_done, eight_ready, chosen, ranked, own = (
            t.sem("r_" + n) for n in ("hi_done", "lo_done", "eight_ready", "chosen", "ranked", "own"))

        with nc.Block() as block:

            @block.sync
            def _(sp):
                load_rows(sp, g, dram, "h_rows", 0)

            @block.scalar
            def _(act):
                for i in range(3):
                    act.wait_ge(g.shared_in, 48)
                    cols = slice(i * KD * F, (i + 1) * KD * F)
                    nc.scalar.activation(g.w_hi[:, 0, cols], g.raw[:, cols], ACT.Copy).then_inc(hi_done, 1)

            @block.gpsimd
            def _(pool):
                for e in range(E):
                    nc.gpsimd.memset(less_eight[:, e:e + 1], float(e - E))
                nc.gpsimd.memset(sums[:, :, 0:CHUNKS // 2, :], 0.0)
                nc.gpsimd.memset(tile_sums[:, :, 0:E // 2], 0.0)
                nc.gpsimd.memset(g.ones[:], 1.0)
                nc.gpsimd.memset(g.before[:], 1.0).then_inc(eight_ready, 1)
                pool.wait_ge(eight_ready, 1)
                nc.gpsimd.affine_select(
                    out=g.before[:], in_=g.before[:], compare_op=ALU.is_gt, fill=0.0, base=0,
                    pattern=[[1, P]], channel_multiplier=-1).then_inc(eight_ready, 1)
                for i in range(1, 3):
                    pool.wait_ge(hi_done, i + 1)
                    cols = slice(i * KD * F, (i + 1) * KD * F)
                    nc.gpsimd.tensor_tensor(g.w_lo[:, 0, cols], g.raw[:, cols], g.w_hi[:, 0, cols].bitcast(F32),
                                            ALU.subtract).then_inc(lo_done, 1)
                pool.wait_ge(lo_done, 2)

            @block.vector
            def _(dve):
                order = OwnOrder(dve, own)
                wide = [P, CHUNKS, E]
                order.step(nc.vector.tensor_reduce(top[:], g.logits[:], AX.X, ALU.max))
                order.step(nc.vector.tensor_tensor(onehot[:], g.logits[:], top[:].unsqueeze(2).broadcast_to(wide),
                                                   ALU.is_ge))
                dve.wait_ge(eight_ready, 1)
                experts = less_eight[:].unsqueeze(1).broadcast_to(wide)
                order.step(nc.vector.tensor_tensor(held[:], onehot[:], experts, ALU.mult))
                order.step(nc.vector.tensor_reduce(top[:], held[:], AX.X, ALU.min))
                nc.vector.tensor_tensor(onehot[:], experts, top[:].unsqueeze(2).broadcast_to(wide),
                                        ALU.is_equal).then_inc(chosen, 1)
                dve.wait_ge(hi_done, 1)
                order(nc.vector.tensor_tensor(g.w_lo[:, 0, 0:KD * F], g.raw[:, 0:KD * F],
                                              g.w_hi[:, 0, 0:KD * F].bitcast(F32), ALU.subtract))
                dve.wait_ge(ranked, 1)
                flat = lambda a: a.rearrange("p c e -> p (c e)")
                order(nc.vector.tensor_copy(flat(counts[:]), count_ps[:, 0:CHUNKS * E]))
                C0, E0 = CHUNKS // 2, E // 2
                order.step(nc.vector.tensor_copy(flat(sums[:, 0, C0:]), count_ps[:, 0:CHUNKS * E]))
                now, d = 0, 1
                while d < CHUNKS:
                    order.step(nc.vector.tensor_tensor(sums[:, 1 - now, C0:], sums[:, now, C0:],
                                                       sums[:, now, C0 - d:C0 - d + CHUNKS], ALU.add))
                    now, d = 1 - now, 2 * d
                order.step(nc.vector.tensor_scalar(tiles[:], sums[:, now, C0 + CHUNKS - 1], float(TILE - 1), None, ALU.add))
                order.step(nc.vector.tensor_copy(whole[:], tiles[:]))
                order.step(nc.vector.tensor_scalar(whole[:], whole[:], TILE.bit_length() - 1, None,
                                                   ALU.logical_shift_right))
                order.step(nc.vector.tensor_copy(tiles[:], whole[:]))
                order.step(nc.vector.tensor_scalar(tiles[:], tiles[:], 1.0, None, ALU.max))
                order.step(nc.vector.tensor_copy(tile_sums[:, 0, E0:], tiles[:]))
                at, d = 0, 1
                while d < E:
                    order.step(nc.vector.tensor_tensor(tile_sums[:, 1 - at, E0:], tile_sums[:, at, E0:],
                                                       tile_sums[:, at, E0 - d:E0 - d + E], ALU.add))
                    at, d = 1 - at, 2 * d
                order(nc.vector.memset(bounds[:, 0:1], float(STEPS)))
                order(nc.vector.tensor_scalar(bounds[:, 1:], tile_sums[:, at, E0:], float(STEPS), None, ALU.add))
                order.step(nc.vector.tensor_tensor(tiles[:], tile_sums[:, at, E0:], tiles[:], ALU.subtract))
                order(nc.vector.tensor_copy(g.bounds[:], bounds[:]))
                order(nc.vector.tensor_scalar(tiles[:], tiles[:], float(TILE), None, ALU.mult))
                order.step(nc.vector.tensor_tensor(sums[:, now, C0:], sums[:, now, C0:], counts[:], ALU.subtract))
                order.step(nc.vector.tensor_tensor(sums[:, now, C0:], sums[:, now, C0:],
                                                   rank_ps[:, 0:CHUNKS * E].rearrange("p (c e) -> p c e", e=E), ALU.add))
                order.step(nc.vector.tensor_tensor(sums[:, now, C0:], sums[:, now, C0:],
                                                   tiles[:].unsqueeze(1).broadcast_to(wide), ALU.add))
                order.step(nc.vector.tensor_tensor(sums[:, now, C0:], sums[:, now, C0:], onehot[:], ALU.mult))
                order.step(nc.vector.tensor_reduce(top[:], sums[:, now, C0:], AX.X, ALU.add))
                order.step(nc.vector.tensor_copy(g.slots[:], top[:]))

            @block.tensor
            def _(pe):
                pe.wait_ge(chosen, 1)
                pe.wait_ge(eight_ready, 2)
                flat = onehot[:].rearrange("p c e -> p (c e)")
                nc.tensor.matmul(rank_ps[:, 0:CHUNKS * E], g.before[:], flat, start=True, stop=True)
                nc.tensor.matmul(count_ps[:, 0:CHUNKS * E], g.ones[:], flat, start=True, stop=True).then_inc(ranked, 1)


def load_rows(sp, g, dram, source, at):
    sp.dma_start(g.rows[:], dram[source][ds(at, TILE), :].rearrange("(s p) d -> p s d", p=P)
                 ).then_inc(g.rows_in, 16)


def load_weights(eng, g, w1, w2, w3, done):
    for i, w in enumerate((w1, w2, w3)):
        n = w.shape[1]
        eng.dma_start(g.raw[:, i * KD * F:(i + 1) * KD * F].rearrange("p (k n) -> p k n", n=n),
                      w.rearrange("(k p) n -> p k n", p=P)).then_inc(done, 16)


PIECES = 8
PIECE = 3 * KD * F // PIECES


def experts(nc, g, dram):
    with ExitStack() as stack:
        t = Tensors(nc, stack)
        rows = g.rows
        index_h = t.sb("index_h", [P, SUB], U32)
        index_x = t.sb("index_x", [P, SUB], U32)
        h_hi = t.sb("e_h_hi", [P, KD, TILE], F32R)
        h_lo = t.sb("e_h_lo", [P, KD, TILE], F32R)
        gelu = t.sb("gelu", [P, 2, TILE])
        a = t.sb("a", [P, 3, TILE])
        a_hi = t.sb("a_hi", [P, KF, TILE], F32R)
        a_lo = t.sb("a_lo", [P, KF, TILE], F32R)
        gated = t.sb("gated_y", [P, SUB, XROW])
        x_rows = t.sb("x_rows", [P, SUB, XROW])
        gates = t.sb("gates", [P, SUB, D])
        gu_ps = t.ps("gu_ps", [P, 4, 512])
        h_ps = t.ps("e_h_ps", [P, KD, TILE])
        y_ps = t.ps("y_ps", [P, SUB, 512])
        names = ("scattered", "index_h_ready", "index_x_ready", "h_transposed", "h_hi_ready", "h_ready", "gu_done",
                 "gelu_done", "mul_done", "a_hi_done", "a_ready", "y_done", "x_ready", "y_used", "x_rows_out",
                 "x_rows_free", "x_in", "gates_ready", "raw_in",
                 "hi_split", "lo_split", "gated_zero", "all_stored")
        s = {n: t.sem("e_" + n) for n in names}
        s["rows_in"] = g.rows_in

        def tiles(eng, body, before=None):
            body(0, 0, 0, False, False)
            with eng.Fori(1, STEPS - 1) as i:
                body(i, 0, None, False, False)
            body(STEPS - 1, 0, None, False, True)

            def expert(e, slot, more):
                first = eng.value_load(g.bounds[0:1, ds(e, 1)], min_val=STEPS, max_val=STEPS + TILES_MAX - 1)
                end = eng.value_load(g.bounds[0:1, ds(e + 1, 1)], min_val=STEPS + 1, max_val=STEPS + TILES_MAX)
                if before:
                    before(e)
                body(first, slot, e + 1 if more else None, True, False)
                with eng.If(end > first + 1):
                    with eng.Fori(first + 1, end) as i:
                        body(i, slot, None, True, False)

            with eng.Fori(0, E // 2 - 1) as k:
                for u in range(2):
                    expert(2 * k + u, (u + 1) % 2, True)
            for e in (E - 2, E - 1):
                expert(e, (e + 1) % 2, e < E - 1)

        def load_next_weights(pool, e):
            load_weights(pool, g, *(dram[n][ds(e, 1)].rearrange("a k n -> (a k) n") for n in ("W1", "W2", "W3")),
                         s["raw_in"])

        with nc.Block() as block:

            @block.sync
            def _(sp):
                def body(i, slot, nxt, routed, last):
                    snap = (lambda v: v) if isinstance(i, int) else (lambda v: sp.snap(sp.to_reg(v)))
                    scattered = snap(SUB * 16 * (i + 1))
                    at = snap((i + 1 - STEPS if routed or last else i + 1) * TILE)
                    x_at = snap((i - STEPS) * TILE)
                    sp.wait_ge(s["h_transposed"], i + 1)
                    if not routed:
                        sp.wait_ge(s["scattered"], scattered)
                    load_rows(sp, g, dram, "h_sorted" if routed or last else "h_rows", at)
                    if routed:
                        sp.wait_ge(s["x_rows_free"], i)
                        sp.dma_start(x_rows[:], dram["x_sorted"][ds(x_at, TILE), :].rearrange(
                            "(s p) d -> p s d", p=P)).then_inc(s["x_in"], 16)

                tiles(sp, body)
                end = sp.value_load(g.bounds[0:1, E:E + 1], min_val=STEPS + E, max_val=STEPS + TILES_MAX)
                rows_all = sp.snap(sp.to_reg(16 * (end + 1)))
                sp.wait_ge(s["x_rows_free"], end)
                sp.wait_ge(s["rows_in"], rows_all)
                sp.sem_inc(s["all_stored"], 1)

            @block.gpsimd
            def _(pool):
                pool.sem_inc(s["mul_done"], 4)
                pool.sem_inc(s["y_used"], 1)
                pool.sem_inc(s["x_in"], 16 * STEPS)
                pool.sem_inc(s["gates_ready"], STEPS)
                load_next_weights(pool, 0)

                def scatter(name, index, rows, done):
                    for c in range(SUB):
                        nc.gpsimd.indirect_dma_start(
                            out=dram[name][:, :],
                            out_offset=bass.IndirectOffsetOnAxis(ap=index[:, c:c + 1], axis=0),
                            in_=rows[:, c, :], in_offset=None).then_inc(s[done], 16)

                def scatter_h(i):
                    if not (isinstance(i, int) and i == 0):
                        pool.wait_ge(s["scattered"], SUB * 16 * i)
                    pool.wait_ge(s["rows_in"], 16 * (i + 1))
                    apart_on_pool(nc, g, 2)
                    nc.gpsimd.tensor_copy(index_h[:], g.slots[:, ds(i * SUB, SUB)]).then_inc(s["index_h_ready"], 1)
                    pool.wait_ge(s["index_h_ready"], i + 1)
                    apart_on_pool(nc, g, 3)
                    scatter("h_sorted", index_h, rows, "scattered")

                def body(i, slot, nxt, routed, last):
                    if not routed and not last:
                        scatter_h(i + 1)
                    if nxt is not None:
                        for p in range(PIECES):
                            pool.wait_ge(s["hi_split"], PIECES * nxt + p + 1)
                            cols = slice(p * PIECE, (p + 1) * PIECE)
                            ins = nc.gpsimd.tensor_tensor(g.w_lo[:, 1 - slot, cols], g.raw[:, cols],
                                                          g.w_hi[:, 1 - slot, cols].bitcast(F32), ALU.subtract)
                        ins.then_inc(s["lo_split"], 1)
                    if not (isinstance(i, int) and i == 0):
                        pool.wait_ge(s["x_rows_free"], i)
                    pool.wait_ge(s["x_ready"], i + 1)
                    apart_on_pool(nc, g, 5)
                    where = x_rows[:, :, D] if routed else g.slots[:, ds(i * SUB, SUB)]
                    nc.gpsimd.tensor_copy(index_x[:], where).then_inc(s["index_x_ready"], 1)
                    pool.wait_ge(s["index_x_ready"], i + 1)
                    apart_on_pool(nc, g, 6)
                    if routed:
                        scatter("out", index_x, x_rows[:, :, 0:D], "x_rows_out")
                    else:
                        scatter("x_sorted", index_x, x_rows, "x_rows_out")
                    pool.wait_ge(s["x_rows_out"], SUB * 16 * (i + 1))
                    apart_on_pool(nc, g, 7).then_inc(s["x_rows_free"], 1)
                    if nxt is not None and (not isinstance(nxt, int) or nxt + 1 < E):
                        pool.wait_ge(s["lo_split"], nxt + 1)
                        apart_on_pool(nc, g, 4)
                        load_next_weights(pool, nxt + 1)

                scatter_h(0)
                tiles(pool, body)

            @block.scalar
            def _(act):
                def evacuate_h(i):
                    act.wait_ge(s["h_transposed"], i + 1)
                    nc.scalar.activation(h_hi[:], h_ps[:], ACT.Copy).then_inc(s["h_hi_ready"], 1)

                def body(i, slot, nxt, routed, last):
                    for j in range(KF):
                        act.wait_ge(s["gu_done"], KF * i + j + 1)
                        act.wait_ge(s["mul_done"], KF * i + j - 1 + 4)
                        nc.scalar.activation(gelu[:, j % 2], gu_ps[:, j % 4, 0:TILE], ACT.Gelu).then_inc(s["gelu_done"], 1)
                        if nxt is not None:
                            if j == 0:
                                act.wait_ge(s["raw_in"], 48 * (nxt + 1))
                            cols = slice(j * PIECE, (j + 1) * PIECE)
                            nc.scalar.activation(g.w_hi[:, 1 - slot, cols], g.raw[:, cols],
                                                 ACT.Copy).then_inc(s["hi_split"], 1)
                    evacuate_h(i + 1)
                evacuate_h(0)
                tiles(act, body)

            @block.vector
            def _(dve):
                def rest_of_h(i):
                    dve.wait_ge(s["h_hi_ready"], i + 1)
                    nc.vector.tensor_tensor(h_lo[:], h_ps[:], h_hi[:].bitcast(F32), ALU.subtract).then_inc(s["h_ready"], 1)

                def body(i, slot, nxt, routed, last):
                    def low(j):
                        dve.wait_ge(s["a_hi_done"], KF * i + j + 1)
                        nc.vector.tensor_tensor(a_lo[:, j], a[:, j % 3], a_hi[:, j].bitcast(F32),
                                                ALU.subtract).then_inc(s["a_ready"], 1)

                    for j in range(KF):
                        dve.wait_ge(s["gelu_done"], KF * i + j + 1)
                        nc.vector.tensor_tensor(a[:, j % 3], gelu[:, j % 2], gu_ps[:, j % 4, TILE:2 * TILE],
                                                ALU.mult).then_inc(s["mul_done"], 1)
                        if j:
                            low(j - 1)
                        dve.wait_ge(s["mul_done"], KF * i + j + 1 + 4)
                        nc.vector.tensor_copy(a_hi[:, j], a[:, j % 3]).then_inc(s["a_hi_done"], 1)
                    low(KF - 1)
                    rest_of_h(i + 1)
                    if routed:
                        dve.wait_ge(s["x_in"], 16 * (i + 1))
                        for c in range(SUB):
                            ins = nc.vector.scalar_tensor_tensor(
                                gates[:, c], g.gate_step[:], x_rows[:, c, D + 1:XROW], g.gate_b[:, 0, :],
                                ALU.mult, ALU.add)
                        ins.then_inc(s["gates_ready"], 1)
                        dve.wait_ge(s["gates_ready"], i + 1)
                        gate = lambda c: gates[:, c]
                    else:
                        shared_gate = g.gate_b[:, ds(i // (STEPS // B), 1), :].rearrange("p a d -> p (a d)")
                        gate = lambda c: shared_gate
                    dve.wait_ge(s["y_done"], i + 1)
                    for c in range(SUB):
                        ins = nc.vector.tensor_tensor(gated[:, c, 0:D], y_ps[:, c, 0:D], gate(c), ALU.mult)
                    ins.then_inc(s["y_used"], 1)
                    dve.wait_ge(s["y_used"], i + 2)
                    if not routed and not (isinstance(i, int) and i == 0):
                        dve.wait_ge(s["x_rows_free"], i)
                    x, n = (x_rows[:], D) if routed else (g.x[:, ds(i * SUB, SUB), :], XROW)
                    nc.vector.tensor_tensor(x_rows[:, :, 0:n], x[:, :, 0:n], gated[:, :, 0:n],
                                            ALU.add).then_inc(s["x_ready"], 1)

                nc.vector.memset(gated[:], 0.0).then_inc(s["gated_zero"], 1)
                dve.wait_ge(s["gated_zero"], 1)
                rest_of_h(0)
                tiles(dve, body)

            @block.tensor
            def _(pe):
                def transpose_h(i):
                    pe.wait_ge(s["rows_in"], 16 * (i + 1))
                    for kd in range(KD):
                        for c in range(SUB):
                            ins = nc.tensor.transpose(h_ps[:, kd, c * P:(c + 1) * P], rows[:, c, kd * P:(kd + 1) * P],
                                                      g.ident[:])
                    ins.then_inc(s["h_transposed"], 1)

                def weights(slot, which, k, cols, n):
                    at = which * KD * F + k * n
                    cols = slice(at + cols.start, at + cols.stop)
                    return g.w_hi[:, slot, cols], g.w_lo[:, slot, cols]

                def body(i, slot, nxt, routed, last):
                    for j in range(KF):
                        if j == 0:
                            pe.wait_ge(s["h_ready"], i + 1)
                        pe.wait_ge(s["mul_done"], KF * i + j + 1)
                        cols = slice(j * P, (j + 1) * P)
                        for which in range(2):
                            products(nc, gu_ps[:, j % 4, which * TILE:(which + 1) * TILE],
                                     [(*weights(slot, which, kd, cols, F), h_hi[:, kd], h_lo[:, kd])
                                      for kd in range(KD)], s["gu_done"] if which else None)
                    transpose_h(i + 1)
                    pe.wait_ge(s["y_used"], i + 1)
                    for k in range(KF):
                        pe.wait_ge(s["a_ready"], KF * i + k + 1)
                        w_hi, w_lo = weights(slot, 2, k, slice(0, D), D)
                        for c in range(SUB):
                            cols = slice(c * P, (c + 1) * P)
                            out = y_ps[:, c, 0:D]
                            nc.tensor.matmul(out, a_lo[:, k, cols], w_hi, start=(k == 0), stop=False)
                            nc.tensor.matmul(out, a_hi[:, k, cols], w_lo, start=False, stop=False)
                            ins = nc.tensor.matmul(out, a_hi[:, k, cols], w_hi, start=False, stop=(k == KF - 1))
                    ins.then_inc(s["y_done"], 1)

                transpose_h(0)
                tiles(pe, body, lambda e: pe.wait_ge(s["lo_split"], e + 1))


class Globals:

    def __init__(self, t):
        self.x = t.sb("x_res", [P, CHUNKS, XROW])
        self.ident = t.sb("ident", [P, P])
        self.eps = t.sb("eps", [P, SUB])
        self.minus_half = t.sb("minus_half", [P, SUB])
        self.three_halves = t.sb("three_halves", [P, SUB])
        self.logits = t.sb("logits", [P, CHUNKS, E])
        self.scrap = t.sb("scrap", [P, 8])
        self.gate_b = t.sb("gate_b", [P, B, D])
        self.raw = t.sb("w_raw", [P, 3 * KD * F])
        self.shared_in = t.sem("shared_in")
        self.gate_step = t.sb("gate_step", [P, D])

    def for_attention(self, t):
        self.identb = t.sb("identb", [P, P], BF16)
        self.mask = t.sb("mask", [P, 2, 512], BF16)
        self.zeros = t.sb("zeros", [P, SUB, XROW])
        self.wmod = self.raw[:, 0:KD * 6 * D].rearrange("p (k n) -> p k n", k=KD)
        self.cond_wide = self.raw[:, KD * 6 * D:KD * (6 * D + B * P)].rearrange("p (k b n) -> p k b n", k=KD, b=B)
        self.x_in = [t.sem(f"x_in{u}") for u in range(2)]
        self.wmod_rest_in, self.wo_in, self.pad_out = (t.sem(n) for n in ("wmod_rest_in", "wo_in", "pad_out"))
        self.qk = t.sb("qk_hilo", [P, 2, 2, 4, TILE], F32R)
        self.v_rows = t.sb("v_rows", [P, 2, SUB, H, VROW], BF16)
        self.qk_out = [t.sem(f"qk_out{u}") for u in range(2)]
        self.v_out = [t.sem(f"v_out{u}") for u in range(2)]
        self.q_stack = t.sb("q_stack", [4 * HD, RING, H, P], F32R)
        self.k_stack = t.sb("k_stack", [4 * HD, RING, H, 2 * P], F32R)
        self.v_win = t.sb("v_win", [P, RING, 2, H * VROW], BF16)
        self.qkv_in = [t.sem(f"qkv_in{r}") for r in range(RING)]
        self.wqkv_hi = t.sb("wqkv_hi", [P, KD, 3 * D], F32R)
        self.wqkv_lo = t.sb("wqkv_lo", [P, KD, 3 * D], F32R)
        self.wo = t.sb("wo_sb", [P, KD, D])
        self.wg = t.sb("wg_sb", [P, KD, E])
        self.shift_a = t.sb("shift_a", [P, B, KD])
        self.scale_a = t.sb("scale_a", [P, B, KD])
        self.gate_a = t.sb("gate_a", [P, B, D])
        self.shift_b = t.sb("shift_b", [P, B, D])
        self.scale_b = t.sb("scale_b", [P, B, D])

    def for_experts(self, t):
        self.slots = t.sb("slots", [P, CHUNKS], U32)
        self.bounds = t.sb("bounds", [P, E + 1], I32)
        self.w_hi = t.sb("w_hi", [P, 2, 3 * KD * F], F32R)
        self.w_lo = t.sb("w_lo", [P, 2, 3 * KD * F], F32R)
        self.rows = t.sb("rows", [P, SUB, D])
        self.rows_in = t.sem("rows_in")
        self.before = t.sb("before", [P, P])
        self.ones = t.sb("ones", [P, P])


def adaln_block(nc, dram, stages=9):
    for name, shape, dtype in (("qk", [2, 2 * D, T + P], F32), ("v", [T + P, H * VROW], BF16),
                               ("h_rows", [T, D], F32), ("h_sorted", [SORTED, D], F32),
                               ("x_sorted", [SORTED, XROW], F32)):
        dram[name] = nc.dram_tensor(name + "_scratch", shape, dtype, kind="Internal").ap()
    with ExitStack() as stack:
        g = Globals(Tensors(nc, stack))
        with ExitStack() as inner:
            g.for_attention(Tensors(nc, inner))
            setup(nc, g, dram)
            project(nc, g, dram)
            if stages >= 2:
                attend(nc, g, dram)
        if stages >= 3:
            g.for_experts(Tensors(nc, stack))
            route(nc, g, dram)
            experts(nc, g, dram)


_INPUTS = {"x": "L0_attn_x", "wq": "L0_attn_Wq", "wk": "L0_attn_Wk", "wv": "L0_attn_Wv", "wo": "L0_attn_Wo",
           "w1s": "L0_ffn_w1s", "w2s": "L0_ffn_w2s", "w3s": "L0_ffn_w3s", "W1": "L0_ffn_W1", "W2": "L0_ffn_W2",
           "W3": "L0_ffn_W3", "wg": "L0_ffn_Wg", "c": "L0_c", "wmod": "L0_wmod"}


def kernel(**inputs):
    import numpy as np
    import concourse.bacc as bacc
    from concourse import mybir
    from concourse.bass_utils import run_bass_kernel_spmd

    nc = bacc.Bacc("TRN2", target_bir_lowering=False, num_devices=1)
    arrays, dram = {}, {}
    for short, name in _INPUTS.items():
        a = np.asarray(inputs[name])
        if short == "x":
            a = a.reshape(T, D)
        if short in ("wq", "wk", "wv", "wo", "c"):
            a = a.T
        arrays["in_" + short] = np.ascontiguousarray(a)
        dram[short] = nc.dram_tensor("in_" + short, a.shape, mybir.dt.from_np(a.dtype), kind="ExternalInput").ap()
    dram["out"] = nc.dram_tensor("out_0_dram", (T + TILE, D), mybir.dt.float32, kind="ExternalOutput").ap()
    adaln_block(nc, dram)
    r = run_bass_kernel_spmd(nc, [arrays], core_ids=[0])
    return r.results[0]["out_0_dram"][0:T].reshape(B, S, D)
```
